# Optimizing a Trainium2 kernel written in Bass

```python
import numpy as np
import jax
import jax.numpy as jnp

def _softmax(x, axis=-1):
    return jax.nn.softmax(x, axis=axis)

def _gelu(x):
    return jax.nn.gelu(x, approximate=True)

def _silu(x):
    return jax.nn.silu(x)

def _sigmoid(x):
    return jax.nn.sigmoid(x)

def _layernorm(x, axis=-1, eps=1e-05):
    m = jnp.mean(x, axis=axis, keepdims=True)
    v = jnp.var(x, axis=axis, keepdims=True)
    return (x - m) / jnp.sqrt(v + eps)

def _scatter_add(tgt, idx, src, axis=0):
    return tgt.at[idx].add(src)

def _segment_sum(src, seg, n):
    return jax.ops.segment_sum(src, seg, n)
kernel_name = 'mk_recurrent_d2_jaxref_r8_a2fcf8'

def setup_inputs(seed: int=0):
    np.random.seed(seed)
    _w = jnp.asarray

    def _L0_attn_setup():
        import jax, jax.numpy as jnp
        import numpy as np
        DIM = 256
        DIM_HEAD = 128
        HEADS = 16
        EPS = 1e-05

        def _rotate_half(t):
            d2 = t.shape[-1] // 2
            x1, x2 = (t[..., :d2], t[..., d2:])
            return jnp.concatenate([-x2, x1], axis=-1)

        def _rotary_pos(n, dim_head, dtype):
            inv_freq = 1.0 / 10000.0 ** (jnp.arange(0, dim_head, 2, dtype=jnp.float32) / dim_head)
            freqs = jnp.arange(n, dtype=jnp.float32)[:, None] * inv_freq[None, :]
            return jnp.concatenate([freqs, freqs], axis=-1).astype(dtype)
        key = jax.random.key(seed)
        ks = jax.random.split(key, 4)
        b, n = (2, 256)
        x = jax.random.normal(ks[0], (b, n, DIM), dtype=jnp.float32)
        gamma = jnp.ones((DIM,), dtype=jnp.float32)
        Wq = jax.random.normal(ks[1], (DIM, HEADS * DIM_HEAD), dtype=jnp.float32) * DIM ** (-0.5)
        Wkv = jax.random.normal(ks[2], (DIM, 2 * DIM_HEAD), dtype=jnp.float32) * DIM ** (-0.5)
        Wo = jax.random.normal(ks[3], (HEADS * DIM_HEAD, DIM), dtype=jnp.float32) * (HEADS * DIM_HEAD) ** (-0.5)
        return {'x': x, 'gamma': gamma, 'Wq': Wq, 'Wkv': Wkv, 'Wo': Wo}
    _L0_attn_in = _L0_attn_setup()

    def _L0_ffn_setup():
        import jax, jax.numpy as jnp
        import numpy as np
        BLOCK_SIZE = 32
        HIDDEN_SIZE = 256
        MLP_DIM = 2048
        NVFP4_LUT = jnp.array([0.0, 0.5, 1.0, 1.5, 2.0, 3.0, 4.0, 6.0, 0.0, -0.5, -1.0, -1.5, -2.0, -3.0, -4.0, -6.0], dtype=jnp.float32)

        def dequant_nvfp4(W_packed, scales, block=BLOCK_SIZE):
            N = W_packed.shape[0]
            low = W_packed & 15
            high = W_packed >> 4 & 15
            idx = jnp.stack([low, high], axis=-1).reshape(N, -1)
            vals = NVFP4_LUT[idx]
            K = vals.shape[1]
            vals = vals.reshape(N, K // block, block) * scales[:, :, None]
            return vals.reshape(N, K)
        key = jax.random.key(seed)
        ks = jax.random.split(key, 7)
        x = jax.random.normal(ks[0], (4, 32, HIDDEN_SIZE), dtype=jnp.float32)
        gate_W_packed = jax.random.randint(ks[1], (MLP_DIM, HIDDEN_SIZE // 2), 0, 32, dtype=jnp.int32)
        gate_scales = jax.random.uniform(ks[2], (MLP_DIM, HIDDEN_SIZE // BLOCK_SIZE), dtype=jnp.float32) * 0.1 + 0.001
        up_W_packed = jax.random.randint(ks[3], (MLP_DIM, HIDDEN_SIZE // 2), 0, 32, dtype=jnp.int32)
        up_scales = jax.random.uniform(ks[4], (MLP_DIM, HIDDEN_SIZE // BLOCK_SIZE), dtype=jnp.float32) * 0.1 + 0.001
        down_W_packed = jax.random.randint(ks[5], (HIDDEN_SIZE, MLP_DIM // 2), 0, 32, dtype=jnp.int32)
        down_scales = jax.random.uniform(ks[6], (HIDDEN_SIZE, MLP_DIM // BLOCK_SIZE), dtype=jnp.float32) * 0.1 + 0.001
        return {'x': x, 'gate_W_packed': gate_W_packed, 'gate_scales': gate_scales, 'up_W_packed': up_W_packed, 'up_scales': up_scales, 'down_W_packed': down_W_packed, 'down_scales': down_scales}
    _L0_ffn_in = _L0_ffn_setup()

    def _L1_attn_setup():
        import jax, jax.numpy as jnp
        import numpy as np
        B, S, D, H = (2, 256, 256, 16)
        HD = D // H

        def _alibi_slopes(num_heads):
            ratio = 2.0 ** (-8.0 / num_heads)
            return ratio ** jnp.arange(1, num_heads + 1, dtype=jnp.float32)
        key = jax.random.key(seed)
        ks = jax.random.split(key, 9)
        sd = 1.0 / np.sqrt(D)
        inp = {'x': jax.random.normal(ks[0], (B, S, D), dtype=jnp.float32)}
        for i, name in enumerate(['Wq', 'Wk', 'Wv', 'Wo']):
            inp[name] = jax.random.normal(ks[1 + i], (D, D), dtype=jnp.float32) * sd
        for i, name in enumerate(['bq', 'bk', 'bv', 'bo']):
            inp[name] = jax.random.normal(ks[5 + i], (D,), dtype=jnp.float32) * 0.02
        return inp
    _L1_attn_in = _L1_attn_setup()

    def _L1_ffn_setup():
        import jax, jax.numpy as jnp
        import numpy as np
        B, S, D = (2, 256, 256)
        E, I, TOPK = (64, 96, 8)
        M = B * S
        CAP = 2 * (M * TOPK) // E

        def _moe(x, router_weight, gate_proj, up_proj, down_proj):
            b, s, d = x.shape
            xf = x.reshape(-1, d)
            m = xf.shape[0]
            logits = xf @ router_weight
            probs = jax.nn.softmax(logits.astype(jnp.float32), axis=-1)
            topw, topi = jax.lax.top_k(probs, TOPK)
            topw = topw / topw.sum(axis=-1, keepdims=True)
            flat_e = topi.reshape(-1)
            flat_w = topw.reshape(-1).astype(x.dtype)
            order = jnp.argsort(flat_e)
            se = flat_e[order]
            tok = order // TOPK
            counts = jax.ops.segment_sum(jnp.ones_like(flat_e), flat_e, num_segments=E)
            starts = jnp.cumsum(counts) - counts
            pos = jnp.arange(m * TOPK) - starts[se]
            valid = pos < CAP
            posc = jnp.minimum(pos, CAP - 1)
            xe = jnp.zeros((E, CAP, d), x.dtype).at[se, pos].set(xf[tok], mode='drop')
            h = jax.nn.silu(jnp.einsum('ecd,edi->eci', xe, gate_proj)) * jnp.einsum('ecd,edi->eci', xe, up_proj)
            ye = jnp.einsum('eci,eid->ecd', h, down_proj)
            contrib = jnp.where(valid[:, None], ye[se, posc], 0.0) * flat_w[order][:, None]
            out = jnp.zeros((m, d), x.dtype).at[tok].add(contrib)
            return out.reshape(b, s, d)
        key = jax.random.key(seed)
        k0, k1, k2, k3, k4 = jax.random.split(key, 5)
        return {'x': jax.random.normal(k0, (B, S, D), jnp.float32), 'router_weight': jax.random.normal(k1, (D, E), jnp.float32) * 0.02, 'gate_proj': jax.random.normal(k2, (E, D, I), jnp.float32) * 0.02, 'up_proj': jax.random.normal(k3, (E, D, I), jnp.float32) * 0.02, 'down_proj': jax.random.normal(k4, (E, I, D), jnp.float32) * 0.02}
    _L1_ffn_in = _L1_ffn_setup()
    _d = {'L0_attn_x': _L0_attn_in['x'], 'L0_attn_gamma': _L0_attn_in['gamma'], 'L0_attn_Wq': _L0_attn_in['Wq'], 'L0_attn_Wkv': _L0_attn_in['Wkv'], 'L0_attn_Wo': _L0_attn_in['Wo'], 'L0_ffn_gate_W_packed': _L0_ffn_in['gate_W_packed'], 'L0_ffn_gate_scales': _L0_ffn_in['gate_scales'], 'L0_ffn_up_W_packed': _L0_ffn_in['up_W_packed'], 'L0_ffn_up_scales': _L0_ffn_in['up_scales'], 'L0_ffn_down_W_packed': _L0_ffn_in['down_W_packed'], 'L0_ffn_down_scales': _L0_ffn_in['down_scales'], 'L1_attn_Wq': _L1_attn_in['Wq'], 'L1_attn_bq': _L1_attn_in['bq'], 'L1_attn_Wk': _L1_attn_in['Wk'], 'L1_attn_bk': _L1_attn_in['bk'], 'L1_attn_Wv': _L1_attn_in['Wv'], 'L1_attn_bv': _L1_attn_in['bv'], 'L1_attn_Wo': _L1_attn_in['Wo'], 'L1_attn_bo': _L1_attn_in['bo'], 'L1_ffn_router_weight': _L1_ffn_in['router_weight'], 'L1_ffn_gate_proj': _L1_ffn_in['gate_proj'], 'L1_ffn_up_proj': _L1_ffn_in['up_proj'], 'L1_ffn_down_proj': _L1_ffn_in['down_proj']}
    _x0 = _d['L0_attn_x']
    _d['L0_attn_x'] = jax.random.normal(jax.random.fold_in(jax.random.key(seed), 1), (1, 2048, 256), dtype=_x0.dtype)
    del _x0
    return _d

def reference(L0_attn_x, L0_attn_gamma, L0_attn_Wq, L0_attn_Wkv, L0_attn_Wo, L0_ffn_gate_W_packed, L0_ffn_gate_scales, L0_ffn_up_W_packed, L0_ffn_up_scales, L0_ffn_down_W_packed, L0_ffn_down_scales, L1_attn_Wq, L1_attn_bq, L1_attn_Wk, L1_attn_bk, L1_attn_Wv, L1_attn_bv, L1_attn_Wo, L1_attn_bo, L1_ffn_router_weight, L1_ffn_gate_proj, L1_ffn_up_proj, L1_ffn_down_proj):

    def _L0_attn_ref(x, gamma, Wq, Wkv, Wo):
        import jax, jax.numpy as jnp
        import numpy as np
        DIM = 256
        DIM_HEAD = 128
        HEADS = 16
        EPS = 1e-05

        def _rotate_half(t):
            d2 = t.shape[-1] // 2
            x1, x2 = (t[..., :d2], t[..., d2:])
            return jnp.concatenate([-x2, x1], axis=-1)

        def _rotary_pos(n, dim_head, dtype):
            inv_freq = 1.0 / 10000.0 ** (jnp.arange(0, dim_head, 2, dtype=jnp.float32) / dim_head)
            freqs = jnp.arange(n, dtype=jnp.float32)[:, None] * inv_freq[None, :]
            return jnp.concatenate([freqs, freqs], axis=-1).astype(dtype)
        b, n, dim = x.shape
        h, dh = (HEADS, DIM_HEAD)
        scale = dh ** (-0.5)
        mu = jnp.mean(x, axis=-1, keepdims=True)
        var = jnp.var(x, axis=-1, keepdims=True)
        xn = (x - mu) * jax.lax.rsqrt(var + EPS) * gamma
        q = (xn @ Wq).reshape(b, n, h, dh).transpose(0, 2, 1, 3)
        kv = xn @ Wkv
        k, v = (kv[..., :dh], kv[..., dh:])
        pos = _rotary_pos(n, dh, x.dtype)
        cos, sin = (jnp.cos(pos), jnp.sin(pos))
        q = q * cos + _rotate_half(q) * sin
        k = k * cos + _rotate_half(k) * sin
        q = q * scale
        sim = jnp.einsum('bhid,bjd->bhij', q, k)
        causal = jnp.triu(jnp.ones((n, n), dtype=bool), k=1)
        neg = -jnp.finfo(sim.dtype).max
        sim = jnp.where(causal, neg, sim)
        sim = sim - jax.lax.stop_gradient(jnp.max(sim, axis=-1, keepdims=True))
        attn = jax.nn.softmax(sim, axis=-1)
        out = jnp.einsum('bhij,bjd->bhid', attn, v)
        out = out.transpose(0, 2, 1, 3).reshape(b, n, h * dh)
        return out @ Wo

    def _L0_ffn_ref(x, gate_W_packed, gate_scales, up_W_packed, up_scales, down_W_packed, down_scales):
        import jax, jax.numpy as jnp
        import numpy as np
        BLOCK_SIZE = 32
        HIDDEN_SIZE = 256
        MLP_DIM = 2048
        NVFP4_LUT = jnp.array([0.0, 0.5, 1.0, 1.5, 2.0, 3.0, 4.0, 6.0, 0.0, -0.5, -1.0, -1.5, -2.0, -3.0, -4.0, -6.0], dtype=jnp.float32)

        def dequant_nvfp4(W_packed, scales, block=BLOCK_SIZE):
            N = W_packed.shape[0]
            low = W_packed & 15
            high = W_packed >> 4 & 15
            idx = jnp.stack([low, high], axis=-1).reshape(N, -1)
            vals = NVFP4_LUT[idx]
            K = vals.shape[1]
            vals = vals.reshape(N, K // block, block) * scales[:, :, None]
            return vals.reshape(N, K)
        B, S, H = x.shape
        xt = x.reshape(B * S, H)
        Wg = dequant_nvfp4(gate_W_packed, gate_scales)
        Wu = dequant_nvfp4(up_W_packed, up_scales)
        Wd = dequant_nvfp4(down_W_packed, down_scales)
        gate = jnp.einsum('th,nh->tn', xt, Wg)
        up = jnp.einsum('th,nh->tn', xt, Wu)
        gelu = jnp.tanh(0.7978845608028654 * (gate + 0.044715 * gate ** 3)) * gate * 0.5 + gate * 0.5
        inter = gelu * up
        out = jnp.einsum('tn,hn->th', inter, Wd)
        return out.reshape(B, S, H)

    def _L1_attn_ref(x, Wq, bq, Wk, bk, Wv, bv, Wo, bo):
        import jax, jax.numpy as jnp
        import numpy as np
        B, S, D, H = (2, 256, 256, 16)
        HD = D // H

        def _alibi_slopes(num_heads):
            ratio = 2.0 ** (-8.0 / num_heads)
            return ratio ** jnp.arange(1, num_heads + 1, dtype=jnp.float32)
        b, s, d = x.shape

        def proj(W, bias):
            return (x @ W + bias).reshape(b, s, H, HD).transpose(0, 2, 1, 3)
        q, k, v = (proj(Wq, bq), proj(Wk, bk), proj(Wv, bv))
        scores = jnp.einsum('bhqd,bhkd->bhqk', q, k) / jnp.sqrt(jnp.float32(HD))
        distances = jnp.arange(1 - s, 1, dtype=jnp.float32)
        bias = _alibi_slopes(H)[None, :, None, None] * distances[None, None, None, :]
        scores = scores + bias
        causal = jnp.tril(jnp.ones((s, s), dtype=bool))[None, None]
        scores = jnp.where(causal, scores, jnp.finfo(scores.dtype).min)
        attn = jax.nn.softmax(scores, axis=-1)
        ctx = jnp.einsum('bhqk,bhkd->bhqd', attn, v)
        ctx = ctx.transpose(0, 2, 1, 3).reshape(b, s, d)
        return ctx @ Wo + bo

    def _L1_ffn_ref(x, router_weight, gate_proj, up_proj, down_proj):
        import jax, jax.numpy as jnp
        import numpy as np
        B, S, D = (2, 256, 256)
        E, I, TOPK = (64, 96, 8)
        M = B * S
        CAP = 2 * (M * TOPK) // E

        def _moe(x, router_weight, gate_proj, up_proj, down_proj):
            b, s, d = x.shape
            xf = x.reshape(-1, d)
            m = xf.shape[0]
            logits = xf @ router_weight
            probs = jax.nn.softmax(logits.astype(jnp.float32), axis=-1)
            topw, topi = jax.lax.top_k(probs, TOPK)
            topw = topw / topw.sum(axis=-1, keepdims=True)
            flat_e = topi.reshape(-1)
            flat_w = topw.reshape(-1).astype(x.dtype)
            order = jnp.argsort(flat_e)
            se = flat_e[order]
            tok = order // TOPK
            counts = jax.ops.segment_sum(jnp.ones_like(flat_e), flat_e, num_segments=E)
            starts = jnp.cumsum(counts) - counts
            pos = jnp.arange(m * TOPK) - starts[se]
            valid = pos < CAP
            posc = jnp.minimum(pos, CAP - 1)
            xe = jnp.zeros((E, CAP, d), x.dtype).at[se, pos].set(xf[tok], mode='drop')
            h = jax.nn.silu(jnp.einsum('ecd,edi->eci', xe, gate_proj)) * jnp.einsum('ecd,edi->eci', xe, up_proj)
            ye = jnp.einsum('eci,eid->ecd', h, down_proj)
            contrib = jnp.where(valid[:, None], ye[se, posc], 0.0) * flat_w[order][:, None]
            out = jnp.zeros((m, d), x.dtype).at[tok].add(contrib)
            return out.reshape(b, s, d)
        return _moe(x, router_weight, gate_proj, up_proj, down_proj)
    x = L0_attn_x
    xn = _layernorm(x, axis=-1)
    s = _L0_attn_ref(xn, L0_attn_gamma, L0_attn_Wq, L0_attn_Wkv, L0_attn_Wo)
    g = _silu(_L0_ffn_ref(xn, L0_ffn_gate_W_packed, L0_ffn_gate_scales, L0_ffn_up_W_packed, L0_ffn_up_scales, L0_ffn_down_W_packed, L0_ffn_down_scales))
    x = x + s * g
    xn = _layernorm(x, axis=-1)
    s = _L1_attn_ref(xn, L1_attn_Wq, L1_attn_bq, L1_attn_Wk, L1_attn_bk, L1_attn_Wv, L1_attn_bv, L1_attn_Wo, L1_attn_bo)
    g = _silu(_L1_ffn_ref(xn, L1_ffn_router_weight, L1_ffn_gate_proj, L1_ffn_up_proj, L1_ffn_down_proj))
    x = x + s * g
    return x

_drawn_inputs = setup_inputs


def setup_inputs(seed=0):
    import zlib

    import numpy as np

    out = dict(_drawn_inputs(seed))
    spreads = {'L0_attn_gamma': (1.0, 0.2)}
    factors = {'L1_attn_Wq': 8.0,
     'L1_attn_bq': 8.0,
     'L1_attn_Wk': 8.0,
     'L1_attn_bk': 200.0,
     'L1_attn_Wv': 8.0,
     'L1_attn_bv': 8.0,
     'L1_attn_Wo': 8.0,
     'L1_attn_bo': 186.179,
     'L1_ffn_router_weight': 8.0,
     'L1_ffn_gate_proj': 8.0,
     'L1_ffn_up_proj': 8.0,
     'L1_ffn_down_proj': 8.0}
    for name, (base, spread) in spreads.items():
        noise = np.random.default_rng([zlib.crc32(name.encode()), seed]).standard_normal(out[name].shape)
        drawn = base * np.exp(spread * noise) if base else spread * noise
        out[name] = jnp.asarray(drawn.astype(out[name].dtype))
    for name, factor in factors.items():
        out[name] = (out[name] * factor).astype(out[name].dtype)
    return out
```

```python
import math
from contextlib import ExitStack

import numpy as np

import concourse.bass as bass
from concourse import mybir

F32 = mybir.dt.float32
BF16 = mybir.dt.bfloat16
I32 = mybir.dt.int32
U32 = mybir.dt.uint32
ALU = mybir.AluOpType
ACT = mybir.ActivationFunctionType
AX = mybir.AxisListType

P = 128
N = 2048
D = 256
NT = N // P
KT = D // P
CH = 512
NC = N // CH
TPC = CH // P
EPS = 1e-5
HEADS = 16
DH = 128
HD = D // HEADS
KA = HD + 1
NBLK = 16
E, I, TOPK = 64, 96, 8
CAP = 2 * (512 * TOPK) // E
EG = 4
NEG = -3.0e38


class Tally:

    def __init__(self, sem):
        self.sem = sem
        self.n = 0

    def need(self, eng, k=1):
        self.n += k
        eng.wait_ge(self.sem, self.n)

    def give_back(self, eng):
        if self.n:
            eng.sem_inc(self.sem, -self.n)
        self.n = 0


class Chain:

    def __init__(self, eng, sem):
        self.eng = eng
        self.t = Tally(sem)

    def __call__(self, ins):
        ins.then_inc(self.t.sem, 1)
        self.t.need(self.eng)

    def give_back(self):
        self.t.give_back(self.eng)


def groups_of(t):
    return [(b, min(4, t + 1 - b)) for b in range(0, t + 1, 4)]


def act_copies(ng):
    return (ng + 1) // 2


def setup_phase(nc, c, io, mem):
    with ExitStack() as ctx:
        sb = lambda n, s, d=F32: ctx.enter_context(nc.sbuf_tensor(n, s, d))
        ps = lambda n, s, d=F32: ctx.enter_context(nc.psum_tensor(n, s, d))
        sem = lambda n: ctx.enter_context(nc.semaphore(n))
        xn = sb("xn0", [P, NT, D])
        xg = sb("xg", [P, NT, D])
        st = sb("st0", [P, 2, NT, 6])
        mv = sb("mv0", [P, 2, NT, 2])
        rstd = sb("rstd0", [P, 2, NT])
        mhalf = sb("mhalf0", [P, NT])
        wkv = sb("wkv", [P, KT, 2 * DH])
        gam = sb("gam", [P, KT])
        maskf = sb("maskf", [P, P])
        ra = sb("rope_a0", [P, CH])
        rb = sb("rope_b0", [P, CH])
        zeros = sb("zeros", [P, 2048])
        TP = [ps(f"TP{i}", [P, 4, P]) for i in range(4)]
        KP = [ps(f"KP{i}", [P, CH]) for i in range(2)]
        VP = [ps(f"VP{i}", [P, CH]) for i in range(2)]
        x_in = [sem(f"x_in{i}") for i in range(NC)]
        const_in, wkv_in, zero_set = sem("const_in"), sem("wkv_in"), sem("zero_set")
        pool0 = sem("pool0")
        dve0, stat_ready, rstd_ready = sem("dve0"), sem("stat_ready"), sem("rstd_ready")
        xn_ready, xg_ready = sem("xn_ready"), sem("xg_ready")
        turned, t_out = sem("turned0"), sem("t_out0")
        k_done, k_free, v_done, v_out = sem("k_done"), sem("k_free"), sem("v_done"), sem("v_out")
        block = ctx.enter_context(nc.Block())

        @block.sync
        def _(sp):
            xv = io["x"][0].rearrange("(t p) c -> p t c", p=P)
            for i in range(NC):
                sp.dma_start(mem.x[:, TPC * i:TPC * (i + 1), :], xv[:, TPC * i:TPC * (i + 1), :]).then_inc(x_in[i], 16)
            sp.dma_start(mem.ident[:], io["identity"]).then_inc(const_in, 16)
            sp.dma_start(maskf[:], io["causal"]).then_inc(const_in, 16)
            sp.dma_start(gam[:], io["gamma"]).then_inc(const_in, 16)
            sp.dma_start(mem.cos[:], io["cos"]).then_inc(const_in, 16)
            sp.dma_start(mem.sin[:], io["sin"]).then_inc(const_in, 16)
            sp.dma_start(wkv[:], io["Wkv"].rearrange("(k p) n -> p k n", p=P)).then_inc(wkv_in, 16)
            sp.wait_ge(zero_set, 1)
            zv = mem.xe.rearrange("(a p r) c -> a p (r c)", a=8, p=P)
            for a in range(8):
                sp.dma_start(zv[a], zeros[:]).then_inc(mem.xe_zeroed, 16)
            sp.wait_ge(mem.xe_zeroed, 8 * 16)

        @block.gpsimd
        def _(pool):
            pool.memset(zeros[:], 0.0).then_inc(zero_set, 1)
            pool.memset(mhalf[:], -0.5).then_inc(pool0, 1)
            for k in range(2):
                pool.wait_ge(stat_ready, NT * (k + 1))
                pool.tensor_scalar(rstd[:, k, :], mv[:, k, :, 1], EPS, None, ALU.add).then_inc(pool0, 1)
                pool.wait_ge(pool0, k + 2)
                pool.tensor_tensor(rstd[:, k, :], rstd[:, k, :], mhalf[:], ALU.pow).then_inc(rstd_ready, 1)

        @block.vector
        def _(v):
            own = Chain(v, dve0)
            v.wait_ge(const_in, 5 * 16)
            v.tensor_copy(mem.ident_bf[:], mem.ident[:]).then_inc(mem.casts, 1)
            v.tensor_copy(mem.mask_bf[:], maskf[:]).then_inc(mem.casts, 1)
            v.memset(mem.acc[:], 0.0).then_inc(mem.casts, 1)
            for k, src, dst, ready in ((0, mem.x, xn, xn_ready), (1, xn, xg, xg_ready)):
                for t in range(NT):
                    if k == 0 and t % TPC == 0:
                        v.wait_ge(x_in[t // TPC], 16)
                    ins = v.bn_stats(st[:, k, t, :], src[:, t, :])
                    ins.then_inc(dve0, 1)
                    own.t.n += 1
                v.wait_ge(dve0, own.t.n)
                for t in range(NT):
                    v.bn_aggr(mv[:, k, t, :], st[:, k, t, :]).then_inc(stat_ready, 1)
                v.wait_ge(rstd_ready, k + 1)
                for t in range(NT):
                    v.tensor_scalar(dst[:, t, :], src[:, t, :], mv[:, k, t, 0:1], rstd[:, k, t:t + 1],
                                    ALU.subtract, ALU.mult).then_inc(ready, 1)
                v.wait_ge(ready, NT)
            for i in range(NC):
                cs = slice(CH * i, CH * (i + 1))
                v.wait_ge(k_done, i + 1)
                v.tensor_tensor(ra[:], KP[i % 2][:], mem.cos[:, cs], ALU.mult).then_inc(dve0, 1)
                v.tensor_tensor(rb[0:64], KP[i % 2][64:P], mem.sin[64:P, cs], ALU.mult).then_inc(dve0, 1)
                own.t.n += 2
                own(v.tensor_tensor(rb[64:P], KP[i % 2][0:64], mem.sin[0:64, cs], ALU.mult))
                own(v.tensor_tensor(ra[:], ra[:], rb[:], ALU.add))
                v.tensor_scalar(mem.kT[:, cs], ra[:], float(DH) ** -0.5, None, ALU.mult).then_inc(k_free, 1)
                v.wait_ge(k_free, i + 1)

        @block.tensor
        def _(pe):
            pe.wait_ge(const_in, 5 * 16)
            n = 0
            for k, src, ready in ((0, xn, xn_ready), (1, xg, xg_ready)):
                for t in range(NT):
                    pe.wait_ge(ready, t + 1)
                    if n % 2 == 0 and n >= 8:
                        pe.wait_ge(t_out, n // 2 - 3)
                    for j in range(KT):
                        cols = src[:, t, j::2] if k == 0 else src[:, t, P * j:P * (j + 1)]
                        ins = pe.transpose(TP[n // 2 % 4][:, 2 * (n % 2) + j, :], cols, mem.ident[:])
                    if n % 2:
                        ins.then_inc(turned, 1)
                    n += 1
            pe.wait_ge(wkv_in, 16)
            pe.wait_ge(t_out, NT)
            for i in range(NC):
                if i >= 2:
                    pe.wait_ge(k_free, i - 1)
                for j in range(KT):
                    ins = pe.matmul(KP[i % 2][:], wkv[:, j, 0:DH], mem.gxT[:, j, CH * i:CH * (i + 1)],
                                    start=(j == 0), stop=(j == KT - 1))
                ins.then_inc(k_done, 1)
            for i in range(NC):
                if i >= 2:
                    pe.wait_ge(v_out, i - 1)
                for q in range(4):
                    t = 4 * i + q
                    for j in range(KT):
                        ins = pe.matmul(VP[i % 2][:, P * q:P * (q + 1)], mem.gxT[:, j, P * t:P * (t + 1)],
                                        wkv[:, j, DH:2 * DH], start=(j == 0), stop=(j == KT - 1))
                ins.then_inc(v_done, 1)

        @block.scalar
        def _(act):
            act.wait_ge(const_in, 5 * 16)
            for n in range(2 * NT // 2):
                k, t = n // (NT // 2), 2 * n % NT
                act.wait_ge(turned, n + 1)
                tp = TP[n % 4][:].rearrange("p (a k) c -> p k a c", a=2)
                if k == 0:
                    dst = mem.xT[:, :, P * t:P * (t + 2)].rearrange("p k (a c) -> p k a c", a=2)
                    for j in range(KT):
                        ins = act.copy(dst[:, j], tp[:, j])
                else:
                    dst = mem.gxT[:, :, P * t:P * (t + 2)].rearrange("p k (a c) -> p k a c", a=2)
                    for j in range(KT):
                        ins = act.activation(dst[:, j], tp[:, j], ACT.Copy, scale=gam[:, j:j + 1])
                ins.then_inc(t_out, 1)
            for i in range(NC):
                act.wait_ge(v_done, i + 1)
                act.copy(mem.v[:, 4 * i:4 * i + 4, :], VP[i % 2][:].rearrange("p (a c) -> p a c", a=4)).then_inc(v_out, 1)


def attention0_phase(nc, c, io, mem):
    with ExitStack() as ctx:
        sb = lambda n, s, d=F32: ctx.enter_context(nc.sbuf_tensor(n, s, d))
        ps = lambda n, s, d=F32: ctx.enter_context(nc.psum_tensor(n, s, d))
        sem = lambda n: ctx.enter_context(nc.semaphore("a0_" + n))
        qT = sb("qT", [P, N])
        wq = sb("wq", [P, KT, DH])
        wo = sb("wo", [P, D])
        probs = sb("probs", [P, 2, N])
        PT = sb("PT", [P, 4, CH])
        oT = sb("oT", [P, 2, P])
        negmax = sb("negmax", [P, 2])
        rowsum = sb("rowsum", [P, 4])
        rinv = sb("rinv", [P, 2])
        ra = sb("rope_a", [P, CH])
        rb = sb("rope_b", [P, CH])
        raw = sb("raw", [P, 3, P], I32)
        scl = sb("scl", [P, 3, P])
        mag = sb("mag", [P, 3, P], I32)
        sgn = sb("sgn", [P, 3, P], I32)
        val = sb("val", [P, 3, P])
        val2 = sb("val2", [P, 3, P])
        sgf = sb("sgf", [P, 3, P])
        S = ps("S", [P, N])
        T = [ps(f"T{i}", [P, CH]) for i in range(2)]
        O = ps("O", [P, CH])
        Y = ps("Y", [P, CH])
        names = ("wq_in wq_free wo_in wo_free dq_in dq_free proj_done q_ready scores_done negmax_ready "
                 "probs_done turned_dve turned_act pt_dve pt_act o_done oT_ready y_done y_free dve")
        s = {n: sem(n) for n in names.split()}
        block = ctx.enter_context(nc.Block())
        tiles = list(range(NT - 1, -1, -1))

        @block.sync
        def _(sp):
            wq_free, wo_free, dq_free = Tally(s["wq_free"]), Tally(s["wo_free"]), Tally(s["dq_free"])
            sp.dma_start(wq[:], io["Wq"][0].rearrange("(k p) n -> p k n", p=P)).then_inc(s["wq_in"], 16)
            with sp.Fori(0, HEADS) as h:
                wo_free.need(sp)
                sp.dma_start(wo[:], io["Wo"][bass.ds(h * DH, DH), :]).then_inc(s["wo_in"], 16)
                dq_free.need(sp)
                sp.dma_start(raw[:], io["packed"][bass.ds(h, 1)].rearrange("a p m n -> p (a m) n")).then_inc(s["dq_in"], 16)
                for a in range(8):
                    src = io["scales"][bass.ds(h, 1), a:a + 1].rearrange("b a m n -> (b a) m n").broadcast_to([16, 3, P])
                    sp.dma_start(scl[16 * a:16 * (a + 1)], src).then_inc(s["dq_in"], 16)
                wq_free.need(sp)
                sp.dma_start(wq[:], io["Wq"][bass.ds(h + 1, 1)].rearrange("a (k p) n -> p (a k) n", p=P)).then_inc(s["wq_in"], 16)
                for x in (wq_free, wo_free, dq_free):
                    x.give_back(sp)

        @block.tensor
        def _(pe):
            wq_in, wo_in, q_ready = Tally(s["wq_in"]), Tally(s["wo_in"]), Tally(s["q_ready"])
            probs_done, pt = Tally(s["probs_done"]), {"dve": Tally(s["pt_dve"]), "act": Tally(s["pt_act"])}
            oT_ready, y_free = Tally(s["oT_ready"]), Tally(s["y_free"])

            def project(i, bank):
                for j in range(KT):
                    ins = pe.matmul(bank, wq[:, j, :], mem.gxT[:, j, CH * i:CH * (i + 1)],
                                    start=(j == 0), stop=(j == KT - 1))
                ins.then_inc(s["proj_done"], 1)
                return ins

            def scores(t):
                nk = P * (t + 1)
                for k0 in range(0, nk, CH):
                    last = k0 + CH >= nk
                    pe.matmul(S[:, k0:min(nk, k0 + CH)], qT[:, P * t:P * (t + 1)], mem.kT[:, k0:min(nk, k0 + CH)],
                              start=True, stop=not last)
                pe.matmul(S[:, nk - P:nk], mem.ident_bf[:], mem.mask_bf[:], start=False, stop=True).then_inc(s["scores_done"], 1)

            wq_in.need(pe, 16)
            project(NC - 1, S[:, 3 * CH:4 * CH])
            wq_in.give_back(pe)
            with pe.Fori(0, HEADS) as h:
                g_at = 0

                def out_proj(i):
                    oT_ready.need(pe)
                    if i == 0:
                        wo_in.need(pe, 16)
                    y_free.need(pe)
                    ins = pe.matmul(Y[:, 0:D], oT[:, i % 2, :], wo[:], start=True, stop=True)
                    ins.then_inc(s["y_done"], 1)

                q_ready.need(pe)
                scores(tiles[0])
                project(2, T[0][:])
                project(1, T[1][:])
                project(0, O[:])
                for i, t in enumerate(tiles):
                    probs_done.need(pe)
                    if i + 1 < NT:
                        scores(tiles[i + 1])
                    if tiles[min(i + 1, NT - 1)] == 4 * (NC - 1) - 1 and i + 1 < NT:
                        wq_in.need(pe, 16)
                        project(NC - 1, S[:, 3 * CH:4 * CH])
                    groups = groups_of(t)
                    na = act_copies(len(groups))

                    def weigh(g):
                        b0, w = groups[g]
                        pt["act" if g < na else "dve"].need(pe)
                        if i == 0 and g == 0:
                            q_ready.need(pe)
                        for b in range(b0, b0 + w):
                            ins = pe.matmul(O[:, 0:P], mem.v[:, b, :],
                                            PT[:, (g_at + g) % 4, P * (b - b0):P * (b - b0 + 1)],
                                            start=(b == 0), stop=(b == t))
                        if g == len(groups) - 1:
                            ins.then_inc(s["o_done"], 1)

                    for g, (b0, w) in enumerate(groups):
                        if i == 0 and g < 2:
                            q_ready.need(pe)
                        for b in range(b0, b0 + w):
                            ins = pe.transpose(T[(g_at + g) % 2][:, P * (b - b0):P * (b - b0 + 1)],
                                               probs[:, i % 2, P * b:P * (b + 1)], mem.ident[:])
                        ins.then_inc(s["turned_act"] if g < na else s["turned_dve"], 1)
                        if g == 0 and i > 0:
                            out_proj(i - 1)
                        if g > 0:
                            weigh(g - 1)
                    weigh(len(groups) - 1)
                    g_at += len(groups)
                out_proj(NT - 1)
                for x in (wq_in, wo_in, q_ready, probs_done, pt["dve"], pt["act"], oT_ready, y_free):
                    x.give_back(pe)

        @block.vector
        def _(v):
            own = Chain(v, s["dve"])
            t_ = {n: Tally(s[n]) for n in "dq_in proj_done scores_done turned_dve y_done".split()}
            v.sem_inc(s["y_free"], 1)
            v.sem_inc(s["wo_free"], 1)
            v.sem_inc(s["dq_free"], 1)

            def rotate(i, bank):
                cs = slice(CH * i, CH * (i + 1))
                t_["proj_done"].need(v)
                v.tensor_tensor(ra[:], bank, mem.cos[:, cs], ALU.mult).then_inc(s["dve"], 1)
                v.tensor_tensor(rb[0:64], bank[64:P], mem.sin[64:P, cs], ALU.mult).then_inc(s["dve"], 1)
                own.t.n += 2
                own(v.tensor_tensor(rb[64:P], bank[0:64], mem.sin[0:64, cs], ALU.mult))
                own(v.tensor_tensor(qT[:, cs], ra[:], rb[:], ALU.add))
                v.sem_inc(s["q_ready"], 1)

            def row_max(i):
                t_["scores_done"].need(v)
                v.tensor_reduce(negmax[:, i % 2:i % 2 + 1], S[:, 0:P * (tiles[i] + 1)], AX.X, ALU.max,
                                negate=True).then_inc(s["negmax_ready"], 1)

            def add_up(i):
                t = tiles[i]
                t_["y_done"].need(v)
                own(v.reciprocal(rinv[:, i % 2:i % 2 + 1], rowsum[:, i % 4:i % 4 + 1]))
                v.scalar_tensor_tensor(mem.acc[:, t, :], Y[:, 0:D], rinv[:, i % 2:i % 2 + 1],
                                       mem.acc[:, t, :], ALU.mult, ALU.add).then_inc(s["y_free"], 1)

            def unpack(step, h):
                k, nib = step % 8, step // 8
                if step == 0:
                    t_["dq_in"].need(v, 9 * 16)
                if k == 0:
                    own(v.tensor_scalar(mag[:], raw[:], 4 * nib, 7, ALU.logical_shift_right, ALU.bitwise_and))
                elif k == 1:
                    own(v.tensor_scalar(sgn[:], raw[:], 4 * nib, 8, ALU.logical_shift_right, ALU.bitwise_and))
                elif k == 2:
                    own(v.scalar_tensor_tensor(val[:], mag[:], 4.0, mag[:], ALU.max, ALU.add))
                elif k == 3:
                    own(v.tensor_scalar(val2[:], mag[:], 6.0, 2.0, ALU.max, ALU.mult))
                elif k == 4:
                    own(v.tensor_tensor(val[:], val[:], val2[:], ALU.add))
                elif k == 5:
                    own(v.tensor_scalar(sgf[:], sgn[:], -0.125, 0.5, ALU.mult, ALU.add))
                elif k == 6:
                    own(v.scalar_tensor_tensor(val2[:], val[:], -16.0, sgf[:], ALU.add, ALU.mult))
                else:
                    own(v.tensor_tensor(mem.W[nib][:, :, bass.ds(h * P, P)], val2[:], scl[:], ALU.mult))

            rotate(NC - 1, S[:, 3 * CH:4 * CH])
            t_["proj_done"].give_back(v)
            own.give_back()
            with v.Fori(0, HEADS) as h:
                row_max(0)
                rotate(2, T[0][:])
                rotate(1, T[1][:])
                rotate(0, O[:])
                v.sem_inc(s["wq_free"], 1)
                g_at = 0
                for i, t in enumerate(tiles):
                    if i + 1 < NT:
                        row_max(i + 1)
                    groups = groups_of(t)
                    for g in range(act_copies(len(groups)), len(groups)):
                        w = groups[g][1] * P
                        t_["turned_dve"].need(v)
                        v.tensor_copy(PT[:, (g_at + g) % 4, 0:w], T[(g_at + g) % 2][:, 0:w]).then_inc(s["pt_dve"], 1)
                    g_at += len(groups)
                    if tiles[min(i + 1, NT - 1)] == 4 * (NC - 1) - 1 and i + 1 < NT:
                        rotate(NC - 1, S[:, 3 * CH:4 * CH])
                    if i > 0:
                        add_up(i - 1)
                    unpack(i, h)
                add_up(NT - 1)
                v.sem_inc(s["wo_free"], 1)
                v.sem_inc(s["dq_free"], 1)
                for x in t_.values():
                    x.give_back(v)
                own.give_back()

        @block.scalar
        def _(act):
            t_ = {n: Tally(s[n]) for n in "negmax_ready turned_act o_done".split()}

            def exponent(i):
                nk = P * (tiles[i] + 1)
                t_["negmax_ready"].need(act)
                act.activation(probs[:, i % 2, 0:nk], S[:, 0:nk], ACT.Exp, bias=negmax[:, i % 2:i % 2 + 1],
                               accum_out=rowsum[:, i % 4:i % 4 + 1]).then_inc(s["probs_done"], 1)

            with act.Fori(0, HEADS) as h:
                exponent(0)
                g_at = 0
                for i, t in enumerate(tiles):
                    groups = groups_of(t)
                    for g in range(act_copies(len(groups))):
                        w = groups[g][1] * P
                        t_["turned_act"].need(act)
                        act.copy(PT[:, (g_at + g) % 4, 0:w], T[(g_at + g) % 2][:, 0:w]).then_inc(s["pt_act"], 1)
                    g_at += len(groups)
                    if i + 1 < NT:
                        exponent(i + 1)
                    t_["o_done"].need(act)
                    act.copy(oT[:, i % 2, :], O[:, 0:P]).then_inc(s["oT_ready"], 1)
                for x in t_.values():
                    x.give_back(act)


def mlp0_phase(nc, c, io, mem):
    with ExitStack() as ctx:
        sb = lambda n, s, d=F32: ctx.enter_context(nc.sbuf_tensor(n, s, d))
        ps = lambda n, s, d=F32: ctx.enter_context(nc.psum_tensor(n, s, d))
        sem = lambda n: ctx.enter_context(nc.semaphore("m0_" + n))
        sq = sb("sq", [P, 2, CH])
        th = sb("th", [P, 2, CH])
        hid = sb("hid", [P, 2, CH])
        thf = sb("thf", [P, TPC, D])
        G = [ps(f"G{i}", [P, CH]) for i in range(2)]
        U = [ps(f"U{i}", [P, CH]) for i in range(2)]
        F = ps("F", [P, TPC, D])
        s = {n: sem(n) for n in "gate_act gate_dve squared poly tanhed hid_ready f_done f_free f_dve f_tanhed dve".split()}
        block = ctx.enter_context(nc.Block())

        @block.tensor
        def _(pe):
            t_ = {n: Tally(s[n]) for n in "hid_ready f_free".split()}
            with pe.Fori(0, NC) as c4:
                def down(b):
                    jt, nib = b // 2, b % 2
                    if b == 0:
                        t_["f_free"].need(pe)
                    t_["hid_ready"].need(pe)
                    for q in range(TPC):
                        ins = pe.matmul(F[:, q, :], hid[:, b % 2, P * q:P * (q + 1)],
                                        mem.W[nib][:, 2, 2 * P * jt:2 * P * (jt + 1)],
                                        start=(b == 0 and q % 2 == 0), stop=(b == NBLK - 1), skip_group_check=True)
                    if b == NBLK - 1:
                        ins.then_inc(s["f_done"], 1)

                for b in range(NBLK):
                    for w, bank in ((0, G[b % 2]), (1, U[b % 2])):
                        for k in range(KT):
                            ins = pe.matmul(bank[:], mem.W[k][:, w, P * b:P * (b + 1)],
                                            mem.xT[:, k, bass.ds(c4 * CH, CH)], start=(k == 0), stop=(k == KT - 1))
                        ins.then_inc(s["gate_act"] if w == 0 else s["gate_dve"], 1)
                    if b > 0:
                        down(b - 1)
                down(NBLK - 1)
                for x in t_.values():
                    x.give_back(pe)

        @block.scalar
        def _(act):
            t_ = {n: Tally(s[n]) for n in "gate_act poly f_done".split()}
            with act.Fori(0, NC) as c4:
                def square(b):
                    t_["gate_act"].need(act)
                    act.activation(sq[:, b % 2, :], G[b % 2][:], ACT.Square).then_inc(s["squared"], 1)

                square(0)
                for b in range(NBLK):
                    t_["poly"].need(act)
                    act.activation(th[:, b % 2, :], sq[:, b % 2, :], ACT.Tanh, scale=0.7978845608028654).then_inc(s["tanhed"], 1)
                    if b + 1 < NBLK:
                        square(b + 1)
                t_["f_done"].need(act)
                act.activation(thf[:], F[:], ACT.Tanh, scale=0.5).then_inc(s["f_tanhed"], 1)
                for x in t_.values():
                    x.give_back(act)

        @block.vector
        def _(v):
            own = Chain(v, s["dve"])
            t_ = {n: Tally(s[n]) for n in "gate_dve squared tanhed f_tanhed".split()}
            v.sem_inc(s["f_free"], 1)
            with v.Fori(0, NC) as c4:
                def poly(b):
                    t_["squared"].need(v)
                    own(v.tensor_scalar(sq[:, b % 2, :], sq[:, b % 2, :], 0.044715, 1.0, ALU.mult, ALU.add))
                    v.tensor_tensor(sq[:, b % 2, :], G[b % 2][:], sq[:, b % 2, :], ALU.mult).then_inc(s["poly"], 1)

                poly(0)
                for b in range(NBLK):
                    if b + 1 < NBLK:
                        poly(b + 1)
                    t_["tanhed"].need(v)
                    own(v.scalar_tensor_tensor(th[:, b % 2, :], th[:, b % 2, :], 1.0, G[b % 2][:], ALU.add, ALU.mult))
                    t_["gate_dve"].need(v)
                    v.scalar_tensor_tensor(hid[:, b % 2, :], th[:, b % 2, :], 0.5, U[b % 2][:], ALU.mult,
                                           ALU.mult).then_inc(s["hid_ready"], 1)
                t_["f_tanhed"].need(v)
                own(v.scalar_tensor_tensor(thf[:], thf[:], 1.0, F[:], ALU.add, ALU.mult))
                v.sem_inc(s["f_free"], 1)
                now = bass.ds(c4 * TPC, TPC)
                own(v.scalar_tensor_tensor(thf[:].rearrange("p a b -> p (a b)"), thf[:].rearrange("p a b -> p (a b)"), 0.5,
                                           mem.acc[:, now, :].rearrange("p a b -> p (a b)"), ALU.mult, ALU.mult))
                own(v.tensor_tensor(mem.x[:, now, :], mem.x[:, now, :], thf[:], ALU.add))
                for x in t_.values():
                    x.give_back(v)
                own.give_back()


def project1_phase(nc, io, mem, l1):
    with ExitStack() as ctx:
        sb = lambda n, s, d=F32: ctx.enter_context(nc.sbuf_tensor(n, s, d))
        ps = lambda n, s, d=F32: ctx.enter_context(nc.psum_tensor(n, s, d))
        sem = lambda n: ctx.enter_context(nc.semaphore("p1_" + n))
        w = {n: sb("w1" + n, [P, KT, D]) for n in "qkv"}
        wr = sb("w1r", [P, KT, E])
        bq, bk, bv = sb("bq", [P, KT]), sb("bk", [P, KT]), sb("bv", [P, D])
        bqs = sb("bqs", [P, KT])
        qk = sb("qk", [P, 2, KT, N])
        st, mv = sb("st1", [P, NT, 6]), sb("mv1", [P, NT, 2])
        rstd, mhalf = sb("rstd1", [P, NT]), sb("mhalf1", [P, NT])
        prob, prob2 = sb("prob", [P, NT, E]), sb("prob2", [P, NT, E])
        rmax, rsum = sb("rmax", [P, NT]), sb("rsum1", [P, NT])
        top, idx, idxf = sb("top", [P, NT, TOPK]), sb("idx", [P, NT, TOPK], U32), sb("idxf", [P, NT, TOPK])
        mask, seen = sb("mask1", [P, NT, E], BF16), sb("seen", [P, NT, E], BF16)
        before, ones = sb("before", [P, P], BF16), sb("ones_bf", [P, P], BF16)
        beforef, eid = sb("beforef", [P, P]), sb("eid", [P, E])
        pos = sb("pos", [P, NT, E])
        hit, hit2 = sb("hit", [P, TOPK, E]), sb("hit2", [P, TOPK, E])
        posk, valid = sb("posk", [P, NT, TOPK]), sb("valid", [P, NT, TOPK])
        tk = sb("tk", [P, NT, TOPK])
        TP = [ps(f"TQ{i}", [P, 4, P]) for i in range(2)]
        MP = [ps(f"MQ{i}", [P, CH]) for i in range(3)]
        LP = ps("LP", [P, NT, E])
        VP = ps("VQ", [P, 2, D])
        names = ("w_in stat_ready rstd_ready xn_ready turned t_out proj_done p_out v_done v_free logits_done "
                 "bias_ready shifted exped mask_ready pos_done dve pool qk_out rows_out")
        s = {n: sem(n) for n in names.split()}
        block = ctx.enter_context(nc.Block())

        @block.sync
        def _(sp):
            for n in "qkv":
                sp.dma_start(w[n][:], io[f"W{n}1"].rearrange("(k p) n -> p k n", p=P)).then_inc(s["w_in"], 16)
            sp.dma_start(wr[:], io["router"].rearrange("(k p) n -> p k n", p=P)).then_inc(s["w_in"], 16)
            sp.dma_start(bq[:], io["bq1"]).then_inc(s["w_in"], 16)
            sp.dma_start(bk[:], io["bk1"]).then_inc(s["w_in"], 16)
            sp.dma_start(bv[:], io["bv1"].rearrange("(a n) -> a n", a=1).broadcast_to([P, D])).then_inc(s["w_in"], 16)
            sp.dma_start(beforef[:], io["before"]).then_inc(s["w_in"], 16)
            sp.dma_start(eid[:], io["expert_ids"]).then_inc(s["w_in"], 16)
            sp.dma_start(mem.qd[:, HD, :], io["slopes"]).then_inc(s["rows_out"], 16)
            sp.dma_start(mem.kd[:, HD, :], io["places"]).then_inc(s["rows_out"], 16)
            for a, dst in enumerate((mem.qd, mem.kd)):
                for m in range(KT):
                    sp.wait_ge(s["p_out"], 4 * (KT * a + m) + 4)
                    for hh in range(8):
                        sp.dma_start(dst[8 * m + hh, 0:HD, :], qk[HD * hh:HD * (hh + 1), a, m, :]).then_inc(s["qk_out"], 16)
            sp.wait_ge(s["rows_out"], 2 * 16)
            sp.wait_ge(s["qk_out"], 32 * 16)

        @block.gpsimd
        def _(pool):
            pool.memset(mhalf[:], -0.5).then_inc(s["pool"], 1)
            pool.memset(ones[:], 1.0).then_inc(s["pool"], 1)
            pool.wait_ge(s["stat_ready"], NT)
            pool.tensor_scalar(rstd[:], mv[:, :, 1], EPS, None, ALU.add).then_inc(s["pool"], 1)
            pool.wait_ge(s["pool"], 3)
            pool.tensor_tensor(rstd[:], rstd[:], mhalf[:], ALU.pow).then_inc(s["rstd_ready"], 1)

        @block.tensor
        def _(pe):
            for t in range(NT):
                pe.wait_ge(s["xn_ready"], t + 1)
                if t % 2 == 0 and t >= 4:
                    pe.wait_ge(s["t_out"], t // 2 - 1)
                for j in range(KT):
                    ins = pe.transpose(TP[t // 2 % 2][:, 2 * (t % 2) + j, :], l1.xn[:, t, P * j:P * (j + 1)], mem.ident[:])
                if t % 2:
                    ins.then_inc(s["turned"], 1)
            pe.wait_ge(s["w_in"], 9 * 16)
            pe.wait_ge(s["t_out"], NT // 2)
            for t in range(NT):
                for j in range(KT):
                    ins = pe.matmul(LP[:, t, :], mem.xT[:, j, P * t:P * (t + 1)], wr[:, j, :], start=(j == 0), stop=(j == KT - 1))
            ins.then_inc(s["logits_done"], 1)
            n = 0
            for a, name in enumerate("qk"):
                for m in range(KT):
                    for i in range(NC):
                        if n >= 3:
                            pe.wait_ge(s["p_out"], n - 2)
                        for j in range(KT):
                            ins = pe.matmul(MP[n % 3][:], w[name][:, j, P * m:P * (m + 1)], mem.xT[:, j, CH * i:CH * (i + 1)],
                                            start=(j == 0), stop=(j == KT - 1))
                        ins.then_inc(s["proj_done"], 1)
                        n += 1
            for t in range(NT):
                if t >= 1:
                    pe.wait_ge(s["v_free"], t)
                for j in range(KT):
                    ins = pe.matmul(VP[:, 0, :], mem.xT[:, j, P * t:P * (t + 1)], w["v"][:, j, :], start=(j == 0), stop=(j == KT - 1))
                ins.then_inc(s["v_done"], 1)
            pe.wait_ge(s["mask_ready"], 1)
            for t in range(NT):
                ins = pe.matmul(LP[:, t, :], before[:], mask[:, t, :], start=True, stop=(t == 0))
                if t:
                    ins = pe.matmul(LP[:, t, :], ones[:], seen[:, t, :], start=False, stop=True)
            ins.then_inc(s["pos_done"], 1)

        @block.scalar
        def _(act):
            for n in range(NT // 2):
                act.wait_ge(s["turned"], n + 1)
                tp = TP[n % 2][:].rearrange("p (a k) c -> p k a c", a=2)
                dst = mem.xT[:, :, 2 * P * n:2 * P * (n + 1)].rearrange("p k (a c) -> p k a c", a=2)
                for j in range(KT):
                    ins = act.copy(dst[:, j], tp[:, j])
                ins.then_inc(s["t_out"], 1)
            act.wait_ge(s["w_in"], 9 * 16)
            act.mul(bqs[:], bq[:], float(HD) ** -0.5).then_inc(s["bias_ready"], 1)
            act.wait_ge(s["bias_ready"], 1)
            n = 0
            for a in range(2):
                for m in range(KT):
                    for i in range(NC):
                        act.wait_ge(s["proj_done"], n + 1)
                        act.activation(qk[:, a, m, CH * i:CH * (i + 1)], MP[n % 3][:], ACT.Identity,
                                       bias=(bqs, bk)[a][:, m:m + 1], scale=(float(HD) ** -0.5, 1.0)[a]).then_inc(s["p_out"], 1)
                        n += 1
                        if n == 6:
                            act.wait_ge(s["shifted"], 1)
                            act.activation(prob[:], prob[:], ACT.Exp).then_inc(s["exped"], 1)

        @block.vector
        def _(v):
            own = Chain(v, s["dve"])
            for t in range(NT):
                v.bn_stats(st[:, t, :], mem.x[:, t, :]).then_inc(s["dve"], 1)
                own.t.n += 1
            v.wait_ge(s["dve"], own.t.n)
            for t in range(NT):
                v.bn_aggr(mv[:, t, :], st[:, t, :]).then_inc(s["stat_ready"], 1)
            v.wait_ge(s["rstd_ready"], 1)
            for t in range(NT):
                v.tensor_scalar(l1.xn[:, t, :], mem.x[:, t, :], mv[:, t, 0:1], rstd[:, t:t + 1],
                                ALU.subtract, ALU.mult).then_inc(s["xn_ready"], 1)
            v.wait_ge(s["w_in"], 9 * 16)
            own(v.tensor_copy(before[:], beforef[:]))
            v.wait_ge(s["logits_done"], 1)
            own(v.tensor_reduce(rmax[:], LP[:], AX.X, ALU.max))
            v.tensor_tensor(prob[:], LP[:], rmax[:].rearrange("p (t a) -> p t a", a=1).broadcast_to([P, NT, E]),
                            ALU.subtract).then_inc(s["shifted"], 1)
            v.wait_ge(s["exped"], 1)
            own(v.tensor_reduce(rsum[:], prob[:], AX.X, ALU.add))
            own(v.reciprocal(rsum[:], rsum[:]))
            own(v.tensor_tensor(prob[:], prob[:], rsum[:].rearrange("p (t a) -> p t a", a=1).broadcast_to([P, NT, E]), ALU.mult))
            for t in range(NT):
                v.max(top[:, t, :], prob[:, t, :]).then_inc(s["dve"], 1)
                own.t.n += 1
            v.wait_ge(s["dve"], own.t.n)
            for t in range(NT):
                v.max_index(idx[:, t, :], top[:, t, :], prob[:, t, :]).then_inc(s["dve"], 1)
                v.match_replace(prob2[:, t, :], top[:, t, :], prob[:, t, :], -1.0).then_inc(s["dve"], 1)
                own.t.n += 2
            v.wait_ge(s["dve"], own.t.n)
            own(v.tensor_scalar(mask[:], prob2[:], 0.0, None, ALU.is_lt))
            own(v.tensor_copy(seen[:, 1, :], mask[:, 0, :]))
            for t in range(2, NT):
                own(v.tensor_tensor(seen[:, t, :], seen[:, t - 1, :], mask[:, t - 1, :], ALU.add))
            v.sem_inc(s["mask_ready"], 1)
            own(v.tensor_reduce(rsum[:], top[:], AX.X, ALU.add))
            own(v.reciprocal(rsum[:], rsum[:]))
            own(v.tensor_tensor(top[:], top[:], rsum[:].rearrange("p (t a) -> p t a", a=1).broadcast_to([P, NT, TOPK]), ALU.mult))
            own(v.tensor_copy(idxf[:], idx[:]))
            for t in range(NT):
                v.wait_ge(s["v_done"], t + 1)
                v.tensor_tensor(mem.v1[:, t, :], VP[:, 0, :], bv[:], ALU.add).then_inc(s["v_free"], 1)
            v.wait_ge(s["pos_done"], 1)
            own(v.tensor_copy(pos[:], LP[:]))
            for t in range(NT):
                own(v.tensor_tensor(hit[:], eid[:].rearrange("p (a e) -> p a e", a=1).broadcast_to([P, TOPK, E]),
                                    idxf[:, t, :].rearrange("p (k a) -> p k a", a=1).broadcast_to([P, TOPK, E]), ALU.is_equal))
                own(v.tensor_tensor(hit2[:], hit[:], pos[:, t, :].rearrange("p (a e) -> p a e", a=1).broadcast_to([P, TOPK, E]), ALU.mult))
                own(v.tensor_reduce(posk[:, t, :], hit2[:], AX.X, ALU.add))
            own(v.tensor_scalar(valid[:], posk[:], float(CAP), None, ALU.is_lt))
            own(v.tensor_tensor(l1.weight[:], top[:], valid[:], ALU.mult))
            own(v.tensor_scalar(posk[:], posk[:], float(CAP - 1), None, ALU.min))
            own(v.scalar_tensor_tensor(posk[:], idxf[:], float(CAP), posk[:], ALU.mult, ALU.add))
            own(v.tensor_copy(l1.take[:], posk[:]))
            own(v.tensor_scalar(tk[:], valid[:], -float(E * CAP), float(E * CAP), ALU.mult, ALU.add))
            own(v.tensor_tensor(tk[:], posk[:], tk[:], ALU.add))
            own(v.tensor_copy(l1.send[:], tk[:]))


def attention1_phase(nc, io, mem, l1, part, pool_work):
    with ExitStack() as ctx:
        sb = lambda n, s, d=F32: ctx.enter_context(nc.sbuf_tensor(f"{n}_{part}", s, d))
        ps = lambda n, s, d=F32: ctx.enter_context(nc.psum_tensor(f"{n}_{part}", s, d))
        sem = lambda n: ctx.enter_context(nc.semaphore(f"a1{part}_" + n))
        qr = sb("qr", [P, 2, N])
        kr = sb("kr", [P, 2, CH])
        vh = sb("vh", [P, 2, NT, HD])
        probs = sb("probs1", [P, 2, N])
        PT = sb("PT1", [P, 4, CH])
        negmax, rowsum, rinv = sb("negmax1", [P, 2]), sb("rowsum1", [P, 4]), sb("rinv1", [P, 2])
        S = ps("S1", [P, N])
        T = [ps(f"T1{i}", [P, CH]) for i in range(2)]
        O = [ps(f"O1{i}", [P, CH]) for i in range(2)]
        names = ("qk_in0 qk_in1 qk_free v_ready scores_done negmax_ready probs_done turned_dve turned_act "
                 "pt_dve pt_act o_done o_free o_seen dve")
        s = {n: sem(n) for n in names.split()}
        order = [(0, t) for t in range(NT)] + [(1, t) for t in range(NT - 1, -1, -1)]
        PAIRS = HEADS // 4
        first = PAIRS * part
        block = ctx.enter_context(nc.Block())

        @block.gpsimd
        def _(pool):
            pool_work(pool)

        @block.sync
        def _(sp):
            qk_free = Tally(s["qk_free"])
            with sp.Fori(first, first + PAIRS) as pair:
                for u in range(2):
                    qk_free.need(sp)
                    for r in range(4):
                        sp.dma_start(qr[32 * r:32 * r + KA, u, :],
                                     mem.qd[bass.ds(pair * 2 + u, 1)].rearrange("a k n -> (a k) n")).then_inc(s[f"qk_in{u}"], 16)
                        sp.dma_start(kr[32 * r:32 * r + KA, u, :],
                                     mem.kd[bass.ds(pair * 2 + u, 1), :, CH * r:CH * (r + 1)].rearrange("a k n -> (a k) n")).then_inc(s[f"qk_in{u}"], 16)
                qk_free.give_back(sp)

        @block.tensor
        def _(pe):
            t_ = {n: Tally(s[n]) for n in "qk_in0 qk_in1 v_ready probs_done pt_dve pt_act o_free".split()}

            def scores(u, t):
                nk = P * (t + 1)
                nch = -(-nk // CH)
                for r in range(nch):
                    w = min(CH, nk - CH * r)
                    pe.matmul(S[:, CH * r:CH * r + w], qr[32 * r:32 * r + KA, u, P * t:P * (t + 1)],
                              kr[32 * r:32 * r + KA, u, 0:w], start=True, stop=(r < nch - 1), tile_position=(32 * r, 0))
                pe.matmul(S[:, nk - P:nk], mem.ident_bf[:], mem.mask_bf[:], start=False, stop=True).then_inc(s["scores_done"], 1)

            with pe.Fori(first, first + PAIRS) as pair:
                g_at = 0
                t_["qk_in0"].need(pe, 8 * 16)
                scores(*order[0])
                for i, (u, t) in enumerate(order):
                    t_["probs_done"].need(pe)
                    if i + 1 < len(order):
                        if i + 1 == NT:
                            t_["qk_in1"].need(pe, 8 * 16)
                        scores(*order[i + 1])
                    if t == (0, NT - 1)[u]:
                        t_["v_ready"].need(pe)
                    groups = groups_of(t)
                    na = act_copies(len(groups))

                    def weigh(g):
                        b0, w = groups[g]
                        t_["pt_act" if g < na else "pt_dve"].need(pe)
                        if g == 0:
                            t_["o_free"].need(pe)
                        for b in range(b0, b0 + w):
                            ins = pe.matmul(O[i % 2][:, 0:HD], PT[:, (g_at + g) % 4, P * (b - b0):P * (b - b0 + 1)],
                                            vh[:, u, b, :], start=(b == 0), stop=(b == t))
                        if g == len(groups) - 1:
                            ins.then_inc(s["o_done"], 1)

                    for g, (b0, w) in enumerate(groups):
                        for b in range(b0, b0 + w):
                            ins = pe.transpose(T[(g_at + g) % 2][:, P * (b - b0):P * (b - b0 + 1)],
                                               probs[:, i % 2, P * b:P * (b + 1)], mem.ident[:])
                        ins.then_inc(s["turned_act"] if g < na else s["turned_dve"], 1)
                        if g > 0:
                            weigh(g - 1)
                    weigh(len(groups) - 1)
                    g_at += len(groups)
                for x in t_.values():
                    x.give_back(pe)

        @block.vector
        def _(v):
            own = Chain(v, s["dve"])
            t_ = {n: Tally(s[n]) for n in "scores_done turned_dve o_done".split()}
            v.sem_inc(s["o_free"], 2)
            v.sem_inc(s["qk_free"], 2)

            with v.Fori(first, first + PAIRS) as pair:
                def row_max(i):
                    t_["scores_done"].need(v)
                    v.tensor_reduce(negmax[:, i % 2:i % 2 + 1], S[:, 0:P * (order[i][1] + 1)], AX.X, ALU.max,
                                    negate=True).then_inc(s["negmax_ready"], 1)

                def finish(i):
                    u, t = order[i]
                    t_["o_done"].need(v)
                    own(v.reciprocal(rinv[:, i % 2:i % 2 + 1], rowsum[:, i % 4:i % 4 + 1]))
                    v.tensor_scalar(mem.ctx[:, t, bass.ds(pair * 2 * HD + u * HD, HD)], O[i % 2][:, 0:HD], rinv[:, i % 2:i % 2 + 1], None,
                                    ALU.mult).then_inc(s["o_free"], 1)
                    if t == (NT - 1, 0)[u]:
                        v.sem_inc(s["qk_free"], 1)

                for u in range(2):
                    v.tensor_copy(vh[:, u], mem.v1[:, :, bass.ds(pair * 2 * HD + u * HD, HD)]).then_inc(s["v_ready"], 1)
                row_max(0)
                g_at = 0
                for i, (u, t) in enumerate(order):
                    if i + 1 < len(order):
                        row_max(i + 1)
                    groups = groups_of(t)
                    for g in range(act_copies(len(groups)), len(groups)):
                        w = groups[g][1] * P
                        t_["turned_dve"].need(v)
                        v.tensor_copy(PT[:, (g_at + g) % 4, 0:w], T[(g_at + g) % 2][:, 0:w]).then_inc(s["pt_dve"], 1)
                    g_at += len(groups)
                    if i > 0:
                        finish(i - 1)
                finish(len(order) - 1)
                for x in t_.values():
                    x.give_back(v)
                own.give_back()

        @block.scalar
        def _(act):
            t_ = {n: Tally(s[n]) for n in "negmax_ready turned_act".split()}

            def exponent(i):
                nk = P * (order[i][1] + 1)
                t_["negmax_ready"].need(act)
                act.activation(probs[:, i % 2, 0:nk], S[:, 0:nk], ACT.Exp, bias=negmax[:, i % 2:i % 2 + 1],
                               accum_out=rowsum[:, i % 4:i % 4 + 1]).then_inc(s["probs_done"], 1)

            with act.Fori(first, first + PAIRS) as pair:
                exponent(0)
                g_at = 0
                for i, (u, t) in enumerate(order):
                    groups = groups_of(t)
                    for g in range(act_copies(len(groups))):
                        w = groups[g][1] * P
                        t_["turned_act"].need(act)
                        act.copy(PT[:, (g_at + g) % 4, 0:w], T[(g_at + g) % 2][:, 0:w]).then_inc(s["pt_act"], 1)
                    g_at += len(groups)
                    if i + 1 < len(order):
                        exponent(i + 1)
                for x in t_.values():
                    x.give_back(act)


def experts_phase(nc, io, mem, l1):
    with ExitStack() as ctx:
        sb = lambda n, s, d=F32: ctx.enter_context(nc.sbuf_tensor(n, s, d))
        ps = lambda n, s, d=F32: ctx.enter_context(nc.psum_tensor(n, s, d))
        sem = lambda n: ctx.enter_context(nc.semaphore("e_" + n))
        rows = sb("rows", [P, 2, EG, D])
        wg, wu = sb("wg", [P, 2, EG, KT, I]), sb("wu", [P, 2, EG, KT, I])
        wd = sb("wd", [I, 2, EG, D])
        rT = sb("rT", [P, 2, EG, KT, P])
        th, hid = sb("the", [I, EG, P]), sb("hide", [I, EG, P])
        res = sb("res", [P, 2, EG, D])
        RT = ps("RT", [P, EG, KT, P])
        G, U = ps("GE", [I, EG, P]), ps("UE", [I, EG, P])
        R = ps("RE", [P, EG, D])
        names = ("in0 in1 in_free turned_act turned_dve rT_act rT_dve gate_done up_done tanhed hid_ready "
                 "res_done r_free copied stored0 stored1 dve")
        s = {n: sem(n) for n in names.split()}
        block = ctx.enter_context(nc.Block())
        ITER = E // EG // 2

        def first_expert(it, u):
            return it * 2 * EG + u * EG

        @block.sync
        def _(sp):
            in_free = Tally(s["in_free"])
            with sp.Fori(0, ITER) as it:
                for u in range(2):
                    in_free.need(sp)
                    e0 = first_expert(it, u)
                    sp.dma_start(rows[:, u], mem.xe[bass.ds(e0 * CAP, EG * CAP), :].rearrange("(e p) c -> p e c", p=P)).then_inc(s[f"in{u}"], 16)
                    for wt, src in ((wg, "gate"), (wu, "up")):
                        sp.dma_start(wt[:, u].rearrange("p e k i -> p (e k) i"),
                                     io[src][bass.ds(e0, EG)].rearrange("e (k p) i -> p (e k) i", p=P)).then_inc(s[f"in{u}"], 16)
                    sp.dma_start(wd[:, u], io["down"][bass.ds(e0, EG)].rearrange("e i d -> i e d")).then_inc(s[f"in{u}"], 16)
                in_free.give_back(sp)

        @block.tensor
        def _(pe):
            t_ = {n: Tally(s[n]) for n in "in0 in1 rT_act rT_dve hid_ready r_free".split()}

            def turn(u):
                t_[f"in{u}"].need(pe, 4 * 16)
                for e in range(EG):
                    for k in range(KT):
                        ins = pe.transpose(RT[:, e, k, :], rows[:, u, e, P * k:P * (k + 1)], mem.ident[:])
                    if e == 1:
                        ins.then_inc(s["turned_act"], 1)
                ins.then_inc(s["turned_dve"], 1)

            def gate_up(u):
                t_["rT_act"].need(pe)
                t_["rT_dve"].need(pe)
                for wt, bank, done in ((wg, G, "gate_done"), (wu, U, "up_done")):
                    for e in range(EG):
                        for k in range(KT):
                            ins = pe.matmul(bank[:, e, :], wt[:, u, e, k, :], rT[:, u, e, k, :],
                                            start=(k == 0), stop=(k == KT - 1))
                    ins.then_inc(s[done], 1)

            def down(u):
                t_["hid_ready"].need(pe)
                t_["r_free"].need(pe)
                for e in range(EG):
                    ins = pe.matmul(R[:, e, :], hid[:, e, :], wd[:, u, e, :], start=True, stop=True)
                ins.then_inc(s["res_done"], 1)

            with pe.Fori(0, ITER) as it:
                turn(0)
                gate_up(0)
                turn(1)
                down(0)
                gate_up(1)
                down(1)
                for x in t_.values():
                    x.give_back(pe)

        @block.scalar
        def _(act):
            own = Chain(act, s["copied"])
            t_ = {n: Tally(s[n]) for n in "turned_act gate_done res_done stored0 stored1".split()}
            act.sem_inc(s["r_free"], 1)
            act.sem_inc(s["in_free"], 2)
            act.sem_inc(s["stored0"], 16)
            act.sem_inc(s["stored1"], 16)
            with act.Fori(0, ITER) as it:
                def turned(u):
                    t_["turned_act"].need(act)
                    act.copy(rT[:, u, 0:2], RT[:, 0:2]).then_inc(s["rT_act"], 1)

                def tanh_half():
                    t_["gate_done"].need(act)
                    act.activation(th[:], G[:], ACT.Tanh, scale=0.5).then_inc(s["tanhed"], 1)

                def store(u):
                    t_["res_done"].need(act)
                    t_[f"stored{u}"].need(act, 16)
                    act.sem_inc(s["in_free"], 1)
                    own(act.copy(res[:, u], R[:]))
                    act.sem_inc(s["r_free"], 1)
                    act.dma_start(mem.ye[bass.ds(first_expert(it, u) * CAP, EG * CAP), :].rearrange("(e p) c -> p e c", p=P),
                                  res[:, u]).then_inc(s[f"stored{u}"], 16)

                turned(0)
                tanh_half()
                turned(1)
                store(0)
                tanh_half()
                store(1)
                for x in t_.values():
                    x.give_back(act)
                own.give_back()
            act.wait_ge(s["stored0"], 16)
            act.wait_ge(s["stored1"], 16)

        @block.vector
        def _(v):
            own = Chain(v, s["dve"])
            t_ = {n: Tally(s[n]) for n in "turned_dve up_done tanhed".split()}
            with v.Fori(0, ITER) as it:
                def turned(u):
                    t_["turned_dve"].need(v)
                    v.tensor_copy(rT[:, u, 2:4], RT[:, 2:4]).then_inc(s["rT_dve"], 1)

                def hidden():
                    t_["tanhed"].need(v)
                    own(v.scalar_tensor_tensor(th[:], th[:], 1.0, G[:], ALU.add, ALU.mult))
                    t_["up_done"].need(v)
                    v.scalar_tensor_tensor(hid[:], th[:], 0.5, U[:], ALU.mult, ALU.mult).then_inc(s["hid_ready"], 1)

                turned(0)
                turned(1)
                hidden()
                hidden()
                for x in t_.values():
                    x.give_back(v)
                own.give_back()


def output_phase(nc, io, mem, l1):
    with ExitStack() as ctx:
        sb = lambda n, s, d=F32: ctx.enter_context(nc.sbuf_tensor(n, s, d))
        ps = lambda n, s, d=F32: ctx.enter_context(nc.psum_tensor(n, s, d))
        sem = lambda n: ctx.enter_context(nc.semaphore("o_" + n))
        wo = sb("wo1", [P, KT, D])
        bo = sb("bo", [P, D])
        th = sb("tho", [P, NT, D])
        att = sb("att", [P, 2, 2, D])
        TP = [ps(f"TO{i}", [P, 4, P]) for i in range(2)]
        Y = [ps(f"YO{i}", [P, 2, D]) for i in range(2)]
        s = {n: sem(n) for n in "w_in turned t_out y_done y_free tanhed out_ready stored dve".split()}
        block = ctx.enter_context(nc.Block())
        PAIRS = NT // 2

        @block.sync
        def _(sp):
            sp.dma_start(wo[:], io["Wo1"].rearrange("(k p) n -> p k n", p=P)).then_inc(s["w_in"], 16)
            sp.dma_start(bo[:], io["bo1"].rearrange("(a n) -> a n", a=1).broadcast_to([P, D])).then_inc(s["w_in"], 16)
            ov = io["out"][0].rearrange("(t p) c -> p t c", p=P)
            for n in range(PAIRS):
                sp.wait_ge(s["out_ready"], n + 1)
                sp.dma_start(ov[:, 2 * n:2 * n + 2, :], mem.x[:, 2 * n:2 * n + 2, :]).then_inc(s["stored"], 16)
            sp.wait_ge(s["stored"], 16 * PAIRS)

        @block.tensor
        def _(pe):
            def turn(n):
                if n >= 2:
                    pe.wait_ge(s["t_out"], n - 1)
                for a in range(2):
                    for j in range(KT):
                        ins = pe.transpose(TP[n % 2][:, 2 * a + j, :], mem.ctx[:, 2 * n + a, P * j:P * (j + 1)], mem.ident[:])
                ins.then_inc(s["turned"], 1)

            turn(0)
            pe.wait_ge(s["w_in"], 2 * 16)
            for n in range(PAIRS):
                if n + 1 < PAIRS:
                    turn(n + 1)
                pe.wait_ge(s["t_out"], n + 1)
                if n >= 2:
                    pe.wait_ge(s["y_free"], n - 1)
                for a in range(2):
                    t = 2 * n + a
                    for j in range(KT):
                        ins = pe.matmul(Y[n % 2][:, a, :], mem.xT[:, j, P * t:P * (t + 1)], wo[:, j, :],
                                        start=(j == 0), stop=(j == KT - 1))
                ins.then_inc(s["y_done"], 1)

        @block.scalar
        def _(act):
            for n in range(PAIRS):
                act.activation(th[:, 2 * n:2 * n + 2, :], mem.f[:, 2 * n:2 * n + 2, :], ACT.Tanh, scale=0.5).then_inc(s["tanhed"], 1)
                act.wait_ge(s["turned"], n + 1)
                tp = TP[n % 2][:].rearrange("p (a k) c -> p k a c", a=2)
                dst = mem.xT[:, :, 2 * P * n:2 * P * (n + 1)].rearrange("p k (a c) -> p k a c", a=2)
                act.copy(dst[:, 0], tp[:, 0])
                act.copy(dst[:, 1], tp[:, 1]).then_inc(s["t_out"], 1)

        @block.vector
        def _(v):
            own = Chain(v, s["dve"])
            v.wait_ge(s["w_in"], 2 * 16)
            bias = bo[:].rearrange("p (a c) -> p a c", a=1).broadcast_to([P, 2, D])
            for n in range(PAIRS):
                now = slice(2 * n, 2 * n + 2)
                v.wait_ge(s["tanhed"], n + 1)
                own(v.scalar_tensor_tensor(th[:, now, :], th[:, now, :], 1.0, mem.f[:, now, :], ALU.add, ALU.mult))
                v.wait_ge(s["y_done"], n + 1)
                v.tensor_tensor(att[:, n % 2], Y[n % 2][:], bias, ALU.add).then_inc(s["y_free"], 1)
                v.wait_ge(s["y_free"], n + 1)
                own(v.scalar_tensor_tensor(th[:, now, :], th[:, now, :], 0.5, att[:, n % 2], ALU.mult, ALU.mult))
                v.tensor_tensor(mem.x[:, now, :], mem.x[:, now, :], th[:, now, :], ALU.add).then_inc(s["out_ready"], 1)


def layer1(nc, io, mem):
    l1 = Memory()
    with ExitStack() as ctx:
        sb = lambda n, s, d=F32: ctx.enter_context(nc.sbuf_tensor(n, s, d))
        sem = lambda n: ctx.enter_context(nc.semaphore("l1_" + n))
        l1.xn = sb("xn1", [P, NT, D])
        l1.weight = sb("weight", [P, NT, TOPK])
        l1.take, l1.send = sb("take", [P, NT, TOPK], U32), sb("send", [P, NT, TOPK], U32)
        mem.v1 = sb("v1", [P, NT, D])
        mem.f = sb("f", [P, NT, D])
        mem.ctx = mem.acc
        got = sb("got", [P, 2, TOPK, D])
        sent, taken, pool = sem("sent"), [sem("taken0"), sem("taken1")], sem("pool")
        project1_phase(nc, io, mem, l1)

        def send_rows(eng):
            eng.wait_ge(mem.xe_zeroed, 8 * 16)
            for t in range(NT):
                for k in range(TOPK):
                    eng.indirect_dma_start(mem.xe, bass.IndirectOffsetOnAxis(l1.send[:, t, k:k + 1], 0), l1.xn[:, t, :], None,
                                           bounds_check=E * CAP - 1, oob_is_err=False).then_inc(sent, 16)
            eng.wait_ge(sent, 16 * NT * TOPK)

        def take_rows(eng):
            own = Chain(eng, pool)

            def combine(t):
                g = got[:, t % 2]
                eng.wait_ge(taken[t % 2], 16 * TOPK * (t // 2 + 1))
                w = l1.weight[:, t, :].rearrange("p (k a) -> p k a", a=1).broadcast_to([P, TOPK, D])
                own(eng.tensor_tensor(g, g, w, ALU.mult))
                own(eng.tensor_tensor(g[:, 0:4], g[:, 0:4], g[:, 4:8], ALU.add))
                own(eng.tensor_tensor(g[:, 0:2], g[:, 0:2], g[:, 2:4], ALU.add))
                own(eng.tensor_tensor(mem.f[:, t, :], g[:, 0], g[:, 1], ALU.add))

            for t in range(NT):
                for k in range(TOPK):
                    eng.indirect_dma_start(got[:, t % 2, k, :], None, mem.ye, bass.IndirectOffsetOnAxis(l1.take[:, t, k:k + 1], 0),
                                           bounds_check=E * CAP - 1, oob_is_err=False).then_inc(taken[t % 2], 16)
                if t:
                    combine(t - 1)
            combine(NT - 1)

        attention1_phase(nc, io, mem, l1, 0, send_rows)
        experts_phase(nc, io, mem, l1)
        attention1_phase(nc, io, mem, l1, 1, take_rows)
        output_phase(nc, io, mem, l1)


class Memory:
    pass


def build(nc, io):
    c = None
    mem = Memory()
    with ExitStack() as ctx:
        sb = lambda n, s, d=F32: ctx.enter_context(nc.sbuf_tensor(n, s, d))
        sem = lambda n: ctx.enter_context(nc.semaphore(n))
        dram = lambda n, s, d=F32: nc.dram_tensor(n, s, d, kind="Internal").ap()
        mem.xe = dram("xe", [E * CAP, D])
        mem.ye = dram("ye", [E * CAP, D])
        mem.qd = dram("qd", [HEADS, KA, N])
        mem.kd = dram("kd", [HEADS, KA, N])
        mem.casts, mem.xe_zeroed = sem("casts"), sem("xe_zeroed")
        mem.x = sb("x", [P, NT, D])
        mem.acc = sb("acc", [P, NT, D])
        mem.xT = sb("xT", [P, KT, N])
        mem.ident = sb("ident", [P, P])
        mem.ident_bf = sb("ident_bf", [P, P], BF16)
        mem.mask_bf = sb("mask_bf", [P, P], BF16)
        with ExitStack() as layer0:
            sb0 = lambda n, s, d=F32: layer0.enter_context(nc.sbuf_tensor(n, s, d))
            mem.W = [sb0(f"W{i}", [P, 3, N]) for i in range(2)]
            with ExitStack() as attn0:
                sba = lambda n, s, d=F32: attn0.enter_context(nc.sbuf_tensor(n, s, d))
                mem.gxT = sba("gxT", [P, KT, N])
                mem.cos = sba("cosT", [P, N])
                mem.sin = sba("sinT", [P, N])
                mem.kT = sba("kT", [P, N])
                mem.v = sba("v", [P, NT, DH])
                setup_phase(nc, c, io, mem)
                attention0_phase(nc, c, io, mem)
            mlp0_phase(nc, c, io, mem)
        layer1(nc, io, mem)


def constants():
    inv = (1.0 / 10000.0 ** (np.arange(0, DH, 2, dtype=np.float32) / np.float32(DH))).astype(np.float32)
    freqs = (np.arange(N, dtype=np.float32)[:, None] * inv[None, :]).astype(np.float32).T
    cos, sin = np.cos(freqs).astype(np.float32), np.sin(freqs).astype(np.float32)
    slopes = (np.float32(2.0 ** (-8.0 / HEADS)) ** np.arange(1, HEADS + 1, dtype=np.float32)).astype(np.float32)
    r = np.arange(P)
    return {
        "cos": np.concatenate([cos, cos]),
        "sin": np.concatenate([sin, -sin]),
        "identity": np.eye(P, dtype=np.float32),
        "causal": np.where(r[None, :] > r[:, None], np.float32(NEG), np.float32(0)).astype(np.float32),
        "before": (r[:, None] < r[None, :]).astype(np.float32),
        "slopes": np.ascontiguousarray(np.broadcast_to(slopes[:, None], (HEADS, N))).astype(np.float32),
        "places": np.ascontiguousarray(np.broadcast_to(np.arange(1 - N, 1, dtype=np.float32), (HEADS, N))),
        "expert_ids": np.ascontiguousarray(np.broadcast_to(np.arange(E, dtype=np.float32), (P, E))),
    }


def layouts(a):
    def gate_like(w):
        return w.reshape(8, P, 2, -1).transpose(0, 2, 3, 1).reshape(NBLK, -1, P)

    def down_like(w, k):
        return w.reshape(2, P, 8, k).transpose(2, 0, 3, 1).reshape(NBLK, k, P)

    def col(w):
        return w.reshape(KT, P).T

    packed = [gate_like(a["L0_ffn_gate_W_packed"]), gate_like(a["L0_ffn_up_W_packed"]),
              down_like(a["L0_ffn_down_W_packed"], P)]
    scales = [gate_like(a["L0_ffn_gate_scales"]), gate_like(a["L0_ffn_up_scales"]),
              down_like(a["L0_ffn_down_scales"], 8)]
    wq = a["L0_attn_Wq"].reshape(D, HEADS, DH).transpose(1, 0, 2)
    out = {
        "x": a["L0_attn_x"], "gamma": col(a["L0_attn_gamma"]), "Wkv": a["L0_attn_Wkv"], "Wo": a["L0_attn_Wo"],
        "Wq": np.concatenate([wq, wq[:1]]),
        "packed": np.stack(packed, axis=2), "scales": np.stack(scales, axis=2),
        "Wq1": a["L1_attn_Wq"], "Wk1": a["L1_attn_Wk"], "Wv1": a["L1_attn_Wv"], "Wo1": a["L1_attn_Wo"],
        "bq1": col(a["L1_attn_bq"]), "bk1": col(a["L1_attn_bk"]), "bv1": a["L1_attn_bv"], "bo1": a["L1_attn_bo"],
        "router": a["L1_ffn_router_weight"], "gate": a["L1_ffn_gate_proj"], "up": a["L1_ffn_up_proj"],
        "down": a["L1_ffn_down_proj"],
    }
    return {k: np.ascontiguousarray(v) for k, v in out.items()}


def kernel(**inputs):
    import concourse.bacc as bacc
    from concourse.bass_utils import run_bass_kernel_spmd

    nc = bacc.Bacc("TRN2", target_bir_lowering=False, num_devices=1)
    arrays, io = {}, {}
    for name, a in {**layouts({k: np.asarray(v) for k, v in inputs.items()}), **constants()}.items():
        arrays["in_" + name] = a
        io[name] = nc.dram_tensor("in_" + name, a.shape, mybir.dt.from_np(a.dtype), kind="ExternalInput").ap()
    io["out"] = nc.dram_tensor("out", [1, N, D], F32, kind="ExternalOutput").ap()
    build(nc, io)
    r = run_bass_kernel_spmd(nc, [arrays], core_ids=[0])
    return r.results[0]["out"]
```

```python
import math
from contextlib import ExitStack

import numpy as np

import concourse.bass as bass
from concourse import mybir

F32 = mybir.dt.float32
BF16 = mybir.dt.bfloat16
I32 = mybir.dt.int32
U32 = mybir.dt.uint32
ALU = mybir.AluOpType
ACT = mybir.ActivationFunctionType
AX = mybir.AxisListType

P = 128
N = 2048
D = 256
NT = N // P
KT = D // P
CH = 512
NC = N // CH
TPC = CH // P
EPS = 1e-5
HEADS = 16
DH = 128
HD = D // HEADS
KA = HD + 1
PARTS = [(0, 0), (1, 0), (2, 0), (0, 1), (1, 1), (0, 2)]
KS = len(PARTS) * (HD + 1)
KM = KS + 3
NBLK = 16
E, I, TOPK = 64, 96, 8
CAP = 2 * (512 * TOPK) // E
EG = 4
NEG = -3.0e38


class Tally:

    def __init__(self, sem):
        self.sem = sem
        self.n = 0

    def need(self, eng, k=1):
        self.n += k
        eng.wait_ge(self.sem, self.n)

    def give_back(self, eng):
        if self.n:
            eng.sem_inc(self.sem, -self.n)
        self.n = 0


class Chain:

    def __init__(self, eng, sem):
        self.eng = eng
        self.t = Tally(sem)

    def __call__(self, ins):
        ins.then_inc(self.t.sem, 1)
        self.t.need(self.eng)

    def give_back(self):
        self.t.give_back(self.eng)


def groups_of(t):
    return [(b, min(4, t + 1 - b)) for b in range(0, t + 1, 4)]


def act_copies(ng):
    return (ng + 1) // 2


def setup_phase(nc, c, io, mem):
    with ExitStack() as ctx:
        sb = lambda n, s, d=F32: ctx.enter_context(nc.sbuf_tensor(n, s, d))
        ps = lambda n, s, d=F32: ctx.enter_context(nc.psum_tensor(n, s, d))
        sem = lambda n: ctx.enter_context(nc.semaphore(n))
        xn = sb("xn0", [P, NT, D])
        xg = sb("xg", [P, NT, D])
        st = sb("st0", [P, 2, NT, 6])
        mv = sb("mv0", [P, 2, NT, 2])
        rstd = sb("rstd0", [P, 2, NT])
        mhalf = sb("mhalf0", [P, NT])
        wkv = sb("wkv", [P, KT, 2 * DH])
        gam = sb("gam", [P, KT])
        maskf = sb("maskf", [P, 2, P])
        ra = sb("rope_a0", [P, CH])
        rb = sb("rope_b0", [P, CH])
        zeros = sb("zeros", [P, 2048])
        TP = [ps(f"TP{i}", [P, 4, P]) for i in range(4)]
        KP = [ps(f"KP{i}", [P, CH]) for i in range(2)]
        VP = [ps(f"VP{i}", [P, CH]) for i in range(2)]
        x_in = [sem(f"x_in{i}") for i in range(NC)]
        const_in, wkv_in, zero_set = sem("const_in"), sem("wkv_in"), sem("zero_set")
        pool0 = sem("pool0")
        dve0, stat_ready, rstd_ready = sem("dve0"), sem("stat_ready"), sem("rstd_ready")
        xn_ready, xg_ready = sem("xn_ready"), sem("xg_ready")
        turned, t_out = sem("turned0"), sem("t_out0")
        k_done, k_free, v_done, v_out = sem("k_done"), sem("k_free"), sem("v_done"), sem("v_out")
        block = ctx.enter_context(nc.Block())

        @block.sync
        def _(sp):
            xv = io["x"][0].rearrange("(t p) c -> p t c", p=P)
            for i in range(NC):
                sp.dma_start(mem.x[:, TPC * i:TPC * (i + 1), :], xv[:, TPC * i:TPC * (i + 1), :]).then_inc(x_in[i], 16)
            sp.dma_start(mem.ident[:], io["identity"]).then_inc(const_in, 16)
            sp.dma_start(maskf[:, 0], io["causal"]).then_inc(const_in, 16)
            sp.dma_start(maskf[:, 1], io["causalT"]).then_inc(const_in, 16)
            sp.dma_start(gam[:], io["gamma"]).then_inc(const_in, 16)
            sp.dma_start(mem.cos[:], io["cos"]).then_inc(const_in, 16)
            sp.dma_start(mem.sin[:], io["sin"]).then_inc(const_in, 16)
            sp.dma_start(wkv[:], io["Wkv"].rearrange("(k p) n -> p k n", p=P)).then_inc(wkv_in, 16)
            sp.wait_ge(zero_set, 1)
            zv = mem.xe.rearrange("(a p r) c -> a p (r c)", a=8, p=P)
            for a in range(8):
                sp.dma_start(zv[a], zeros[:]).then_inc(mem.xe_zeroed, 16)
            sp.wait_ge(mem.xe_zeroed, 8 * 16)

        @block.gpsimd
        def _(pool):
            pool.memset(zeros[:], 0.0).then_inc(zero_set, 1)
            pool.memset(mhalf[:], -0.5).then_inc(pool0, 1)
            for k in range(2):
                pool.wait_ge(stat_ready, NT * (k + 1))
                pool.tensor_scalar(rstd[:, k, :], mv[:, k, :, 1], EPS, None, ALU.add).then_inc(pool0, 1)
                pool.wait_ge(pool0, k + 2)
                pool.tensor_tensor(rstd[:, k, :], rstd[:, k, :], mhalf[:], ALU.pow).then_inc(rstd_ready, 1)

        @block.vector
        def _(v):
            own = Chain(v, dve0)
            v.wait_ge(const_in, 6 * 16)
            v.tensor_copy(mem.ident_bf[:], mem.ident[:]).then_inc(mem.casts, 1)
            v.tensor_copy(mem.mask_bf[:], maskf[:, 0]).then_inc(mem.casts, 1)
            v.tensor_copy(mem.maskT_bf[:], maskf[:, 1]).then_inc(mem.casts, 1)
            v.memset(mem.acc[:], 0.0).then_inc(mem.casts, 1)
            for k, src, dst, ready in ((0, mem.x, xn, xn_ready), (1, xn, xg, xg_ready)):
                for t in range(NT):
                    if k == 0 and t % TPC == 0:
                        v.wait_ge(x_in[t // TPC], 16)
                    ins = v.bn_stats(st[:, k, t, :], src[:, t, :])
                    ins.then_inc(dve0, 1)
                    own.t.n += 1
                v.wait_ge(dve0, own.t.n)
                for t in range(NT):
                    v.bn_aggr(mv[:, k, t, :], st[:, k, t, :]).then_inc(stat_ready, 1)
                v.wait_ge(rstd_ready, k + 1)
                for t in range(NT):
                    v.tensor_scalar(dst[:, t, :], src[:, t, :], mv[:, k, t, 0:1], rstd[:, k, t:t + 1],
                                    ALU.subtract, ALU.mult).then_inc(ready, 1)
                v.wait_ge(ready, NT)
            for i in range(NC):
                cs = slice(CH * i, CH * (i + 1))
                v.wait_ge(k_done, i + 1)
                v.tensor_tensor(ra[:], KP[i % 2][:], mem.cos[:, cs], ALU.mult).then_inc(dve0, 1)
                v.tensor_tensor(rb[0:64], KP[i % 2][64:P], mem.sin[64:P, cs], ALU.mult).then_inc(dve0, 1)
                own.t.n += 2
                own(v.tensor_tensor(rb[64:P], KP[i % 2][0:64], mem.sin[0:64, cs], ALU.mult))
                own(v.tensor_tensor(ra[:], ra[:], rb[:], ALU.add))
                v.tensor_scalar(mem.kT[:, cs], ra[:], float(DH) ** -0.5, None, ALU.mult).then_inc(k_free, 1)
                v.wait_ge(k_free, i + 1)

        @block.tensor
        def _(pe):
            pe.wait_ge(const_in, 6 * 16)
            n = 0
            for k, src, ready in ((0, xn, xn_ready), (1, xg, xg_ready)):
                for t in range(NT):
                    pe.wait_ge(ready, t + 1)
                    if n % 2 == 0 and n >= 8:
                        pe.wait_ge(t_out, n // 2 - 3)
                    for j in range(KT):
                        cols = src[:, t, j::2] if k == 0 else src[:, t, P * j:P * (j + 1)]
                        ins = pe.transpose(TP[n // 2 % 4][:, 2 * (n % 2) + j, :], cols, mem.ident[:])
                    if n % 2:
                        ins.then_inc(turned, 1)
                    n += 1
            pe.wait_ge(wkv_in, 16)
            pe.wait_ge(t_out, NT)
            for i in range(NC):
                if i >= 2:
                    pe.wait_ge(k_free, i - 1)
                for j in range(KT):
                    ins = pe.matmul(KP[i % 2][:], wkv[:, j, 0:DH], mem.gxT[:, j, CH * i:CH * (i + 1)],
                                    start=(j == 0), stop=(j == KT - 1))
                ins.then_inc(k_done, 1)
            for i in range(NC):
                if i >= 2:
                    pe.wait_ge(v_out, i - 1)
                for q in range(4):
                    t = 4 * i + q
                    for j in range(KT):
                        ins = pe.matmul(VP[i % 2][:, P * q:P * (q + 1)], mem.gxT[:, j, P * t:P * (t + 1)],
                                        wkv[:, j, DH:2 * DH], start=(j == 0), stop=(j == KT - 1))
                ins.then_inc(v_done, 1)

        @block.scalar
        def _(act):
            act.wait_ge(const_in, 6 * 16)
            for n in range(2 * NT // 2):
                k, t = n // (NT // 2), 2 * n % NT
                act.wait_ge(turned, n + 1)
                tp = TP[n % 4][:].rearrange("p (a k) c -> p k a c", a=2)
                if k == 0:
                    dst = mem.xT[:, :, P * t:P * (t + 2)].rearrange("p k (a c) -> p k a c", a=2)
                    for j in range(KT):
                        ins = act.copy(dst[:, j], tp[:, j])
                else:
                    dst = mem.gxT[:, :, P * t:P * (t + 2)].rearrange("p k (a c) -> p k a c", a=2)
                    for j in range(KT):
                        ins = act.activation(dst[:, j], tp[:, j], ACT.Copy, scale=gam[:, j:j + 1])
                ins.then_inc(t_out, 1)
            for i in range(NC):
                act.wait_ge(v_done, i + 1)
                act.copy(mem.v[:, 4 * i:4 * i + 4, :], VP[i % 2][:].rearrange("p (a c) -> p a c", a=4)).then_inc(v_out, 1)


def attention0_phase(nc, c, io, mem):
    with ExitStack() as ctx:
        sb = lambda n, s, d=F32: ctx.enter_context(nc.sbuf_tensor(n, s, d))
        ps = lambda n, s, d=F32: ctx.enter_context(nc.psum_tensor(n, s, d))
        sem = lambda n: ctx.enter_context(nc.semaphore("a0_" + n))
        qT = sb("qT", [P, N])
        wq = sb("wq", [P, KT, DH])
        wo = sb("wo", [P, D])
        probs = sb("probs", [P, 2, N])
        PT = sb("PT", [P, 4, CH])
        oT = sb("oT", [P, 2, P])
        negmax = sb("negmax", [P, 2])
        rowsum = sb("rowsum", [P, 4])
        rinv = sb("rinv", [P, 2])
        ra = sb("rope_a", [P, CH])
        rb = sb("rope_b", [P, CH])
        raw = sb("raw", [P, 3, P], I32)
        scl = sb("scl", [P, 3, P])
        mag = sb("mag", [P, 3, P], I32)
        sgn = sb("sgn", [P, 3, P], I32)
        val = sb("val", [P, 3, P])
        val2 = sb("val2", [P, 3, P])
        sgf = sb("sgf", [P, 3, P])
        S = ps("S", [P, N])
        T = [ps(f"T{i}", [P, CH]) for i in range(2)]
        O = ps("O", [P, CH])
        Y = ps("Y", [P, CH])
        names = ("wq_in wq_free wo_in wo_free dq_in dq_free proj_done q_ready scores_done negmax_ready "
                 "probs_done turned_dve turned_act pt_dve pt_act o_done oT_ready y_done y_free dve")
        s = {n: sem(n) for n in names.split()}
        block = ctx.enter_context(nc.Block())
        tiles = list(range(NT - 1, -1, -1))

        @block.sync
        def _(sp):
            wq_free, wo_free, dq_free = Tally(s["wq_free"]), Tally(s["wo_free"]), Tally(s["dq_free"])
            sp.dma_start(wq[:], io["Wq"][0].rearrange("(k p) n -> p k n", p=P)).then_inc(s["wq_in"], 16)
            with sp.Fori(0, HEADS) as h:
                wo_free.need(sp)
                sp.dma_start(wo[:], io["Wo"][bass.ds(h * DH, DH), :]).then_inc(s["wo_in"], 16)
                dq_free.need(sp)
                sp.dma_start(raw[:], io["packed"][bass.ds(h, 1)].rearrange("a p m n -> p (a m) n")).then_inc(s["dq_in"], 16)
                for a in range(8):
                    src = io["scales"][bass.ds(h, 1), a:a + 1].rearrange("b a m n -> (b a) m n").broadcast_to([16, 3, P])
                    sp.dma_start(scl[16 * a:16 * (a + 1)], src).then_inc(s["dq_in"], 16)
                wq_free.need(sp)
                sp.dma_start(wq[:], io["Wq"][bass.ds(h + 1, 1)].rearrange("a (k p) n -> p (a k) n", p=P)).then_inc(s["wq_in"], 16)
                for x in (wq_free, wo_free, dq_free):
                    x.give_back(sp)

        @block.tensor
        def _(pe):
            wq_in, wo_in, q_ready = Tally(s["wq_in"]), Tally(s["wo_in"]), Tally(s["q_ready"])
            probs_done, pt = Tally(s["probs_done"]), {"dve": Tally(s["pt_dve"]), "act": Tally(s["pt_act"])}
            oT_ready, y_free = Tally(s["oT_ready"]), Tally(s["y_free"])

            def project(i, bank):
                for j in range(KT):
                    ins = pe.matmul(bank, wq[:, j, :], mem.gxT[:, j, CH * i:CH * (i + 1)],
                                    start=(j == 0), stop=(j == KT - 1))
                ins.then_inc(s["proj_done"], 1)
                return ins

            def scores(t):
                nk = P * (t + 1)
                for k0 in range(0, nk, CH):
                    last = k0 + CH >= nk
                    pe.matmul(S[:, k0:min(nk, k0 + CH)], qT[:, P * t:P * (t + 1)], mem.kT[:, k0:min(nk, k0 + CH)],
                              start=True, stop=not last)
                pe.matmul(S[:, nk - P:nk], mem.ident_bf[:], mem.mask_bf[:], start=False, stop=True).then_inc(s["scores_done"], 1)

            wq_in.need(pe, 16)
            project(NC - 1, S[:, 3 * CH:4 * CH])
            wq_in.give_back(pe)
            with pe.Fori(0, HEADS) as h:
                g_at = 0

                def out_proj(i):
                    oT_ready.need(pe)
                    if i == 0:
                        wo_in.need(pe, 16)
                    y_free.need(pe)
                    ins = pe.matmul(Y[:, 0:D], oT[:, i % 2, :], wo[:], start=True, stop=True)
                    ins.then_inc(s["y_done"], 1)

                q_ready.need(pe)
                scores(tiles[0])
                project(2, T[0][:])
                project(1, T[1][:])
                project(0, O[:])
                for i, t in enumerate(tiles):
                    probs_done.need(pe)
                    if i + 1 < NT:
                        scores(tiles[i + 1])
                    if tiles[min(i + 1, NT - 1)] == 4 * (NC - 1) - 1 and i + 1 < NT:
                        wq_in.need(pe, 16)
                        project(NC - 1, S[:, 3 * CH:4 * CH])
                    groups = groups_of(t)
                    na = act_copies(len(groups))

                    def weigh(g):
                        b0, w = groups[g]
                        pt["act" if g < na else "dve"].need(pe)
                        if i == 0 and g == 0:
                            q_ready.need(pe)
                        for b in range(b0, b0 + w):
                            ins = pe.matmul(O[:, 0:P], mem.v[:, b, :],
                                            PT[:, (g_at + g) % 4, P * (b - b0):P * (b - b0 + 1)],
                                            start=(b == 0), stop=(b == t))
                        if g == len(groups) - 1:
                            ins.then_inc(s["o_done"], 1)

                    for g, (b0, w) in enumerate(groups):
                        if i == 0 and g < 2:
                            q_ready.need(pe)
                        for b in range(b0, b0 + w):
                            ins = pe.transpose(T[(g_at + g) % 2][:, P * (b - b0):P * (b - b0 + 1)],
                                               probs[:, i % 2, P * b:P * (b + 1)], mem.ident[:])
                        ins.then_inc(s["turned_act"] if g < na else s["turned_dve"], 1)
                        if g == 0 and i > 0:
                            out_proj(i - 1)
                        if g > 0:
                            weigh(g - 1)
                    weigh(len(groups) - 1)
                    g_at += len(groups)
                out_proj(NT - 1)
                for x in (wq_in, wo_in, q_ready, probs_done, pt["dve"], pt["act"], oT_ready, y_free):
                    x.give_back(pe)

        @block.vector
        def _(v):
            own = Chain(v, s["dve"])
            t_ = {n: Tally(s[n]) for n in "dq_in proj_done scores_done turned_dve y_done".split()}
            v.sem_inc(s["y_free"], 1)
            v.sem_inc(s["wo_free"], 1)
            v.sem_inc(s["dq_free"], 1)

            def rotate(i, bank):
                cs = slice(CH * i, CH * (i + 1))
                t_["proj_done"].need(v)
                v.tensor_tensor(ra[:], bank, mem.cos[:, cs], ALU.mult).then_inc(s["dve"], 1)
                v.tensor_tensor(rb[0:64], bank[64:P], mem.sin[64:P, cs], ALU.mult).then_inc(s["dve"], 1)
                own.t.n += 2
                own(v.tensor_tensor(rb[64:P], bank[0:64], mem.sin[0:64, cs], ALU.mult))
                own(v.tensor_tensor(qT[:, cs], ra[:], rb[:], ALU.add))
                v.sem_inc(s["q_ready"], 1)

            def row_max(i):
                t_["scores_done"].need(v)
                v.tensor_reduce(negmax[:, i % 2:i % 2 + 1], S[:, 0:P * (tiles[i] + 1)], AX.X, ALU.max,
                                negate=True).then_inc(s["negmax_ready"], 1)

            def add_up(i):
                t = tiles[i]
                t_["y_done"].need(v)
                own(v.reciprocal(rinv[:, i % 2:i % 2 + 1], rowsum[:, i % 4:i % 4 + 1]))
                v.scalar_tensor_tensor(mem.acc[:, t, :], Y[:, 0:D], rinv[:, i % 2:i % 2 + 1],
                                       mem.acc[:, t, :], ALU.mult, ALU.add).then_inc(s["y_free"], 1)

            def unpack(step, h):
                k, nib = step % 8, step // 8
                if step == 0:
                    t_["dq_in"].need(v, 9 * 16)
                if k == 0:
                    own(v.tensor_scalar(mag[:], raw[:], 4 * nib, 7, ALU.logical_shift_right, ALU.bitwise_and))
                elif k == 1:
                    own(v.tensor_scalar(sgn[:], raw[:], 4 * nib, 8, ALU.logical_shift_right, ALU.bitwise_and))
                elif k == 2:
                    own(v.scalar_tensor_tensor(val[:], mag[:], 4.0, mag[:], ALU.max, ALU.add))
                elif k == 3:
                    own(v.tensor_scalar(val2[:], mag[:], 6.0, 2.0, ALU.max, ALU.mult))
                elif k == 4:
                    own(v.tensor_tensor(val[:], val[:], val2[:], ALU.add))
                elif k == 5:
                    own(v.tensor_scalar(sgf[:], sgn[:], -0.125, 0.5, ALU.mult, ALU.add))
                elif k == 6:
                    own(v.scalar_tensor_tensor(val2[:], val[:], -16.0, sgf[:], ALU.add, ALU.mult))
                else:
                    own(v.tensor_tensor(mem.W[nib][:, :, bass.ds(h * P, P)], val2[:], scl[:], ALU.mult))

            rotate(NC - 1, S[:, 3 * CH:4 * CH])
            t_["proj_done"].give_back(v)
            own.give_back()
            with v.Fori(0, HEADS) as h:
                row_max(0)
                rotate(2, T[0][:])
                rotate(1, T[1][:])
                rotate(0, O[:])
                v.sem_inc(s["wq_free"], 1)
                g_at = 0
                for i, t in enumerate(tiles):
                    if i + 1 < NT:
                        row_max(i + 1)
                    groups = groups_of(t)
                    for g in range(act_copies(len(groups)), len(groups)):
                        w = groups[g][1] * P
                        t_["turned_dve"].need(v)
                        v.tensor_copy(PT[:, (g_at + g) % 4, 0:w], T[(g_at + g) % 2][:, 0:w]).then_inc(s["pt_dve"], 1)
                    g_at += len(groups)
                    if tiles[min(i + 1, NT - 1)] == 4 * (NC - 1) - 1 and i + 1 < NT:
                        rotate(NC - 1, S[:, 3 * CH:4 * CH])
                    if i > 0:
                        add_up(i - 1)
                    unpack(i, h)
                add_up(NT - 1)
                v.sem_inc(s["wo_free"], 1)
                v.sem_inc(s["dq_free"], 1)
                for x in t_.values():
                    x.give_back(v)
                own.give_back()

        @block.scalar
        def _(act):
            t_ = {n: Tally(s[n]) for n in "negmax_ready turned_act o_done".split()}

            def exponent(i):
                nk = P * (tiles[i] + 1)
                t_["negmax_ready"].need(act)
                act.activation(probs[:, i % 2, 0:nk], S[:, 0:nk], ACT.Exp, bias=negmax[:, i % 2:i % 2 + 1],
                               accum_out=rowsum[:, i % 4:i % 4 + 1]).then_inc(s["probs_done"], 1)

            with act.Fori(0, HEADS) as h:
                exponent(0)
                g_at = 0
                for i, t in enumerate(tiles):
                    groups = groups_of(t)
                    for g in range(act_copies(len(groups))):
                        w = groups[g][1] * P
                        t_["turned_act"].need(act)
                        act.copy(PT[:, (g_at + g) % 4, 0:w], T[(g_at + g) % 2][:, 0:w]).then_inc(s["pt_act"], 1)
                    g_at += len(groups)
                    if i + 1 < NT:
                        exponent(i + 1)
                    t_["o_done"].need(act)
                    act.copy(oT[:, i % 2, :], O[:, 0:P]).then_inc(s["oT_ready"], 1)
                for x in t_.values():
                    x.give_back(act)


def mlp0_phase(nc, c, io, mem):
    with ExitStack() as ctx:
        sb = lambda n, s, d=F32: ctx.enter_context(nc.sbuf_tensor(n, s, d))
        ps = lambda n, s, d=F32: ctx.enter_context(nc.psum_tensor(n, s, d))
        sem = lambda n: ctx.enter_context(nc.semaphore("m0_" + n))
        sq = sb("sq", [P, 2, CH])
        th = sb("th", [P, 2, CH])
        hid = sb("hid", [P, 2, CH])
        thf = sb("thf", [P, TPC, D])
        G = [ps(f"G{i}", [P, CH]) for i in range(2)]
        U = [ps(f"U{i}", [P, CH]) for i in range(2)]
        F = ps("F", [P, TPC, D])
        s = {n: sem(n) for n in "gate_act gate_dve squared poly tanhed hid_ready f_done f_free f_dve f_tanhed dve".split()}
        block = ctx.enter_context(nc.Block())

        @block.tensor
        def _(pe):
            t_ = {n: Tally(s[n]) for n in "hid_ready f_free".split()}
            with pe.Fori(0, NC) as c4:
                def down(b):
                    jt, nib = b // 2, b % 2
                    if b == 0:
                        t_["f_free"].need(pe)
                    t_["hid_ready"].need(pe)
                    for q in range(TPC):
                        ins = pe.matmul(F[:, q, :], hid[:, b % 2, P * q:P * (q + 1)],
                                        mem.W[nib][:, 2, 2 * P * jt:2 * P * (jt + 1)],
                                        start=(b == 0 and q % 2 == 0), stop=(b == NBLK - 1), skip_group_check=True)
                    if b == NBLK - 1:
                        ins.then_inc(s["f_done"], 1)

                for b in range(NBLK):
                    for w, bank in ((0, G[b % 2]), (1, U[b % 2])):
                        for k in range(KT):
                            ins = pe.matmul(bank[:], mem.W[k][:, w, P * b:P * (b + 1)],
                                            mem.xT[:, k, bass.ds(c4 * CH, CH)], start=(k == 0), stop=(k == KT - 1))
                        ins.then_inc(s["gate_act"] if w == 0 else s["gate_dve"], 1)
                    if b > 0:
                        down(b - 1)
                down(NBLK - 1)
                for x in t_.values():
                    x.give_back(pe)

        @block.scalar
        def _(act):
            t_ = {n: Tally(s[n]) for n in "gate_act poly f_done".split()}
            with act.Fori(0, NC) as c4:
                def square(b):
                    t_["gate_act"].need(act)
                    act.activation(sq[:, b % 2, :], G[b % 2][:], ACT.Square).then_inc(s["squared"], 1)

                square(0)
                for b in range(NBLK):
                    t_["poly"].need(act)
                    act.activation(th[:, b % 2, :], sq[:, b % 2, :], ACT.Tanh, scale=0.7978845608028654).then_inc(s["tanhed"], 1)
                    if b + 1 < NBLK:
                        square(b + 1)
                t_["f_done"].need(act)
                act.activation(thf[:], F[:], ACT.Tanh, scale=0.5).then_inc(s["f_tanhed"], 1)
                for x in t_.values():
                    x.give_back(act)

        @block.vector
        def _(v):
            own = Chain(v, s["dve"])
            t_ = {n: Tally(s[n]) for n in "gate_dve squared tanhed f_tanhed".split()}
            v.sem_inc(s["f_free"], 1)
            with v.Fori(0, NC) as c4:
                def poly(b):
                    t_["squared"].need(v)
                    own(v.tensor_scalar(sq[:, b % 2, :], sq[:, b % 2, :], 0.044715, 1.0, ALU.mult, ALU.add))
                    v.tensor_tensor(sq[:, b % 2, :], G[b % 2][:], sq[:, b % 2, :], ALU.mult).then_inc(s["poly"], 1)

                poly(0)
                for b in range(NBLK):
                    if b + 1 < NBLK:
                        poly(b + 1)
                    t_["tanhed"].need(v)
                    own(v.scalar_tensor_tensor(th[:, b % 2, :], th[:, b % 2, :], 1.0, G[b % 2][:], ALU.add, ALU.mult))
                    t_["gate_dve"].need(v)
                    v.scalar_tensor_tensor(hid[:, b % 2, :], th[:, b % 2, :], 0.5, U[b % 2][:], ALU.mult,
                                           ALU.mult).then_inc(s["hid_ready"], 1)
                t_["f_tanhed"].need(v)
                own(v.scalar_tensor_tensor(thf[:], thf[:], 1.0, F[:], ALU.add, ALU.mult))
                v.sem_inc(s["f_free"], 1)
                now = bass.ds(c4 * TPC, TPC)
                own(v.scalar_tensor_tensor(thf[:].rearrange("p a b -> p (a b)"), thf[:].rearrange("p a b -> p (a b)"), 0.5,
                                           mem.acc[:, now, :].rearrange("p a b -> p (a b)"), ALU.mult, ALU.mult))
                own(v.tensor_tensor(mem.x[:, now, :], mem.x[:, now, :], thf[:], ALU.add))
                for x in t_.values():
                    x.give_back(v)
                own.give_back()


def project1_phase(nc, io, mem, l1):
    with ExitStack() as ctx:
        sb = lambda n, s, d=F32: ctx.enter_context(nc.sbuf_tensor(n, s, d))
        ps = lambda n, s, d=F32: ctx.enter_context(nc.psum_tensor(n, s, d))
        sem = lambda n: ctx.enter_context(nc.semaphore("p1_" + n))
        w = {n: sb("w1" + n, [P, KT, D]) for n in "qkv"}
        wr = sb("w1r", [P, KT, E])
        bq, bk, bv = sb("bq", [P, KT]), sb("bk", [P, KT]), sb("bv", [P, D])
        bqs = sb("bqs", [P, KT])
        qf = sb("qf", [P, 4, CH])
        parts = sb("parts", [P, 2, KT, 3, N], BF16)
        st, mv = sb("st1", [P, NT, 6]), sb("mv1", [P, NT, 2])
        rstd, mhalf = sb("rstd1", [P, NT]), sb("mhalf1", [P, NT])
        prob, prob2 = sb("prob", [P, NT, E]), sb("prob2", [P, NT, E])
        rmax, rsum = sb("rmax", [P, NT]), sb("rsum1", [P, NT])
        top, idx, idxf = sb("top", [P, NT, TOPK]), sb("idx", [P, NT, TOPK], U32), sb("idxf", [P, NT, TOPK])
        mask, seen = sb("mask1", [P, NT, E], BF16), sb("seen", [P, NT, E], BF16)
        before, ones = sb("before", [P, P], BF16), sb("ones_bf", [P, P], BF16)
        beforef, eid = sb("beforef", [P, P]), sb("eid", [P, E])
        pos = prob
        hit, hit2 = sb("hit", [P, TOPK, E]), sb("hit2", [P, TOPK, E])
        posk, valid = sb("posk", [P, NT, TOPK]), sb("valid", [P, NT, TOPK])
        tk = sb("tk", [P, NT, TOPK])
        TP = [ps(f"TQ{i}", [P, 4, P]) for i in range(2)]
        MP = [ps(f"MQ{i}", [P, CH]) for i in range(3)]
        LP = ps("LP", [P, NT, E])
        VP = ps("VQ", [P, 2, D])
        names = ("w_in stat_ready rstd_ready xn_ready turned t_out proj_done p_out v_done v_free logits_done "
                 "bias_ready shifted exped mask_ready pos_done dve pool qk_out split split_done")
        s = {n: sem(n) for n in names.split()}
        block = ctx.enter_context(nc.Block())

        @block.sync
        def _(sp):
            for n in "qkv":
                sp.dma_start(w[n][:], io[f"W{n}1"].rearrange("(k p) n -> p k n", p=P)).then_inc(s["w_in"], 16)
            sp.dma_start(wr[:], io["router"].rearrange("(k p) n -> p k n", p=P)).then_inc(s["w_in"], 16)
            sp.dma_start(bq[:], io["bq1"]).then_inc(s["w_in"], 16)
            sp.dma_start(bk[:], io["bk1"]).then_inc(s["w_in"], 16)
            sp.dma_start(bv[:], io["bv1"].rearrange("(a n) -> a n", a=1).broadcast_to([P, D])).then_inc(s["w_in"], 16)
            sp.dma_start(beforef[:], io["before"]).then_inc(s["w_in"], 16)
            sp.dma_start(eid[:], io["expert_ids"]).then_inc(s["w_in"], 16)
            for a, dst in enumerate((mem.qd, mem.kd)):
                for m in range(KT):
                    sp.wait_ge(s["split_done"], NC * (KT * a + m + 1))
                    for j in range(3):
                        sp.dma_start(dst[j, P * m:P * (m + 1), :], parts[:, a, m, j, :]).then_inc(s["qk_out"], 16)
            sp.wait_ge(s["qk_out"], 12 * 16)

        @block.gpsimd
        def _(pool):
            pool.memset(mhalf[:], -0.5).then_inc(s["pool"], 1)
            pool.memset(ones[:], 1.0).then_inc(s["pool"], 1)
            pool.wait_ge(s["stat_ready"], NT)
            pool.tensor_scalar(rstd[:], mv[:, :, 1], EPS, None, ALU.add).then_inc(s["pool"], 1)
            pool.wait_ge(s["pool"], 3)
            pool.tensor_tensor(rstd[:], rstd[:], mhalf[:], ALU.pow).then_inc(s["rstd_ready"], 1)
            pool.memset(mem.v1[:, :, :, HD:32], 0.0).then_inc(s["pool"], 1)
            pool.wait_ge(s["pool"], 4)
            pool.memset(mem.v1[:, :, :, HD:KA], 1.0).then_inc(s["pool"], 1)
            n = 0
            own = Chain(pool, s["split"])
            for a in range(2):
                for m in range(KT):
                    for i in range(NC):
                        pool.wait_ge(s["p_out"], n + 1)
                        f = qf[:, n % 4, :]
                        hi, mid, lo = (parts[:, a, m, j, CH * i:CH * (i + 1)] for j in range(3))
                        own(pool.tensor_tensor(f, f, hi, ALU.subtract))
                        own(pool.tensor_copy(mid, f))
                        pool.tensor_tensor(lo, f, mid, ALU.subtract).then_inc(s["split_done"], 1)
                        n += 1

        @block.tensor
        def _(pe):
            for t in range(NT):
                pe.wait_ge(s["xn_ready"], t + 1)
                if t % 2 == 0 and t >= 4:
                    pe.wait_ge(s["t_out"], t // 2 - 1)
                for j in range(KT):
                    ins = pe.transpose(TP[t // 2 % 2][:, 2 * (t % 2) + j, :], l1.xn[:, t, P * j:P * (j + 1)], mem.ident[:])
                if t % 2:
                    ins.then_inc(s["turned"], 1)
            pe.wait_ge(s["w_in"], 9 * 16)
            pe.wait_ge(s["t_out"], NT // 2)
            for t in range(NT):
                for j in range(KT):
                    ins = pe.matmul(LP[:, t, :], mem.xT[:, j, P * t:P * (t + 1)], wr[:, j, :], start=(j == 0), stop=(j == KT - 1))
            ins.then_inc(s["logits_done"], 1)
            n = 0
            for a, name in enumerate("qk"):
                for m in range(KT):
                    for i in range(NC):
                        if n >= 3:
                            pe.wait_ge(s["p_out"], n - 2)
                        for j in range(KT):
                            ins = pe.matmul(MP[n % 3][:], w[name][:, j, P * m:P * (m + 1)], mem.xT[:, j, CH * i:CH * (i + 1)],
                                            start=(j == 0), stop=(j == KT - 1))
                        ins.then_inc(s["proj_done"], 1)
                        n += 1
            for t in range(NT):
                if t >= 1:
                    pe.wait_ge(s["v_free"], t)
                for j in range(KT):
                    ins = pe.matmul(VP[:, 0, :], mem.xT[:, j, P * t:P * (t + 1)], w["v"][:, j, :], start=(j == 0), stop=(j == KT - 1))
                ins.then_inc(s["v_done"], 1)
            pe.wait_ge(s["mask_ready"], 1)
            for t in range(NT):
                ins = pe.matmul(LP[:, t, :], before[:], mask[:, t, :], start=True, stop=(t == 0))
                if t:
                    ins = pe.matmul(LP[:, t, :], ones[:], seen[:, t, :], start=False, stop=True)
            ins.then_inc(s["pos_done"], 1)

        @block.scalar
        def _(act):
            for n in range(NT // 2):
                act.wait_ge(s["turned"], n + 1)
                tp = TP[n % 2][:].rearrange("p (a k) c -> p k a c", a=2)
                dst = mem.xT[:, :, 2 * P * n:2 * P * (n + 1)].rearrange("p k (a c) -> p k a c", a=2)
                for j in range(KT):
                    ins = act.copy(dst[:, j], tp[:, j])
                ins.then_inc(s["t_out"], 1)
            act.wait_ge(s["w_in"], 9 * 16)
            act.mul(bqs[:], bq[:], float(HD) ** -0.5).then_inc(s["bias_ready"], 1)
            act.wait_ge(s["bias_ready"], 1)
            n = 0
            for a in range(2):
                for m in range(KT):
                    for i in range(NC):
                        act.wait_ge(s["proj_done"], n + 1)
                        if n >= 4:
                            act.wait_ge(s["split_done"], n - 3)
                        bias, scale = ((bqs, float(HD) ** -0.5), (bk, 1.0))[a]
                        act.activation(qf[:, n % 4, :], MP[n % 3][:], ACT.Identity, bias=bias[:, m:m + 1], scale=scale)
                        act.activation(parts[:, a, m, 0, CH * i:CH * (i + 1)], MP[n % 3][:], ACT.Identity,
                                       bias=bias[:, m:m + 1], scale=scale).then_inc(s["p_out"], 1)
                        n += 1
                        if n == 6:
                            act.wait_ge(s["shifted"], 1)
                            act.activation(prob[:], prob[:], ACT.Exp).then_inc(s["exped"], 1)

        @block.vector
        def _(v):
            own = Chain(v, s["dve"])
            for t in range(NT):
                v.bn_stats(st[:, t, :], mem.x[:, t, :]).then_inc(s["dve"], 1)
                own.t.n += 1
            v.wait_ge(s["dve"], own.t.n)
            for t in range(NT):
                v.bn_aggr(mv[:, t, :], st[:, t, :]).then_inc(s["stat_ready"], 1)
            v.wait_ge(s["rstd_ready"], 1)
            for t in range(NT):
                v.tensor_scalar(l1.xn[:, t, :], mem.x[:, t, :], mv[:, t, 0:1], rstd[:, t:t + 1],
                                ALU.subtract, ALU.mult).then_inc(s["xn_ready"], 1)
            v.wait_ge(s["w_in"], 9 * 16)
            own(v.tensor_copy(before[:], beforef[:]))
            v.wait_ge(s["logits_done"], 1)
            own(v.tensor_reduce(rmax[:], LP[:], AX.X, ALU.max))
            v.tensor_tensor(prob[:], LP[:], rmax[:].rearrange("p (t a) -> p t a", a=1).broadcast_to([P, NT, E]),
                            ALU.subtract).then_inc(s["shifted"], 1)
            v.wait_ge(s["exped"], 1)
            own(v.tensor_reduce(rsum[:], prob[:], AX.X, ALU.add))
            own(v.reciprocal(rsum[:], rsum[:]))
            own(v.tensor_tensor(prob[:], prob[:], rsum[:].rearrange("p (t a) -> p t a", a=1).broadcast_to([P, NT, E]), ALU.mult))
            for t in range(NT):
                v.max(top[:, t, :], prob[:, t, :]).then_inc(s["dve"], 1)
                own.t.n += 1
            v.wait_ge(s["dve"], own.t.n)
            for t in range(NT):
                v.max_index(idx[:, t, :], top[:, t, :], prob[:, t, :]).then_inc(s["dve"], 1)
                v.match_replace(prob2[:, t, :], top[:, t, :], prob[:, t, :], -1.0).then_inc(s["dve"], 1)
                own.t.n += 2
            v.wait_ge(s["dve"], own.t.n)
            own(v.tensor_scalar(mask[:], prob2[:], 0.0, None, ALU.is_lt))
            own(v.tensor_copy(seen[:, 1, :], mask[:, 0, :]))
            for t in range(2, NT):
                own(v.tensor_tensor(seen[:, t, :], seen[:, t - 1, :], mask[:, t - 1, :], ALU.add))
            v.sem_inc(s["mask_ready"], 1)
            own(v.tensor_reduce(rsum[:], top[:], AX.X, ALU.add))
            own(v.reciprocal(rsum[:], rsum[:]))
            own(v.tensor_tensor(top[:], top[:], rsum[:].rearrange("p (t a) -> p t a", a=1).broadcast_to([P, NT, TOPK]), ALU.mult))
            own(v.tensor_copy(idxf[:], idx[:]))
            for t in range(NT):
                v.wait_ge(s["v_done"], t + 1)
                v.tensor_tensor(mem.v1[:, t, :, 0:HD], VP[:, 0, :].rearrange("p (h d) -> p h d", d=HD),
                                bv[:].rearrange("p (h d) -> p h d", d=HD), ALU.add).then_inc(s["v_free"], 1)
            v.wait_ge(s["pos_done"], 1)
            own(v.tensor_copy(pos[:], LP[:]))
            for t in range(NT):
                own(v.tensor_tensor(hit[:], eid[:].rearrange("p (a e) -> p a e", a=1).broadcast_to([P, TOPK, E]),
                                    idxf[:, t, :].rearrange("p (k a) -> p k a", a=1).broadcast_to([P, TOPK, E]), ALU.is_equal))
                own(v.tensor_tensor(hit2[:], hit[:], pos[:, t, :].rearrange("p (a e) -> p a e", a=1).broadcast_to([P, TOPK, E]), ALU.mult))
                own(v.tensor_reduce(posk[:, t, :], hit2[:], AX.X, ALU.add))
            own(v.tensor_scalar(valid[:], posk[:], float(CAP), None, ALU.is_lt))
            own(v.tensor_tensor(l1.weight[:], top[:], valid[:], ALU.mult))
            own(v.tensor_scalar(posk[:], posk[:], float(CAP - 1), None, ALU.min))
            own(v.scalar_tensor_tensor(posk[:], idxf[:], float(CAP), posk[:], ALU.mult, ALU.add))
            own(v.tensor_copy(l1.take[:], posk[:]))
            own(v.tensor_scalar(tk[:], valid[:], -float(E * CAP), float(E * CAP), ALU.mult, ALU.add))
            own(v.tensor_tensor(tk[:], posk[:], tk[:], ALU.add))
            own(v.tensor_copy(l1.send[:], tk[:]))


def attention1_phase(nc, io, mem, l1, part, pool_work):
    with ExitStack() as ctx:
        sb = lambda n, s, d=F32: ctx.enter_context(nc.sbuf_tensor(f"{n}_{part}", s, d))
        ps = lambda n, s, d=F32: ctx.enter_context(nc.psum_tensor(f"{n}_{part}", s, d))
        sem = lambda n: ctx.enter_context(nc.semaphore(f"a1{part}_" + n))
        PT = sb("PT1", [P, 2, 4, CH])
        oT = sb("oT1", [P, CH])
        pmax = sb("pmax", [P, 4, NT, NC])
        negm = sb("negm", [P, 4, NT])
        rest = sb("restm", [P, 4, NT])
        mp = sb("mp", [P, 4, 3, NT], BF16)
        msb = sb("msb", [96, 2, P], BF16)
        rinv = sb("rinv1", [P, 4, 4])
        ST = [ps(f"ST{i}", [P, 2, CH]) for i in range(2)]
        MX = [ps(f"MX{i}", [P, CH]) for i in range(2)]
        O = ps("O1", [P, CH])
        TR = ps("TR", [P, CH])
        TRb = TR[:].bitcast(BF16)[0:96, 0:2 * P].rearrange("p (a q) -> p a q", a=2)
        names = ("in00 in01 in02 in03 in10 in11 in12 in13 m_out m_in st_done exp_done mx_done mx_free o_done oT_ready tr_done tr_free "
                 "mp_ready mt_done msb_ready main_done dve")
        s = {n: sem(n) for n in names.split()}
        block = ctx.enter_context(nc.Block())
        UNITS = [(c, kb) for c in range(NC) for kb in range(4 * c + 4)]
        MAXES = [(hd, t, r) for hd in range(4) for t in range(NT) for r in range(t // 4 + 1)]
        START, PER = 8, 6
        stages = [(None, 0), (0, 1), (1, 2)] if part == 0 else [(2, 3), (3, None)]

        def maxes_at(u):
            return MAXES[max(0, u - START) * PER:(u - START + 1) * PER] if u >= START else []

        LAST_MAX = START + -(-len(MAXES) // PER) - 1

        @block.gpsimd
        def _(pool):
            pool_work(pool)

        @block.sync
        def _(sp):
            t_ = {n: Tally(s[n]) for n in "msb_ready main_done".split()}
            n_out = [0]

            def load(g):
                q, k = l1.qs[g % 2], l1.ks[g % 2]
                for hd in range(4):
                    h = 4 * g + hd
                    arrived = s[f"in{g % 2}{hd}"]
                    for n, (a, b) in enumerate(PARTS):
                        rows = slice(n * HD, (n + 1) * HD)
                        sp.dma_start(q[rows, hd, :], mem.qd[a, h * HD:(h + 1) * HD, :]).then_inc(arrived, 16)
                        sp.dma_start(k[rows, hd, :], mem.kd[b, h * HD:(h + 1) * HD, :]).then_inc(arrived, 16)
                    sp.dma_start(q[KS - 6:KS, hd, :], io["alibi_q"][h].bitcast(BF16)).then_inc(arrived, 16)
                    sp.dma_start(k[KS - 6:KM, hd, :], io["alibi_k"].bitcast(BF16)).then_inc(arrived, 16)

            def send_max(g):
                t_["msb_ready"].need(sp)
                for a in range(2):
                    sp.dma_start(mem.md[g, 2 * a:2 * a + 2].rearrange("h k t q -> (h k t) q"), msb[:, a, :]).then_inc(s["m_out"], 16)
                n_out[0] += 2 * 16
                sp.wait_ge(s["m_out"], n_out[0])
                sp.dma_start(l1.qs[g % 2][KS:KM], mem.md[g].rearrange("h k t q -> k h (t q)")).then_inc(s["m_in"], 16)

            if part == 0:
                load(0)
                load(1)
                send_max(0)
                send_max(1)
                t_["main_done"].need(sp)
                load(2)
                send_max(2)
            else:
                load(3)
                send_max(3)
            sp.wait_ge(s["m_in"], 16 * (3 if part == 0 else 1))

        @block.tensor
        def _(pe):
            t_ = {n: Tally(s[n]) for n in "in00 in01 in02 in03 in10 in11 in12 in13 m_in exp_done mx_free oT_ready tr_free mp_ready".split()}
            n_max = [0]

            def first_pass(g, hd, t, r):
                if (t, r) == (0, 0):
                    t_[f"in{g % 2}{hd}"].need(pe, 14 * 16)
                w = min(CH, P * (t + 1) - CH * r)
                bank = MX[n_max[0] % 2]
                n_max[0] += 1
                t_["mx_free"].need(pe)
                last = r == t // 4
                ins = pe.matmul(bank[:, 0:w], l1.qs[g % 2][0:KS, hd, P * t:P * (t + 1)],
                                l1.ks[g % 2][0:KS, hd, CH * r:CH * r + w], start=True, stop=not last)
                if last:
                    ins = pe.matmul(bank[:, w - P:w], mem.ident_bf[:], mem.mask_bf[:], start=False, stop=True)
                ins.then_inc(s["mx_done"], 1)

            def turn_max():
                t_["mp_ready"].need(pe)
                t_["tr_free"].need(pe)
                for a in range(2):
                    ins = pe.transpose(TRb[:, a, :], mp[:, 2 * a:2 * a + 2].rearrange("p h k t -> p (h k t)"), mem.ident_bf[:])
                ins.then_inc(s["mt_done"], 1)

            def second_pass(g, u):
                c, kb = UNITS[u]
                q0 = P * max(0, kb - 4 * c)
                for pr in range(2):
                    if u > 0:
                        t_["exp_done"].need(pe)
                    for i in range(2):
                        hd = 2 * pr + i
                        ins = pe.matmul(ST[pr][:, i, q0:CH], l1.ks[g % 2][0:KM, hd, P * kb:P * (kb + 1)],
                                        l1.qs[g % 2][0:KM, hd, CH * c + q0:CH * (c + 1)], start=True, stop=(kb < 4 * c))
                        if kb >= 4 * c:
                            ins = pe.matmul(ST[pr][:, i, q0:q0 + P], mem.ident_bf[:], mem.maskT_bf[:], start=False, stop=True)
                    ins.then_inc(s["st_done"], 1)

            def weigh(g, u):
                c, kb = UNITS[u]
                q0 = P * max(0, kb - 4 * c)
                if kb == 0 and not (u == 0):
                    t_["oT_ready"].need(pe)
                    turn_out()
                for hd in range(4):
                    ins = pe.matmul(O[32 * hd:32 * hd + 32, q0:CH], mem.v1[:, kb, 4 * g + hd, :], PT[:, u % 2, hd, q0:CH],
                                    start=(kb == 0), stop=(kb == 4 * c + 3), tile_position=(0, 32 * hd))
                if kb == 4 * c + 3:
                    ins.then_inc(s["o_done"], 1)

            def turn_out():
                t_["tr_free"].need(pe)
                for q in range(4):
                    ins = pe.transpose(TR[:, P * q:P * (q + 1)], oT[:, P * q:P * (q + 1)], mem.ident[:])
                ins.then_inc(s["tr_done"], 1)

            for g, gm in stages:
                if g is None:
                    for m in MAXES:
                        first_pass(gm, *m)
                    turn_max()
                    continue
                if (part, g) != (1, 2):
                    t_["m_in"].need(pe, 16)
                for u in range(len(UNITS)):
                    second_pass(g, u)
                    if gm is not None:
                        for m in maxes_at(u):
                            first_pass(gm, *m)
                        if u == LAST_MAX + 1:
                            turn_max()
                    if u > 0:
                        weigh(g, u - 1)
                t_["exp_done"].need(pe, 2)
                weigh(g, len(UNITS) - 1)
                t_["oT_ready"].need(pe)
                turn_out()

        @block.vector
        def _(v):
            own = Chain(v, s["dve"])
            t_ = {n: Tally(s[n]) for n in "mx_done tr_done mt_done".split()}
            v.sem_inc(s["mx_free"], 2)
            v.sem_inc(s["tr_free"], 1)
            n_max = [0]

            def row_max(hd, t, r):
                w = min(CH, P * (t + 1) - CH * r)
                bank = MX[n_max[0] % 2]
                n_max[0] += 1
                t_["mx_done"].need(v)
                ins = v.tensor_reduce(pmax[:, hd, t, r:r + 1], bank[:, 0:w], AX.X, ALU.max)
                if (hd, t, r) == MAXES[-1]:
                    own(ins)
                    v.sem_inc(s["mx_free"], 1)
                else:
                    ins.then_inc(s["mx_free"], 1)

            def split_max():
                for c in range(NC):
                    ins = v.tensor_reduce(negm[:, :, 4 * c:4 * c + 4], pmax[:, :, 4 * c:4 * c + 4, 0:c + 1], AX.X, ALU.max, negate=True)
                    ins.then_inc(s["dve"], 1)
                    own.t.n += 1
                v.wait_ge(s["dve"], own.t.n)
                own(v.tensor_copy(mp[:, :, 0, :], negm[:]))
                own(v.tensor_tensor(rest[:], negm[:], mp[:, :, 0, :], ALU.subtract))
                own(v.tensor_copy(mp[:, :, 1, :], rest[:]))
                v.tensor_tensor(mp[:, :, 2, :], rest[:], mp[:, :, 1, :], ALU.subtract).then_inc(s["mp_ready"], 1)

            def pass_max():
                t_["mt_done"].need(v)
                own(v.tensor_copy(msb[:], TRb))
                v.sem_inc(s["tr_free"], 1)
                v.sem_inc(s["msb_ready"], 1)

            def finish(g, c):
                t_["tr_done"].need(v)
                rows = TR[:].rearrange("p (q h d) -> p q h d", q=4, h=4)
                own(v.reciprocal(rinv[:], rows[:, :, :, HD]))
                v.tensor_tensor(mem.ctx[:, 4 * c:4 * c + 4, 4 * HD * g:4 * HD * (g + 1)].rearrange("p q (h d) -> p q h d", h=4),
                                rows[:, :, :, 0:HD], rinv[:].rearrange("p q (h a) -> p q h a", a=1).broadcast_to([P, 4, 4, HD]),
                                ALU.mult).then_inc(s["tr_free"], 1)

            for g, gm in stages:
                if g is None:
                    for m in MAXES:
                        row_max(*m)
                    split_max()
                    pass_max()
                    continue
                for u in range(len(UNITS)):
                    if gm is not None:
                        for m in maxes_at(u):
                            row_max(*m)
                        if u == LAST_MAX:
                            split_max()
                        if u == LAST_MAX + 1:
                            pass_max()
                    c, kb = UNITS[u]
                    if kb == 1 and c > 0:
                        finish(g, c - 1)
                finish(g, NC - 1)
                v.sem_inc(s["main_done"], 1)

        @block.scalar
        def _(act):
            t_ = {n: Tally(s[n]) for n in "st_done o_done".split()}

            def copy_out():
                t_["o_done"].need(act)
                act.copy(oT[:], O[:]).then_inc(s["oT_ready"], 1)

            for g, gm in stages:
                if g is None:
                    continue
                for u in range(len(UNITS)):
                    c, kb = UNITS[u]
                    q0 = P * max(0, kb - 4 * c)
                    for pr in range(2):
                        t_["st_done"].need(act)
                        act.activation(PT[:, u % 2, 2 * pr:2 * pr + 2, q0:CH], ST[pr][:, :, q0:CH], ACT.Exp).then_inc(s["exp_done"], 1)
                    if kb == 0 and c > 0:
                        copy_out()
                copy_out()


def experts_phase(nc, io, mem, l1):
    with ExitStack() as ctx:
        sb = lambda n, s, d=F32: ctx.enter_context(nc.sbuf_tensor(n, s, d))
        ps = lambda n, s, d=F32: ctx.enter_context(nc.psum_tensor(n, s, d))
        sem = lambda n: ctx.enter_context(nc.semaphore("e_" + n))
        room = [x[:].rearrange("p h n -> p (h n)").bitcast(F32) for x in (l1.qs[1], l1.ks[1])]
        rows = room[0][:, 0:2 * EG * D].rearrange("p (u e c) -> p u e c", u=2, e=EG)
        res = room[1][:, 0:2 * EG * D].rearrange("p (u e c) -> p u e c", u=2, e=EG)
        wd = room[1][0:I, 2 * EG * D:4 * EG * D].rearrange("p (u e c) -> p u e c", u=2, e=EG)
        wg, wu = sb("wg", [P, 2, EG, KT, I]), sb("wu", [P, 2, EG, KT, I])
        rT = sb("rT", [P, 2, EG, KT, P])
        th, hid = sb("the", [I, EG, P]), sb("hide", [I, EG, P])
        RT = ps("RT", [P, EG, KT, P])
        G, U = ps("GE", [I, EG, P]), ps("UE", [I, EG, P])
        R = ps("RE", [P, EG, D])
        names = ("in0 in1 in_free turned_act turned_dve rT_act rT_dve gate_done up_done tanhed hid_ready "
                 "res_done r_free copied stored0 stored1 dve")
        s = {n: sem(n) for n in names.split()}
        block = ctx.enter_context(nc.Block())
        ITER = E // EG // 2

        def first_expert(it, u):
            return it * 2 * EG + u * EG

        @block.sync
        def _(sp):
            in_free = Tally(s["in_free"])
            with sp.Fori(0, ITER) as it:
                for u in range(2):
                    in_free.need(sp)
                    e0 = first_expert(it, u)
                    sp.dma_start(rows[:, u], mem.xe[bass.ds(e0 * CAP, EG * CAP), :].rearrange("(e p) c -> p e c", p=P)).then_inc(s[f"in{u}"], 16)
                    for wt, src in ((wg, "gate"), (wu, "up")):
                        sp.dma_start(wt[:, u].rearrange("p e k i -> p (e k) i"),
                                     io[src][bass.ds(e0, EG)].rearrange("e (k p) i -> p (e k) i", p=P)).then_inc(s[f"in{u}"], 16)
                    sp.dma_start(wd[:, u], io["down"][bass.ds(e0, EG)].rearrange("e i d -> i e d")).then_inc(s[f"in{u}"], 16)
                in_free.give_back(sp)

        @block.tensor
        def _(pe):
            t_ = {n: Tally(s[n]) for n in "in0 in1 rT_act rT_dve hid_ready r_free".split()}

            def turn(u):
                t_[f"in{u}"].need(pe, 4 * 16)
                for e in range(EG):
                    for k in range(KT):
                        ins = pe.transpose(RT[:, e, k, :], rows[:, u, e, P * k:P * (k + 1)], mem.ident[:])
                    if e == 1:
                        ins.then_inc(s["turned_act"], 1)
                ins.then_inc(s["turned_dve"], 1)

            def gate_up(u):
                t_["rT_act"].need(pe)
                t_["rT_dve"].need(pe)
                for wt, bank, done in ((wg, G, "gate_done"), (wu, U, "up_done")):
                    for e in range(EG):
                        for k in range(KT):
                            ins = pe.matmul(bank[:, e, :], wt[:, u, e, k, :], rT[:, u, e, k, :],
                                            start=(k == 0), stop=(k == KT - 1))
                    ins.then_inc(s[done], 1)

            def down(u):
                t_["hid_ready"].need(pe)
                t_["r_free"].need(pe)
                for e in range(EG):
                    ins = pe.matmul(R[:, e, :], hid[:, e, :], wd[:, u, e, :], start=True, stop=True)
                ins.then_inc(s["res_done"], 1)

            with pe.Fori(0, ITER) as it:
                turn(0)
                gate_up(0)
                turn(1)
                down(0)
                gate_up(1)
                down(1)
                for x in t_.values():
                    x.give_back(pe)

        @block.scalar
        def _(act):
            own = Chain(act, s["copied"])
            t_ = {n: Tally(s[n]) for n in "turned_act gate_done res_done stored0 stored1".split()}
            act.sem_inc(s["r_free"], 1)
            act.sem_inc(s["in_free"], 2)
            act.sem_inc(s["stored0"], 16)
            act.sem_inc(s["stored1"], 16)
            with act.Fori(0, ITER) as it:
                def turned(u):
                    t_["turned_act"].need(act)
                    act.copy(rT[:, u, 0:2], RT[:, 0:2]).then_inc(s["rT_act"], 1)

                def tanh_half():
                    t_["gate_done"].need(act)
                    act.activation(th[:], G[:], ACT.Tanh, scale=0.5).then_inc(s["tanhed"], 1)

                def store(u):
                    t_["res_done"].need(act)
                    t_[f"stored{u}"].need(act, 16)
                    act.sem_inc(s["in_free"], 1)
                    own(act.copy(res[:, u], R[:]))
                    act.sem_inc(s["r_free"], 1)
                    act.dma_start(mem.ye[bass.ds(first_expert(it, u) * CAP, EG * CAP), :].rearrange("(e p) c -> p e c", p=P),
                                  res[:, u]).then_inc(s[f"stored{u}"], 16)

                turned(0)
                tanh_half()
                turned(1)
                store(0)
                tanh_half()
                store(1)
                for x in t_.values():
                    x.give_back(act)
                own.give_back()
            act.wait_ge(s["stored0"], 16)
            act.wait_ge(s["stored1"], 16)

        @block.vector
        def _(v):
            own = Chain(v, s["dve"])
            t_ = {n: Tally(s[n]) for n in "turned_dve up_done tanhed".split()}
            with v.Fori(0, ITER) as it:
                def turned(u):
                    t_["turned_dve"].need(v)
                    v.tensor_copy(rT[:, u, 2:4], RT[:, 2:4]).then_inc(s["rT_dve"], 1)

                def hidden():
                    t_["tanhed"].need(v)
                    own(v.scalar_tensor_tensor(th[:], th[:], 1.0, G[:], ALU.add, ALU.mult))
                    t_["up_done"].need(v)
                    v.scalar_tensor_tensor(hid[:], th[:], 0.5, U[:], ALU.mult, ALU.mult).then_inc(s["hid_ready"], 1)

                turned(0)
                turned(1)
                hidden()
                hidden()
                for x in t_.values():
                    x.give_back(v)
                own.give_back()


def output_phase(nc, io, mem, l1):
    with ExitStack() as ctx:
        sb = lambda n, s, d=F32: ctx.enter_context(nc.sbuf_tensor(n, s, d))
        ps = lambda n, s, d=F32: ctx.enter_context(nc.psum_tensor(n, s, d))
        sem = lambda n: ctx.enter_context(nc.semaphore("o_" + n))
        wo = sb("wo1", [P, KT, D])
        bo = sb("bo", [P, D])
        th = sb("tho", [P, NT, D])
        att = sb("att", [P, 2, 2, D])
        TP = [ps(f"TO{i}", [P, 4, P]) for i in range(2)]
        Y = [ps(f"YO{i}", [P, 2, D]) for i in range(2)]
        s = {n: sem(n) for n in "w_in turned t_out y_done y_free tanhed out_ready stored dve".split()}
        block = ctx.enter_context(nc.Block())
        PAIRS = NT // 2

        @block.sync
        def _(sp):
            sp.dma_start(wo[:], io["Wo1"].rearrange("(k p) n -> p k n", p=P)).then_inc(s["w_in"], 16)
            sp.dma_start(bo[:], io["bo1"].rearrange("(a n) -> a n", a=1).broadcast_to([P, D])).then_inc(s["w_in"], 16)
            ov = io["out"][0].rearrange("(t p) c -> p t c", p=P)
            for n in range(PAIRS):
                sp.wait_ge(s["out_ready"], n + 1)
                sp.dma_start(ov[:, 2 * n:2 * n + 2, :], mem.x[:, 2 * n:2 * n + 2, :]).then_inc(s["stored"], 16)
            sp.wait_ge(s["stored"], 16 * PAIRS)

        @block.tensor
        def _(pe):
            def turn(n):
                if n >= 2:
                    pe.wait_ge(s["t_out"], n - 1)
                for a in range(2):
                    for j in range(KT):
                        ins = pe.transpose(TP[n % 2][:, 2 * a + j, :], mem.ctx[:, 2 * n + a, P * j:P * (j + 1)], mem.ident[:])
                ins.then_inc(s["turned"], 1)

            turn(0)
            pe.wait_ge(s["w_in"], 2 * 16)
            for n in range(PAIRS):
                if n + 1 < PAIRS:
                    turn(n + 1)
                pe.wait_ge(s["t_out"], n + 1)
                if n >= 2:
                    pe.wait_ge(s["y_free"], n - 1)
                for a in range(2):
                    t = 2 * n + a
                    for j in range(KT):
                        ins = pe.matmul(Y[n % 2][:, a, :], mem.xT[:, j, P * t:P * (t + 1)], wo[:, j, :],
                                        start=(j == 0), stop=(j == KT - 1))
                ins.then_inc(s["y_done"], 1)

        @block.scalar
        def _(act):
            for n in range(PAIRS):
                act.activation(th[:, 2 * n:2 * n + 2, :], mem.f[:, 2 * n:2 * n + 2, :], ACT.Tanh, scale=0.5).then_inc(s["tanhed"], 1)
                act.wait_ge(s["turned"], n + 1)
                tp = TP[n % 2][:].rearrange("p (a k) c -> p k a c", a=2)
                dst = mem.xT[:, :, 2 * P * n:2 * P * (n + 1)].rearrange("p k (a c) -> p k a c", a=2)
                act.copy(dst[:, 0], tp[:, 0])
                act.copy(dst[:, 1], tp[:, 1]).then_inc(s["t_out"], 1)

        @block.vector
        def _(v):
            own = Chain(v, s["dve"])
            v.wait_ge(s["w_in"], 2 * 16)
            bias = bo[:].rearrange("p (a c) -> p a c", a=1).broadcast_to([P, 2, D])
            for n in range(PAIRS):
                now = slice(2 * n, 2 * n + 2)
                v.wait_ge(s["tanhed"], n + 1)
                own(v.scalar_tensor_tensor(th[:, now, :], th[:, now, :], 1.0, mem.f[:, now, :], ALU.add, ALU.mult))
                v.wait_ge(s["y_done"], n + 1)
                v.tensor_tensor(att[:, n % 2], Y[n % 2][:], bias, ALU.add).then_inc(s["y_free"], 1)
                v.wait_ge(s["y_free"], n + 1)
                own(v.scalar_tensor_tensor(th[:, now, :], th[:, now, :], 0.5, att[:, n % 2], ALU.mult, ALU.mult))
                v.tensor_tensor(mem.x[:, now, :], mem.x[:, now, :], th[:, now, :], ALU.add).then_inc(s["out_ready"], 1)


def layer1(nc, io, mem):
    l1 = Memory()
    with ExitStack() as ctx:
        sb = lambda n, s, d=F32: ctx.enter_context(nc.sbuf_tensor(n, s, d))
        sem = lambda n: ctx.enter_context(nc.semaphore("l1_" + n))
        l1.xn = sb("xn1", [P, NT, D])
        l1.weight = sb("weight", [P, NT, TOPK])
        l1.take, l1.send = sb("take", [P, NT, TOPK], U32), sb("send", [P, NT, TOPK], U32)
        mem.v1 = sb("v1", [P, NT, HEADS, 32])
        mem.f = l1.xn
        mem.ctx = mem.acc
        got = mem.xT[:].rearrange("p k (b c) -> p k b c", c=D)
        sent, taken, pool = sem("sent"), [sem("taken0"), sem("taken1")], sem("pool")
        project1_phase(nc, io, mem, l1)
        l1.qs = [sb(f"qs{i}", [P, 4, N], BF16) for i in range(2)]
        l1.ks = [sb(f"ks{i}", [P, 4, N], BF16) for i in range(2)]

        def send_rows(eng):
            eng.wait_ge(mem.xe_zeroed, 8 * 16)
            for t in range(NT):
                for k in range(TOPK):
                    eng.indirect_dma_start(mem.xe, bass.IndirectOffsetOnAxis(l1.send[:, t, k:k + 1], 0), l1.xn[:, t, :], None,
                                           bounds_check=E * CAP - 1, oob_is_err=False).then_inc(sent, 16)
            eng.wait_ge(sent, 16 * NT * TOPK)

        def take_rows(eng):
            own = Chain(eng, pool)

            def combine(t):
                g = got[:, t % 2]
                eng.wait_ge(taken[t % 2], 16 * TOPK * (t // 2 + 1))
                w = l1.weight[:, t, :].rearrange("p (k a) -> p k a", a=1).broadcast_to([P, TOPK, D])
                own(eng.tensor_tensor(g, g, w, ALU.mult))
                own(eng.tensor_tensor(g[:, 0:4], g[:, 0:4], g[:, 4:8], ALU.add))
                own(eng.tensor_tensor(g[:, 0:2], g[:, 0:2], g[:, 2:4], ALU.add))
                own(eng.tensor_tensor(mem.f[:, t, :], g[:, 0], g[:, 1], ALU.add))

            for t in range(NT):
                for k in range(TOPK):
                    eng.indirect_dma_start(got[:, t % 2, k, :], None, mem.ye, bass.IndirectOffsetOnAxis(l1.take[:, t, k:k + 1], 0),
                                           bounds_check=E * CAP - 1, oob_is_err=False).then_inc(taken[t % 2], 16)
                if t:
                    combine(t - 1)
            combine(NT - 1)

        attention1_phase(nc, io, mem, l1, 0, send_rows)
        experts_phase(nc, io, mem, l1)
        attention1_phase(nc, io, mem, l1, 1, take_rows)
        output_phase(nc, io, mem, l1)


class Memory:
    pass


def build(nc, io):
    c = None
    mem = Memory()
    with ExitStack() as ctx:
        sb = lambda n, s, d=F32: ctx.enter_context(nc.sbuf_tensor(n, s, d))
        sem = lambda n: ctx.enter_context(nc.semaphore(n))
        dram = lambda n, s, d=F32: nc.dram_tensor(n, s, d, kind="Internal").ap()
        mem.xe = dram("xe", [E * CAP, D])
        mem.ye = dram("ye", [E * CAP, D])
        mem.qd = dram("qd", [3, D, N], BF16)
        mem.kd = dram("kd", [3, D, N], BF16)
        mem.md = dram("md", [4, 4, 3, NT, P], BF16)
        mem.casts, mem.xe_zeroed = sem("casts"), sem("xe_zeroed")
        mem.x = sb("x", [P, NT, D])
        mem.acc = sb("acc", [P, NT, D])
        mem.xT = sb("xT", [P, KT, N])
        mem.ident = sb("ident", [P, P])
        mem.ident_bf = sb("ident_bf", [P, P], BF16)
        mem.mask_bf = sb("mask_bf", [P, P], BF16)
        mem.maskT_bf = sb("maskT_bf", [P, P], BF16)
        with ExitStack() as layer0:
            sb0 = lambda n, s, d=F32: layer0.enter_context(nc.sbuf_tensor(n, s, d))
            mem.W = [sb0(f"W{i}", [P, 3, N]) for i in range(2)]
            with ExitStack() as attn0:
                sba = lambda n, s, d=F32: attn0.enter_context(nc.sbuf_tensor(n, s, d))
                mem.gxT = sba("gxT", [P, KT, N])
                mem.cos = sba("cosT", [P, N])
                mem.sin = sba("sinT", [P, N])
                mem.kT = sba("kT", [P, N])
                mem.v = sba("v", [P, NT, DH])
                setup_phase(nc, c, io, mem)
                attention0_phase(nc, c, io, mem)
            mlp0_phase(nc, c, io, mem)
        layer1(nc, io, mem)


def constants():
    inv = (1.0 / 10000.0 ** (np.arange(0, DH, 2, dtype=np.float32) / np.float32(DH))).astype(np.float32)
    freqs = (np.arange(N, dtype=np.float32)[:, None] * inv[None, :]).astype(np.float32).T
    cos, sin = np.cos(freqs).astype(np.float32), np.sin(freqs).astype(np.float32)
    slopes = (np.float32(2.0 ** (-8.0 / HEADS)) ** np.arange(1, HEADS + 1, dtype=np.float32)).astype(np.float32)
    r = np.arange(P)

    def parts(w):
        out = []
        for _ in range(3):
            out.append((w.view(np.uint32) >> 16).astype(np.uint16))
            w = w - (out[-1].astype(np.uint32) << 16).view(np.float32)
        return out

    slope, place = parts(slopes), parts(np.arange(1 - N, 1, dtype=np.float32))
    alibi_q = np.stack([slope[a] for a, _ in PARTS], 1)[:, :, None] + np.zeros((1, 1, N), np.uint16)
    ones = parts(np.ones(N, np.float32))[0]
    alibi_k = np.stack([place[b] for _, b in PARTS] + [ones] * 3)
    return {
        "cos": np.concatenate([cos, cos]),
        "sin": np.concatenate([sin, -sin]),
        "identity": np.eye(P, dtype=np.float32),
        "causal": np.where(r[None, :] > r[:, None], np.float32(NEG), np.float32(0)).astype(np.float32),
        "before": (r[:, None] < r[None, :]).astype(np.float32),
        "alibi_q": alibi_q, "alibi_k": alibi_k,
        "causalT": np.where(r[:, None] > r[None, :], np.float32(NEG), np.float32(0)).astype(np.float32),
        "expert_ids": np.ascontiguousarray(np.broadcast_to(np.arange(E, dtype=np.float32), (P, E))),
    }


def layouts(a):
    def gate_like(w):
        return w.reshape(8, P, 2, -1).transpose(0, 2, 3, 1).reshape(NBLK, -1, P)

    def down_like(w, k):
        return w.reshape(2, P, 8, k).transpose(2, 0, 3, 1).reshape(NBLK, k, P)

    def col(w):
        return w.reshape(KT, P).T

    packed = [gate_like(a["L0_ffn_gate_W_packed"]), gate_like(a["L0_ffn_up_W_packed"]),
              down_like(a["L0_ffn_down_W_packed"], P)]
    scales = [gate_like(a["L0_ffn_gate_scales"]), gate_like(a["L0_ffn_up_scales"]),
              down_like(a["L0_ffn_down_scales"], 8)]
    wq = a["L0_attn_Wq"].reshape(D, HEADS, DH).transpose(1, 0, 2)
    out = {
        "x": a["L0_attn_x"], "gamma": col(a["L0_attn_gamma"]), "Wkv": a["L0_attn_Wkv"], "Wo": a["L0_attn_Wo"],
        "Wq": np.concatenate([wq, wq[:1]]),
        "packed": np.stack(packed, axis=2), "scales": np.stack(scales, axis=2),
        "Wq1": a["L1_attn_Wq"], "Wk1": a["L1_attn_Wk"], "Wv1": a["L1_attn_Wv"], "Wo1": a["L1_attn_Wo"],
        "bq1": col(a["L1_attn_bq"]), "bk1": col(a["L1_attn_bk"]), "bv1": a["L1_attn_bv"], "bo1": a["L1_attn_bo"],
        "router": a["L1_ffn_router_weight"], "gate": a["L1_ffn_gate_proj"], "up": a["L1_ffn_up_proj"],
        "down": a["L1_ffn_down_proj"],
    }
    return {k: np.ascontiguousarray(v) for k, v in out.items()}


def kernel(**inputs):
    import concourse.bacc as bacc
    from concourse.bass_utils import run_bass_kernel_spmd

    nc = bacc.Bacc("TRN2", target_bir_lowering=False, num_devices=1)
    arrays, io = {}, {}
    for name, a in {**layouts({k: np.asarray(v) for k, v in inputs.items()}), **constants()}.items():
        arrays["in_" + name] = a
        io[name] = nc.dram_tensor("in_" + name, a.shape, mybir.dt.from_np(a.dtype), kind="ExternalInput").ap()
    io["out"] = nc.dram_tensor("out", [1, N, D], F32, kind="ExternalOutput").ap()
    build(nc, io)
    r = run_bass_kernel_spmd(nc, [arrays], core_ids=[0])
    return r.results[0]["out"]
```

```python
import math
from contextlib import ExitStack

import numpy as np

import concourse.bass as bass
from concourse import mybir

F32 = mybir.dt.float32
BF16 = mybir.dt.bfloat16
F16 = mybir.dt.float16
I32 = mybir.dt.int32
U32 = mybir.dt.uint32
ALU = mybir.AluOpType
ACT = mybir.ActivationFunctionType
AX = mybir.AxisListType

P = 128
N = 2048
D = 256
NT = N // P
KT = D // P
CH = 512
NC = N // CH
TPC = CH // P
EPS = 1e-5
HEADS = 16
DH = 128
HD = D // HEADS
KA = HD + 1
PARTS = [(0, 0), (1, 0), (2, 0), (0, 1), (1, 1), (0, 2)]
KS = len(PARTS) * (HD + 1)
KM = KS + 3
NBLK = 16
E, I, TOPK = 64, 96, 8
CAP = 2 * (512 * TOPK) // E
EG = 4
NEG = -3.0e38
HALVES = [(0, 0), (1, 0), (0, 1)]
KTHALVES = [(k, ab) for k in range(KT) for ab in HALVES]
WO_SCALE, O_SCALE = 64.0, 1 / 8
WSCALE = 64.0


class Tally:

    def __init__(self, sem):
        self.sem = sem
        self.n = 0

    def need(self, eng, k=1):
        self.n += k
        eng.wait_ge(self.sem, self.n)

    def give_back(self, eng):
        if self.n:
            eng.sem_inc(self.sem, -self.n)
        self.n = 0


class Chain:

    def __init__(self, eng, sem):
        self.eng = eng
        self.t = Tally(sem)

    def __call__(self, ins):
        ins.then_inc(self.t.sem, 1)
        self.t.need(self.eng)

    def give_back(self):
        self.t.give_back(self.eng)


def groups_of(t):
    return [(b, min(4, t + 1 - b)) for b in range(0, t + 1, 4)]


def setup_phase(nc, io, mem):
    with ExitStack() as ctx:
        sb = lambda n, s, d=F32: ctx.enter_context(nc.sbuf_tensor(n, s, d))
        ps = lambda n, s, d=F32: ctx.enter_context(nc.psum_tensor(n, s, d))
        sem = lambda n: ctx.enter_context(nc.semaphore(n))
        xn = sb("xn0", [P, NT, D])
        xg = sb("xg", [P, NT, D])
        st = sb("st0", [P, 2, NT, 6])
        mv = sb("mv0", [P, 2, NT, 2])
        rstd = sb("rstd0", [P, 2, NT])
        mhalf = sb("mhalf0", [P, NT])
        wkv = sb("wkv", [P, KT, 2 * DH])
        gam = sb("gam", [P, KT])
        maskf = sb("maskf", [P, 2, P])
        ra = sb("rope_a0", [P, CH])
        rb = sb("rope_b0", [P, CH])
        zeros = sb("zeros", [P, 2048])
        wkv_part = [sb(f"wkv_part{i}", [P, KT, 2 * DH], F16) for i in range(2)]
        TP = [ps(f"TP{i}", [P, 4, P]) for i in range(4)]
        KP = [ps(f"KP{i}", [P, CH]) for i in range(2)]
        VP = [ps(f"VP{i}", [P, CH]) for i in range(2)]
        x_in = [sem(f"x_in{i}") for i in range(2)]
        const_in, zero_set = sem("const_in"), sem("zero_set")
        pool0 = sem("pool0")
        dve0, stat_ready, rstd_ready = sem("dve0"), sem("stat_ready"), sem("rstd_ready")
        xn_ready, xg_ready = sem("xn_ready"), sem("xg_ready")
        turned, t_out, x_high, x_low = sem("turned0"), sem("t_out0"), sem("x_high"), sem("x_low")
        k_done, k_free, v_done, v_high, v_out = (sem(n) for n in ("k_done", "k_free", "v_done", "v_high", "v_out"))
        block = ctx.enter_context(nc.Block())
        ORDER = [("k", 0), ("k", 1), ("v", 0), ("v", 1), ("k", 2), ("v", 2), ("k", 3), ("v", 3)]

        @block.sync
        def _(sp):
            xv = io["x"][0].rearrange("(t p) c -> p t c", p=P)
            for i in range(NC):
                sp.dma_start(mem.x[:, TPC * i:TPC * (i + 1), :], xv[:, TPC * i:TPC * (i + 1), :]).then_inc(x_in[min(i, 1)], 16)
            sp.dma_start(mem.ident[:], io["identity"]).then_inc(const_in, 16)
            sp.dma_start(maskf[:, 0], io["causal"]).then_inc(const_in, 16)
            sp.dma_start(maskf[:, 1], io["causalT"]).then_inc(const_in, 16)
            sp.dma_start(gam[:], io["gamma"]).then_inc(const_in, 16)
            sp.dma_start(mem.cos[:], io["cos"]).then_inc(const_in, 16)
            sp.dma_start(mem.sin[:], io["sin"]).then_inc(const_in, 16)
            sp.dma_start(wkv[:], io["Wkv"].rearrange("(k p) n -> p k n", p=P)).then_inc(const_in, 16)
            sp.wait_ge(zero_set, 1)
            zv = mem.xe.rearrange("(a p r) c -> a p (r c)", a=8, p=P)
            for a in range(8):
                sp.dma_start(zv[a], zeros[:]).then_inc(mem.xe_zeroed, 16)
            sp.wait_ge(mem.xe_zeroed, 8 * 16)

        @block.gpsimd
        def _(pool):
            pool.memset(zeros[:], 0.0).then_inc(zero_set, 1)
            pool.memset(mhalf[:], -0.5).then_inc(pool0, 1)
            for part in range(2):
                pool.memset(mem.xT[part][:, :, N:], 0.0).then_inc(zero_set, 1)
            pool.memset(mem.acc[:], 0.0).then_inc(zero_set, 1)
            for k in range(2):
                pool.wait_ge(stat_ready, NT * (k + 1))
                pool.tensor_scalar(rstd[:, k, :], mv[:, k, :, 1], EPS, None, ALU.add).then_inc(pool0, 1)
                pool.wait_ge(pool0, k + 2)
                pool.tensor_tensor(rstd[:, k, :], rstd[:, k, :], mhalf[:], ALU.pow).then_inc(rstd_ready, 1)

        @block.vector
        def _(v):
            own = Chain(v, dve0)
            for k, src, dst, ready in ((0, mem.x, xn, xn_ready), (1, xn, xg, xg_ready)):
                for t in range(NT):
                    if k == 0 and t in (0, TPC):
                        v.wait_ge(x_in[t // TPC], 16 if t == 0 else 16 * (NC - 1))
                    ins = v.bn_stats(st[:, k, t, :], src[:, t, :])
                    ins.then_inc(dve0, 1)
                    own.t.n += 1
                    if k == 1 and t % 2:
                        n = t // 2
                        v.wait_ge(x_high, n + 1)
                        tp = TP[n % 4][:].rearrange("p (a k) c -> p k a c", a=2)
                        now = slice(P * (t - 1), P * (t + 1))
                        for j in range(KT):
                            hi, lo = (mem.xT[i][:, j, now].rearrange("p (a c) -> p a c", a=2) for i in range(2))
                            ins = v.tensor_tensor(lo, tp[:, j], hi, ALU.subtract)
                        ins.then_inc(x_low, 1)
                v.wait_ge(dve0, own.t.n)
                for t in range(NT):
                    v.bn_aggr(mv[:, k, t, :], st[:, k, t, :]).then_inc(stat_ready, 1)
                if k == 0:
                    v.wait_ge(const_in, 7 * 16)
                    v.tensor_copy(mem.ident_bf[:], mem.ident[:]).then_inc(dve0, 1)
                    v.tensor_copy(mem.mask_bf[:], maskf[:, 0]).then_inc(dve0, 1)
                    v.tensor_copy(mem.maskT_bf[:], maskf[:, 1]).then_inc(dve0, 1)
                    own.t.n += 3
                    own(v.tensor_copy(wkv_part[0][:], wkv[:]))
                    own(v.tensor_tensor(wkv_part[1][:], wkv[:], wkv_part[0][:], ALU.subtract))
                v.wait_ge(rstd_ready, k + 1)
                for t in range(NT):
                    v.tensor_scalar(dst[:, t, :], src[:, t, :], mv[:, k, t, 0:1], rstd[:, k, t:t + 1],
                                    ALU.subtract, ALU.mult).then_inc(ready, 1)
                v.wait_ge(ready, NT)
            for n in range(NT // 2, NT):
                v.wait_ge(x_high, n + 1)
                tp = TP[n % 4][:].rearrange("p (a k) c -> p k a c", a=2)
                t = 2 * n - NT
                now = slice(P * t, P * (t + 2))
                for j in range(KT):
                    hi, lo = (mem.gxT[i][:, j, now].rearrange("p (a c) -> p a c", a=2) for i in range(2))
                    ins = v.scalar_tensor_tensor(lo, tp[:, j], gam[:, j:j + 1], hi, ALU.mult, ALU.subtract)
                ins.then_inc(t_out, 1)

            def finish_keys(i):
                cs = slice(CH * i, CH * (i + 1))
                v.wait_ge(k_done, i + 1)
                v.tensor_tensor(ra[:], KP[i % 2][:], mem.cos[:, cs], ALU.mult).then_inc(dve0, 1)
                v.tensor_tensor(rb[0:64], KP[i % 2][64:P], mem.sin[64:P, cs], ALU.mult).then_inc(dve0, 1)
                own.t.n += 2
                own(v.tensor_tensor(rb[64:P], KP[i % 2][0:64], mem.sin[0:64, cs], ALU.mult))
                own(v.tensor_tensor(ra[:], ra[:], rb[:], ALU.add))
                own(v.tensor_scalar(ra[:], ra[:], float(DH) ** -0.5, None, ALU.mult))
                own(v.tensor_copy(mem.kT[0][:, cs], ra[:]))
                v.tensor_tensor(mem.kT[1][:, cs], ra[:], mem.kT[0][:, cs], ALU.subtract).then_inc(k_free, 1)
                v.wait_ge(k_free, i + 1)

            def finish_values(i):
                v.wait_ge(v_high, i + 1)
                rows = slice(4 * i, 4 * i + 4)
                v.tensor_tensor(mem.v[1][:, rows, :], VP[i % 2][:].rearrange("p (a c) -> p a c", a=4),
                                mem.v[0][:, rows, :], ALU.subtract).then_inc(v_out, 1)

            for what, i in ORDER:
                finish_keys(i) if what == "k" else finish_values(i)

        @block.tensor
        def _(pe):
            pe.wait_ge(const_in, 7 * 16)
            n = 0
            for k, src, ready in ((0, xn, xn_ready), (1, xg, xg_ready)):
                for t in range(NT):
                    pe.wait_ge(ready, t + 1)
                    if n % 2 == 0 and n >= 8:
                        if n < NT + 8:
                            pe.wait_ge(x_low, n // 2 - 3)
                        else:
                            pe.wait_ge(t_out, n // 2 - 3 - NT // 2)
                    for j in range(KT):
                        cols = src[:, t, j::2] if k == 0 else src[:, t, P * j:P * (j + 1)]
                        ins = pe.transpose(TP[n // 2 % 4][:, 2 * (n % 2) + j, :], cols, mem.ident[:])
                    if n % 2:
                        ins.then_inc(turned, 1)
                    n += 1
            pe.wait_ge(t_out, NT // 2)

            def keys(i):
                if i >= 2:
                    pe.wait_ge(k_free, i - 1)
                for n, (j, (a, b)) in enumerate(KTHALVES):
                    ins = pe.matmul(KP[i % 2][:], wkv_part[a][:, j, 0:DH], mem.gxT[b][:, j, CH * i:CH * (i + 1)],
                                    start=(n == 0), stop=(n == len(KTHALVES) - 1))
                ins.then_inc(k_done, 1)

            def values(i):
                if i >= 2:
                    pe.wait_ge(v_out, i - 1)
                for q in range(4):
                    t = 4 * i + q
                    for n, (j, (a, b)) in enumerate(KTHALVES):
                        ins = pe.matmul(VP[i % 2][:, P * q:P * (q + 1)], mem.gxT[a][:, j, P * t:P * (t + 1)],
                                        wkv_part[b][:, j, DH:2 * DH], start=(n == 0), stop=(n == len(KTHALVES) - 1))
                ins.then_inc(v_done, 1)

            for what, i in ORDER:
                keys(i) if what == "k" else values(i)

        @block.scalar
        def _(act):
            act.wait_ge(const_in, 7 * 16)
            for n in range(2 * NT // 2):
                k, t = n // (NT // 2), 2 * n % NT
                act.wait_ge(turned, n + 1)
                tp = TP[n % 4][:].rearrange("p (a k) c -> p k a c", a=2)
                dst = (mem.xT, mem.gxT)[k][0][:, :, P * t:P * (t + 2)].rearrange("p k (a c) -> p k a c", a=2)
                for j in range(KT):
                    if k == 0:
                        ins = act.copy(dst[:, j], tp[:, j])
                    else:
                        ins = act.activation(dst[:, j], tp[:, j], ACT.Copy, scale=gam[:, j:j + 1])
                ins.then_inc(x_high, 1)
            for i in range(NC):
                act.wait_ge(v_done, i + 1)
                act.copy(mem.v[0][:, 4 * i:4 * i + 4, :], VP[i % 2][:].rearrange("p (a c) -> p a c", a=4)).then_inc(v_high, 1)


def attention0_phase(nc, io, mem):
    with ExitStack() as ctx:
        sb = lambda n, s, d=F32: ctx.enter_context(nc.sbuf_tensor(n, s, d))
        ps = lambda n, s, d=F32: ctx.enter_context(nc.psum_tensor(n, s, d))
        sem = lambda n: ctx.enter_context(nc.semaphore("a0_" + n))
        qT = [sb(f"qT{i}", [P, N], F16) for i in range(2)]
        wq = sb("wq", [P, KT, DH])
        wo = sb("wo", [P, D])
        wq_part = [sb(f"wq_part{i}", [P, KT, DH], F16) for i in range(2)]
        wo_part = [sb(f"wo_part{i}", [P, D], F16) for i in range(2)]
        probs = sb("probs", [P, 2, N])
        PT = [sb(f"PT{i}", [P, 4, CH], F16) for i in range(2)]
        oT = [sb(f"oT{i}", [P, 2, P], F16) for i in range(2)]
        piecemax = sb("piecemax", [P, 2, 2])
        negmax = sb("negmax", [P, 2])
        rowsum = sb("rowsum", [P, 4, 2])
        rinv = sb("rinv", [P, 2])
        qraw = sb("qraw", [P, 2, CH])
        ra = sb("rope_a", [P, CH])
        rb = sb("rope_b", [P, CH])
        raw = sb("raw", [P, 3, P], I32)
        scl = sb("scl", [P, 3, P])
        mag = sb("mag", [P, 2, 3, P], I32)
        sgn = sb("sgn", [P, 2, 3, P], I32)
        val = sb("val", [P, 3, P])
        val2 = sb("val2", [P, 3, P])
        sgf = rb[:, 0:3 * P].rearrange("p (m n) -> p m n", m=3)
        S = ps("S", [P, N])
        T = [ps(f"T{i}", [P, CH]) for i in range(2)]
        O = ps("O", [P, CH])
        Y = ps("Y", [P, CH])
        names = ("w_in w_free parts_ready parts_free raw_in raw_free scl_in scl_free fields_ready fields_free "
                 "proj_done bank_free qraw_in qraw_free q_ready scores_done "
                 "negmax_ready probs_done turned pt_high pt_low o_done oT_high oT_ready y_done y_free act dve pool")
        s = {n: sem(n) for n in names.split()}
        block = ctx.enter_context(nc.Block())
        tiles = list(range(NT - 1, -1, -1))
        HALF = N // 2

        def pieces(i):
            nk = P * (tiles[i] + 1)
            return [(k0, min(nk, k0 + HALF)) for k0 in range(0, nk, HALF)]

        def place(i):
            return 0 if len(pieces(i)) == 2 or i % 2 == 0 else HALF

        first_small = next(i for i in range(NT) if len(pieces(i)) == 1)
        early = {i: [(i + 1, p) for p in range(len(pieces(i + 1)))] for i in range(first_small)}
        early.update({i: [(i + 2, 0)] for i in range(first_small, NT - 1)})
        early[NT - 1] = [(NT, 1)]
        late = {first_small - 1: [(first_small + 1, 0)]}
        third, second = tiles.index(4 * (NC - 1)), NT - TPC

        @block.sync
        def _(sp):
            w_free, raw_free, scl_free = (Tally(s[n]) for n in ("w_free", "raw_free", "scl_free"))
            sp.dma_start(wq[:], io["Wq"][0].rearrange("(k p) n -> p k n", p=P)).then_inc(s["w_in"], 16)
            with sp.Fori(0, HEADS) as h:
                w_free.need(sp)
                sp.dma_start(wq[:], io["Wq"][bass.ds(h + 1, 1)].rearrange("a (k p) n -> p (a k) n", p=P)).then_inc(s["w_in"], 16)
                sp.dma_start(wo[:], io["Wo"][bass.ds(h * DH, DH), :]).then_inc(s["w_in"], 16)
                raw_free.need(sp)
                sp.dma_start(raw[:], io["packed"][bass.ds(h, 1)].rearrange("a p m n -> p (a m) n")).then_inc(s["raw_in"], 16)
                scl_free.need(sp)
                for a in range(8):
                    src = io["scales"][bass.ds(h, 1), a:a + 1].rearrange("b a m n -> (b a) m n").broadcast_to([16, 3, P])
                    sp.dma_start(scl[16 * a:16 * (a + 1)], src).then_inc(s["scl_in"], 16)
                for x in (w_free, raw_free, scl_free):
                    x.give_back(sp)

        @block.gpsimd
        def _(pool):
            qraw_in, own = Tally(s["qraw_in"]), Chain(pool, s["pool"])
            scl_in, fields_ready = Tally(s["scl_in"]), Tally(s["fields_ready"])
            w_in, parts_free = Tally(s["w_in"]), Tally(s["parts_free"])
            pool.sem_inc(s["qraw_free"], 2)
            pool.sem_inc(s["scl_free"], 1)
            pool.sem_inc(s["fields_free"], 1)

            def rotate(i):
                cs, n = slice(CH * i, CH * (i + 1)), (NC - 1 - i) % 2
                qraw_in.need(pool)
                own(pool.tensor_tensor(ra[:], qraw[:, n], mem.cos[:, cs], ALU.mult))
                own(pool.tensor_tensor(rb[0:64], qraw[64:P, n], mem.sin[64:P, cs], ALU.mult))
                own(pool.tensor_tensor(rb[64:P], qraw[0:64, n], mem.sin[0:64, cs], ALU.mult))
                pool.sem_inc(s["qraw_free"], 1)
                own(pool.tensor_tensor(ra[:], ra[:], rb[:], ALU.add))
                own(pool.tensor_copy(qT[0][:, cs], ra[:]))
                own(pool.tensor_tensor(qT[1][:, cs], ra[:], qT[0][:, cs], ALU.subtract))
                pool.sem_inc(s["q_ready"], 1)

            def unpack(nib, h):
                own(pool.tensor_scalar(val[:], mag[:, nib], 4.0, None, ALU.max))
                own(pool.tensor_scalar(val2[:], mag[:, nib], 6.0, 2.0, ALU.max, ALU.mult))
                own(pool.tensor_scalar(sgf[:], mag[:, nib], 0.0, None, ALU.add))
                own(pool.tensor_tensor(val[:], val[:], sgf[:], ALU.add))
                own(pool.tensor_tensor(val[:], val[:], val2[:], ALU.add))
                own(pool.tensor_scalar(sgf[:], sgn[:, nib], -0.125 * WSCALE, 0.5 * WSCALE, ALU.mult, ALU.add))
                own(pool.tensor_tensor(sgf[:], sgf[:], scl[:], ALU.mult))
                own(pool.tensor_scalar(val2[:], val[:], -16.0, None, ALU.add))
                own(pool.tensor_tensor(val[:], val2[:], sgf[:], ALU.mult))
                high, low = (mem.W[nib][part][:, :, bass.ds(h * P, P)] for part in range(2))
                own(pool.tensor_copy(high, val[:]))
                own(pool.tensor_tensor(low, val[:], high, ALU.subtract))

            def split_queries():
                own(pool.tensor_copy(wq_part[0][:], wq[:]))
                own(pool.tensor_tensor(wq_part[1][:], wq[:], wq_part[0][:], ALU.subtract))

            w_in.need(pool, 16)
            split_queries()
            pool.sem_inc(s["parts_ready"], 1)
            pool.sem_inc(s["w_free"], 1)
            rotate(3)
            rotate(2)
            w_in.give_back(pool)
            qraw_in.give_back(pool)
            own.give_back()
            with pool.Fori(0, HEADS) as h:
                w_in.need(pool, 2 * 16)
                parts_free.need(pool)
                own(pool.tensor_scalar(wo[:], wo[:], WO_SCALE, None, ALU.mult))
                own(pool.tensor_copy(wo_part[0][:], wo[:]))
                own(pool.tensor_tensor(wo_part[1][:], wo[:], wo_part[0][:], ALU.subtract))
                split_queries()
                pool.sem_inc(s["parts_ready"], 1)
                pool.sem_inc(s["w_free"], 1)
                rotate(1)
                rotate(0)
                rotate(3)
                scl_in.need(pool, 8 * 16)
                fields_ready.need(pool)
                unpack(0, h)
                unpack(1, h)
                pool.sem_inc(s["scl_free"], 1)
                pool.sem_inc(s["fields_free"], 1)
                rotate(2)
                for x in (qraw_in, scl_in, fields_ready, w_in, parts_free):
                    x.give_back(pool)
                own.give_back()

        @block.tensor
        def _(pe):
            parts_ready, q_ready = Tally(s["parts_ready"]), Tally(s["q_ready"])
            probs_done, pt = Tally(s["probs_done"]), Tally(s["pt_low"])
            oT_ready, y_free, bank_free = Tally(s["oT_ready"]), Tally(s["y_free"]), Tally(s["bank_free"])

            def project(i, bank):
                for n, (j, (a, b)) in enumerate(KTHALVES):
                    ins = pe.matmul(bank, wq_part[a][:, j, :], mem.gxT[b][:, j, CH * i:CH * (i + 1)],
                                    start=(n == 0), stop=(n == len(KTHALVES) - 1))
                ins.then_inc(s["proj_done"], 1)

            def scores(i, piece):
                i %= NT
                t = tiles[i]
                if piece == 0 and t % TPC == TPC - 1:
                    q_ready.need(pe)
                p0, p1 = pieces(i)[piece]
                for k0 in range(p0, p1, CH):
                    k1 = min(p1, k0 + CH)
                    diagonal = k1 == P * (t + 1)
                    out = S[:, place(i) + k0:place(i) + k1]
                    for n, (a, b) in enumerate(HALVES):
                        ins = pe.matmul(out, qT[a][:, P * t:P * (t + 1)], mem.kT[b][:, k0:k1],
                                        start=(n == 0), stop=(n == len(HALVES) - 1 and not diagonal))
                    if diagonal:
                        ins = pe.matmul(S[:, place(i) + k1 - P:place(i) + k1], mem.ident_bf[:], mem.mask_bf[:],
                                        start=False, stop=True)
                ins.then_inc(s["scores_done"], 1)

            parts_ready.need(pe)
            project(3, S[:, 3 * CH:4 * CH])
            project(2, S[:, CH:2 * CH])
            bank_free.need(pe, 2)
            for p in range(2):
                scores(0, p)
            project(1, T[0][:])
            project(0, T[1][:])
            for x in (parts_ready, bank_free, q_ready):
                x.give_back(pe)
            with pe.Fori(0, HEADS) as h:
                g_at = 0

                def out_proj(i):
                    oT_ready.need(pe)
                    if i == 0:
                        parts_ready.need(pe)
                    y_free.need(pe)
                    for n, (a, b) in enumerate(HALVES):
                        ins = pe.matmul(Y[:, 0:D], oT[a][:, i % 2, :], wo_part[b][:], start=(n == 0), stop=(n == len(HALVES) - 1))
                    ins.then_inc(s["y_done"], 1)

                for i, t in enumerate(tiles):
                    groups = groups_of(t)

                    def turn(g):
                        b0, w = groups[g]
                        if i == 0 and g < 2:
                            bank_free.need(pe)
                        for b in range(b0, b0 + w):
                            ins = pe.transpose(T[(g_at + g) % 2][:, P * (b - b0):P * (b - b0 + 1)],
                                               probs[:, i % 2, P * b:P * (b + 1)], mem.ident[:])
                        ins.then_inc(s["turned"], 1)

                    def weigh(g):
                        b0, w = groups[g]
                        for b in range(b0, b0 + w):
                            for n, (x, y) in enumerate(HALVES):
                                ins = pe.matmul(O[:, 0:P], mem.v[x][:, b, :],
                                                PT[y][:, (g_at + g) % 4, P * (b - b0):P * (b - b0 + 1)],
                                                start=(b == 0 and n == 0), stop=(b == t and n == len(HALVES) - 1))
                        if g == len(groups) - 1:
                            ins.then_inc(s["o_done"], 1)

                    probs_done.need(pe)
                    turn(0)
                    if len(groups) > 1:
                        turn(1)
                    if i == NT - 2:
                        bank_free.need(pe)
                    for n, (j, p) in enumerate(early[i]):
                        if n == 1:
                            probs_done.need(pe)
                        scores(j, p)
                    if i > 0:
                        out_proj(i - 1)
                    if i == third:
                        project(3, S[:, 3 * CH:4 * CH])
                    if i == second:
                        project(2, S[:, CH:2 * CH])
                    if i == NT - 1:
                        project(1, T[(g_at + 1) % 2][:])
                    if len(groups) > 2:
                        if len(early[i]) == 1:
                            probs_done.need(pe)
                        pt.need(pe)
                        turn(2)
                        pt.need(pe)
                        if len(groups) > 3:
                            turn(3)
                        weigh(0)
                        for j, p in late.get(i, []):
                            bank_free.need(pe)
                            scores(j, p)
                        weigh(1)
                        for g in range(2, len(groups)):
                            pt.need(pe)
                            weigh(g)
                    else:
                        for g in range(len(groups)):
                            pt.need(pe)
                            weigh(g)
                    if i == NT - 1:
                        project(0, T[g_at % 2][:])
                    g_at += len(groups)
                out_proj(NT - 1)
                for x in (parts_ready, q_ready, probs_done, pt, oT_ready, y_free, bank_free):
                    x.give_back(pe)

        @block.vector
        def _(v):
            own = Chain(v, s["dve"])
            t_ = {n: Tally(s[n]) for n in "scores_done pt_high oT_high y_done raw_in fields_free".split()}
            v.sem_inc(s["y_free"], 1)
            v.sem_inc(s["raw_free"], 1)

            def row_max(i, piece):
                i %= NT
                p0, p1 = pieces(i)[piece]
                src = S[:, place(i) + p0:place(i) + p1]
                t_["scores_done"].need(v)
                if len(pieces(i)) == 1:
                    v.tensor_reduce(negmax[:, i % 2:i % 2 + 1], src, AX.X, ALU.max,
                                    negate=True).then_inc(s["negmax_ready"], 1)
                    return
                own(v.tensor_reduce(piecemax[:, i % 2, piece:piece + 1], src, AX.X, ALU.max))
                if piece == 1:
                    v.tensor_reduce(negmax[:, i % 2:i % 2 + 1], piecemax[:, i % 2, :], AX.X, ALU.max,
                                    negate=True).then_inc(s["negmax_ready"], 1)

            def output_low(i):
                t_["oT_high"].need(v)
                v.scalar_tensor_tensor(oT[1][:, i % 2, :], O[:, 0:P], O_SCALE, oT[0][:, i % 2, :], ALU.mult,
                                       ALU.subtract).then_inc(s["oT_ready"], 1)

            def add_up(i):
                t = tiles[i]
                t_["y_done"].need(v)
                if len(pieces(i)) == 2:
                    own(v.tensor_tensor(rowsum[:, i % 4, 0:1], rowsum[:, i % 4, 0:1], rowsum[:, i % 4, 1:2], ALU.add))
                own(v.reciprocal(rinv[:, i % 2:i % 2 + 1], rowsum[:, i % 4, 0:1]))
                v.scalar_tensor_tensor(mem.acc[:, t, :], Y[:, 0:D], rinv[:, i % 2:i % 2 + 1],
                                       mem.acc[:, t, :], ALU.mult, ALU.add).then_inc(s["y_free"], 1)

            for p in range(2):
                row_max(0, p)
            t_["scores_done"].give_back(v)
            own.give_back()
            with v.Fori(0, HEADS) as h:
                g_at = 0
                for i, t in enumerate(tiles):
                    groups = groups_of(t)

                    def low(g):
                        w = groups[g][1] * P
                        t_["pt_high"].need(v)
                        v.tensor_tensor(PT[1][:, (g_at + g) % 4, 0:w], T[(g_at + g) % 2][:, 0:w],
                                        PT[0][:, (g_at + g) % 4, 0:w], ALU.subtract).then_inc(s["pt_low"], 1)

                    if i > 0:
                        output_low(i - 1)
                    for g in range(min(2, len(groups))):
                        low(g)
                    for j, p in early[i]:
                        row_max(j, p)
                    for g in range(2, len(groups)):
                        low(g)
                    for j, p in late.get(i, []):
                        row_max(j, p)
                    if i > 0:
                        add_up(i - 1)
                    if i == 1:
                        t_["raw_in"].need(v, 16)
                        t_["fields_free"].need(v)
                    if 1 <= i < 5:
                        nib, field, mask = (i - 1) // 2, (sgn, mag)[i % 2], (8, 7)[i % 2]
                        own(v.tensor_scalar(field[:, nib], raw[:], 4 * nib, mask, ALU.logical_shift_right, ALU.bitwise_and))
                    if i == 4:
                        v.sem_inc(s["fields_ready"], 1)
                        v.sem_inc(s["raw_free"], 1)
                    g_at += len(groups)
                output_low(NT - 1)
                add_up(NT - 1)
                v.sem_inc(s["parts_free"], 1)
                for x in t_.values():
                    x.give_back(v)
                own.give_back()

        @block.scalar
        def _(act):
            own = Chain(act, s["act"])
            t_ = {n: Tally(s[n]) for n in "negmax_ready turned o_done proj_done qraw_free".split()}

            def exponent(i, piece):
                i %= NT
                p0, p1 = pieces(i)[piece]
                if piece == 0:
                    t_["negmax_ready"].need(act)
                act.activation(probs[:, i % 2, p0:p1], S[:, place(i) + p0:place(i) + p1], ACT.Exp,
                               bias=negmax[:, i % 2:i % 2 + 1],
                               accum_out=rowsum[:, i % 4, piece:piece + 1]).then_inc(s["probs_done"], 1)

            def take_output(i):
                t_["o_done"].need(act)
                act.activation(oT[0][:, i % 2, :], O[:, 0:P], ACT.Copy, scale=O_SCALE).then_inc(s["oT_high"], 1)

            def take_queries(i, bank):
                t_["proj_done"].need(act)
                t_["qraw_free"].need(act)
                own(act.copy(qraw[:, (NC - 1 - i) % 2], bank))
                act.sem_inc(s["qraw_in"], 1)
                act.sem_inc(s["bank_free"], 1)

            take_queries(3, S[:, 3 * CH:4 * CH])
            take_queries(2, S[:, CH:2 * CH])
            exponent(0, 0)
            exponent(0, 1)
            take_queries(1, T[0][:])
            take_queries(0, T[1][:])
            act.sem_inc(s["parts_free"], 1)
            for x in t_.values():
                x.give_back(act)
            own.give_back()
            with act.Fori(0, HEADS) as h:
                g_at = 0
                for i, t in enumerate(tiles):
                    groups = groups_of(t)

                    def high(g):
                        w = groups[g][1] * P
                        t_["turned"].need(act)
                        act.copy(PT[0][:, (g_at + g) % 4, 0:w], T[(g_at + g) % 2][:, 0:w]).then_inc(s["pt_high"], 1)

                    if i > 0:
                        take_output(i - 1)
                    for g in range(len(groups)):
                        high(g)
                    exponent(i + 1, 0)
                    if i == NT - 1:
                        take_output(i)
                        take_queries(1, T[(g_at + 1) % 2][:])
                    if len(pieces((i + 1) % NT)) == 2:
                        exponent(i + 1, 1)
                    if i == third:
                        take_queries(3, S[:, 3 * CH:4 * CH])
                    if i == second:
                        take_queries(2, S[:, CH:2 * CH])
                    if i == NT - 1:
                        take_queries(0, T[g_at % 2][:])
                    g_at += len(groups)
                for x in t_.values():
                    x.give_back(act)
                own.give_back()


def mlp0_phase(nc, io, mem):
    with ExitStack() as ctx:
        sb = lambda n, s, d=F32: ctx.enter_context(nc.sbuf_tensor(n, s, d))
        ps = lambda n, s, d=F32: ctx.enter_context(nc.psum_tensor(n, s, d))
        sem = lambda n: ctx.enter_context(nc.semaphore("m0_" + n))
        sq = sb("sq", [P, 2, CH])
        th = sb("th", [P, 2, CH])
        hid = sb("hid", [P, 2, CH])
        hid_part = [sb(f"hid_part{i}", [P, 4, CH], F16) for i in range(2)]
        thf = sb("thf", [P, TPC, D])
        G = [ps(f"G{i}", [P, CH]) for i in range(3)]
        U = [ps(f"U{i}", [P, CH]) for i in range(3)]
        F = ps("F", [P, TPC, D])
        names = ("gate_act gate_dve squared poly tanhed hid_ready hid_high hid_low f_done f_free f_tanhed f_gated "
                 "thf_free dve pool")
        s = {n: sem(n) for n in names.split()}
        block = ctx.enter_context(nc.Block())

        def bank_of(b):
            b %= NBLK
            return b % 3 if b < NBLK - 1 else 1

        @block.tensor
        def _(pe):
            t_ = {n: Tally(s[n]) for n in "hid_low f_free".split()}

            def gate_up(b, c4):
                c4, b, bank = c4 + b // NBLK, b % NBLK, bank_of(b)
                for w, out in ((0, G[bank]), (1, U[bank])):
                    n = 0
                    for k in range(KT):
                        for x, y in HALVES:
                            ins = pe.matmul(out[:], mem.W[k][x][:, w, P * b:P * (b + 1)],
                                            mem.xT[y][:, k, bass.ds(c4 * CH, CH)],
                                            start=(n == 0), stop=(n == KT * len(HALVES) - 1))
                            n += 1
                    if w == 0:
                        ins.then_inc(s["gate_act"], 1)
                    else:
                        ins.then_inc(s["gate_dve"], 1)

            def down(b):
                jt, nib = b // 2, b % 2
                if b == 0:
                    t_["f_free"].need(pe)
                t_["hid_low"].need(pe)
                for q in range(TPC):
                    for n, (x, y) in enumerate(HALVES):
                        ins = pe.matmul(F[:, q, :], hid_part[x][:, b % 4, P * q:P * (q + 1)],
                                        mem.W[nib][y][:, 2, 2 * P * jt:2 * P * (jt + 1)],
                                        start=(b == 0 and q % 2 == 0 and n == 0), stop=(b == NBLK - 1 and n == 2),
                                        skip_group_check=True)
                if b == NBLK - 1:
                    ins.then_inc(s["f_done"], 1)

            gate_up(0, 0)
            gate_up(1, 0)
            with pe.Fori(0, NC) as c4:
                for b in range(NBLK):
                    later = bank_of(b + 2) == bank_of(b)
                    if not later:
                        gate_up(b + 2, c4)
                    down(b)
                    if later:
                        gate_up(b + 2, c4)
                for x in t_.values():
                    x.give_back(pe)

        @block.scalar
        def _(act):
            t_ = {n: Tally(s[n]) for n in "gate_act poly hid_ready f_done thf_free".split()}
            with act.Fori(0, NC) as c4:
                def square(b):
                    t_["gate_act"].need(act)
                    act.activation(sq[:, b % 2, :], G[bank_of(b)][:], ACT.Square, scale=1 / WSCALE).then_inc(s["squared"], 1)

                square(0)
                for b in range(NBLK):
                    t_["poly"].need(act)
                    act.activation(th[:, b % 2, :], sq[:, b % 2, :], ACT.Tanh, scale=0.7978845608028654 / WSCALE).then_inc(s["tanhed"], 1)
                    if b + 1 < NBLK:
                        square(b + 1)
                    t_["hid_ready"].need(act)
                    act.copy(hid_part[0][:, b % 4, :], hid[:, b % 2, :]).then_inc(s["hid_high"], 1)
                t_["thf_free"].need(act)
                t_["f_done"].need(act)
                act.activation(thf[:], F[:], ACT.Tanh, scale=0.5 / WSCALE).then_inc(s["f_tanhed"], 1)
                for x in t_.values():
                    x.give_back(act)

        @block.vector
        def _(v):
            own = Chain(v, s["dve"])
            t_ = {n: Tally(s[n]) for n in "gate_dve squared tanhed hid_high f_tanhed".split()}
            v.sem_inc(s["f_free"], 1)
            with v.Fori(0, NC) as c4:
                def low(b):
                    t_["hid_high"].need(v)
                    v.tensor_tensor(hid_part[1][:, b % 4, :], hid[:, b % 2, :], hid_part[0][:, b % 4, :],
                                    ALU.subtract).then_inc(s["hid_low"], 1)

                def poly(b):
                    t_["squared"].need(v)
                    own(v.tensor_scalar(sq[:, b % 2, :], sq[:, b % 2, :], 0.044715, 1.0, ALU.mult, ALU.add))
                    v.tensor_tensor(sq[:, b % 2, :], G[bank_of(b)][:], sq[:, b % 2, :], ALU.mult).then_inc(s["poly"], 1)

                poly(0)
                for b in range(NBLK):
                    t_["tanhed"].need(v)
                    own(v.scalar_tensor_tensor(th[:, b % 2, :], th[:, b % 2, :], 1.0, G[bank_of(b)][:], ALU.add, ALU.mult))
                    t_["gate_dve"].need(v)
                    v.scalar_tensor_tensor(hid[:, b % 2, :], th[:, b % 2, :], 0.5 / WSCALE ** 2, U[bank_of(b)][:], ALU.mult,
                                           ALU.mult).then_inc(s["hid_ready"], 1)
                    if b + 1 < NBLK:
                        poly(b + 1)
                    low(b)
                t_["f_tanhed"].need(v)
                own(v.scalar_tensor_tensor(thf[:], thf[:], 1.0, F[:], ALU.add, ALU.mult))
                v.sem_inc(s["f_free"], 1)
                v.sem_inc(s["f_gated"], 1)
                for x in t_.values():
                    x.give_back(v)
                own.give_back()

        @block.gpsimd
        def _(pool):
            own = Chain(pool, s["pool"])
            f_gated = Tally(s["f_gated"])
            pool.sem_inc(s["thf_free"], 1)
            own(pool.tensor_scalar(mem.acc[:], mem.acc[:], 0.5 / (WSCALE * WO_SCALE * O_SCALE), None, ALU.mult))
            own.give_back()
            with pool.Fori(0, NC) as c4:
                now = bass.ds(c4 * TPC, TPC)
                f_gated.need(pool)
                own(pool.tensor_tensor(thf[:], thf[:], mem.acc[:, now, :], ALU.mult))
                own(pool.tensor_tensor(mem.x[:, now, :], mem.x[:, now, :], thf[:], ALU.add))
                pool.sem_inc(s["thf_free"], 1)
                f_gated.give_back(pool)
                own.give_back()


def project1_phase(nc, io, mem, l1):
    with ExitStack() as ctx:
        sb = lambda n, s, d=F32: ctx.enter_context(nc.sbuf_tensor(n, s, d))
        ps = lambda n, s, d=F32: ctx.enter_context(nc.psum_tensor(n, s, d))
        sem = lambda n: ctx.enter_context(nc.semaphore("p1_" + n))
        w = {n: sb("w1" + n, [P, KT, D]) for n in "qkv"}
        wr = sb("w1r", [P, KT, E])
        bq, bk, bv = sb("bq", [P, KT]), sb("bk", [P, KT]), sb("bv", [P, D])
        bqs = sb("bqs", [P, KT])
        qf = sb("qf", [P, 4, CH])
        parts = sb("parts", [P, 2, KT, 3, N], BF16)
        st, mv = sb("st1", [P, NT, 6]), sb("mv1", [P, NT, 2])
        rstd, mhalf = sb("rstd1", [P, NT]), sb("mhalf1", [P, NT])
        prob, prob2 = sb("prob", [P, NT, E]), sb("prob2", [P, NT, E])
        rmax, rsum = sb("rmax", [P, NT]), sb("rsum1", [P, NT])
        top, idx, idxf = sb("top", [P, NT, TOPK]), sb("idx", [P, NT, TOPK], U32), sb("idxf", [P, NT, TOPK])
        mask, seen = sb("mask1", [P, NT, E], BF16), sb("seen", [P, NT, E], BF16)
        before, ones = sb("before", [P, P], BF16), sb("ones_bf", [P, P], BF16)
        beforef, eid = sb("beforef", [P, P]), sb("eid", [P, E])
        pos = prob
        hit, hit2 = sb("hit", [P, TOPK, E]), sb("hit2", [P, TOPK, E])
        posk, valid = sb("posk", [P, NT, TOPK]), sb("valid", [P, NT, TOPK])
        tk = sb("tk", [P, NT, TOPK])
        TP = [ps(f"TQ{i}", [P, 4, P]) for i in range(2)]
        MP = [ps(f"MQ{i}", [P, CH]) for i in range(3)]
        LP = ps("LP", [P, NT, E])
        VP = ps("VQ", [P, D])
        VALUES = [VP[:], TP[0][:, 0:2, :].rearrange("p a c -> p (a c)")]
        names = ("w_in stat_ready rstd_ready xn_ready turned t_out proj_done p_out v_done v_free logits_done "
                 "bias_ready shifted exped mask_ready pos_done dve pool qk_out rest_ready mid_ready split_done")
        s = {n: sem(n) for n in names.split()}
        block = ctx.enter_context(nc.Block())

        def part_of(n, j):
            i = n % NC
            return parts[:, n // (KT * NC), n // NC % KT, j, CH * i:CH * (i + 1)]

        @block.sync
        def _(sp):
            for n in "qkv":
                sp.dma_start(w[n][:], io[f"W{n}1"].rearrange("(k p) n -> p k n", p=P)).then_inc(s["w_in"], 16)
            sp.dma_start(wr[:], io["router"].rearrange("(k p) n -> p k n", p=P)).then_inc(s["w_in"], 16)
            sp.dma_start(bq[:], io["bq1"]).then_inc(s["w_in"], 16)
            sp.dma_start(bk[:], io["bk1"]).then_inc(s["w_in"], 16)
            sp.dma_start(bv[:], io["bv1"].rearrange("(a n) -> a n", a=1).broadcast_to([P, D])).then_inc(s["w_in"], 16)
            sp.dma_start(beforef[:], io["before"]).then_inc(s["w_in"], 16)
            sp.dma_start(eid[:], io["expert_ids"]).then_inc(s["w_in"], 16)
            for a, dst in enumerate((mem.qd, mem.kd)):
                for m in range(KT):
                    sp.wait_ge(s["split_done"], NC * (KT * a + m + 1))
                    for j in range(3):
                        sp.dma_start(dst[j, P * m:P * (m + 1), :], parts[:, a, m, j, :]).then_inc(s["qk_out"], 16)
            sp.wait_ge(s["qk_out"], 12 * 16)

        @block.gpsimd
        def _(pool):
            pool.memset(mhalf[:], -0.5).then_inc(s["pool"], 1)
            pool.memset(ones[:], 1.0).then_inc(s["pool"], 1)
            pool.wait_ge(s["stat_ready"], NT)
            pool.tensor_scalar(rstd[:], mv[:, :, 1], EPS, None, ALU.add).then_inc(s["pool"], 1)
            pool.wait_ge(s["pool"], 3)
            pool.tensor_tensor(rstd[:], rstd[:], mhalf[:], ALU.pow).then_inc(s["rstd_ready"], 1)
            pool.memset(mem.v1[:, :, :, HD:32], 0.0).then_inc(s["pool"], 1)
            pool.wait_ge(s["pool"], 4)
            pool.memset(mem.v1[:, :, :, HD:KA], 1.0).then_inc(s["pool"], 1)
            def rest(n):
                pool.wait_ge(s["p_out"], n + 1)
                pool.tensor_tensor(qf[:, n % 4, :], qf[:, n % 4, :], part_of(n, 0), ALU.subtract).then_inc(s["rest_ready"], 1)

            def low(n):
                pool.wait_ge(s["mid_ready"], n + 1)
                pool.tensor_tensor(part_of(n, 2), qf[:, n % 4, :], part_of(n, 1), ALU.subtract).then_inc(s["split_done"], 1)

            rest(0)
            for n in range(1, 2 * KT * NC):
                rest(n)
                low(n - 1)
            low(2 * KT * NC - 1)

        @block.tensor
        def _(pe):
            for t in range(NT):
                pe.wait_ge(s["xn_ready"], t + 1)
                if t % 2 == 0 and t >= 4:
                    pe.wait_ge(s["t_out"], t // 2 - 1)
                for j in range(KT):
                    ins = pe.transpose(TP[t // 2 % 2][:, 2 * (t % 2) + j, :], l1.xn[:, t, P * j:P * (j + 1)], mem.ident[:])
                if t % 2:
                    ins.then_inc(s["turned"], 1)
            pe.wait_ge(s["w_in"], 9 * 16)
            pe.wait_ge(s["t_out"], NT // 2)
            for t in range(NT):
                for j in range(KT):
                    ins = pe.matmul(LP[:, t, :], mem.xT[:, j, P * t:P * (t + 1)], wr[:, j, :], start=(j == 0), stop=(j == KT - 1))
            ins.then_inc(s["logits_done"], 1)
            n = 0
            for a, name in enumerate("qk"):
                for m in range(KT):
                    for i in range(NC):
                        if n >= 3:
                            pe.wait_ge(s["p_out"], n - 2)
                        for j in range(KT):
                            ins = pe.matmul(MP[n % 3][:], w[name][:, j, P * m:P * (m + 1)], mem.xT[:, j, CH * i:CH * (i + 1)],
                                            start=(j == 0), stop=(j == KT - 1))
                        ins.then_inc(s["proj_done"], 1)
                        n += 1
            pe.wait_ge(s["mask_ready"], 1)
            for t in range(NT):
                ins = pe.matmul(LP[:, t, :], before[:], mask[:, t, :], start=True, stop=(t == 0))
                if t:
                    ins = pe.matmul(LP[:, t, :], ones[:], seen[:, t, :], start=False, stop=True)
            ins.then_inc(s["pos_done"], 1)
            for t in range(NT):
                if t >= 2:
                    pe.wait_ge(s["v_free"], t - 1)
                for j in range(KT):
                    ins = pe.matmul(VALUES[t % 2], mem.xT[:, j, P * t:P * (t + 1)], w["v"][:, j, :], start=(j == 0), stop=(j == KT - 1))
                ins.then_inc(s["v_done"], 1)

        @block.scalar
        def _(act):
            for n in range(NT // 2):
                act.wait_ge(s["turned"], n + 1)
                tp = TP[n % 2][:].rearrange("p (a k) c -> p k a c", a=2)
                dst = mem.xT[:, :, 2 * P * n:2 * P * (n + 1)].rearrange("p k (a c) -> p k a c", a=2)
                for j in range(KT):
                    ins = act.copy(dst[:, j], tp[:, j])
                ins.then_inc(s["t_out"], 1)
            act.wait_ge(s["w_in"], 9 * 16)
            act.mul(bqs[:], bq[:], float(HD) ** -0.5).then_inc(s["bias_ready"], 1)
            act.wait_ge(s["bias_ready"], 1)

            def middle(n):
                act.wait_ge(s["rest_ready"], n + 1)
                act.copy(part_of(n, 1), qf[:, n % 4, :]).then_inc(s["mid_ready"], 1)

            for n in range(2 * KT * NC):
                a, m = n // (KT * NC), n // NC % KT
                act.wait_ge(s["proj_done"], n + 1)
                if n >= 4:
                    act.wait_ge(s["split_done"], n - 3)
                bias, scale = ((bqs, float(HD) ** -0.5), (bk, 1.0))[a]
                act.activation(qf[:, n % 4, :], MP[n % 3][:], ACT.Identity, bias=bias[:, m:m + 1], scale=scale)
                act.activation(part_of(n, 0), MP[n % 3][:], ACT.Identity,
                               bias=bias[:, m:m + 1], scale=scale).then_inc(s["p_out"], 1)
                if n:
                    middle(n - 1)
                if n == 5:
                    act.wait_ge(s["shifted"], 1)
                    act.activation(prob[:], prob[:], ACT.Exp).then_inc(s["exped"], 1)
            middle(2 * KT * NC - 1)

        @block.vector
        def _(v):
            own = Chain(v, s["dve"])
            for t in range(NT):
                v.bn_stats(st[:, t, :], mem.x[:, t, :]).then_inc(s["dve"], 1)
                own.t.n += 1
            v.wait_ge(s["dve"], own.t.n)
            for t in range(NT):
                v.bn_aggr(mv[:, t, :], st[:, t, :]).then_inc(s["stat_ready"], 1)
            v.wait_ge(s["rstd_ready"], 1)
            for t in range(NT):
                v.tensor_scalar(l1.xn[:, t, :], mem.x[:, t, :], mv[:, t, 0:1], rstd[:, t:t + 1],
                                ALU.subtract, ALU.mult).then_inc(s["xn_ready"], 1)
            v.wait_ge(s["w_in"], 9 * 16)
            own(v.tensor_copy(before[:], beforef[:]))
            v.wait_ge(s["logits_done"], 1)
            own(v.tensor_reduce(rmax[:], LP[:], AX.X, ALU.max))
            v.tensor_tensor(prob[:], LP[:], rmax[:].rearrange("p (t a) -> p t a", a=1).broadcast_to([P, NT, E]),
                            ALU.subtract).then_inc(s["shifted"], 1)
            v.wait_ge(s["exped"], 1)
            own(v.tensor_reduce(rsum[:], prob[:], AX.X, ALU.add))
            own(v.reciprocal(rsum[:], rsum[:]))
            own(v.tensor_tensor(prob[:], prob[:], rsum[:].rearrange("p (t a) -> p t a", a=1).broadcast_to([P, NT, E]), ALU.mult))
            for t in range(NT):
                v.max(top[:, t, :], prob[:, t, :]).then_inc(s["dve"], 1)
                own.t.n += 1
            v.wait_ge(s["dve"], own.t.n)
            for t in range(NT):
                v.max_index(idx[:, t, :], top[:, t, :], prob[:, t, :]).then_inc(s["dve"], 1)
                v.match_replace(prob2[:, t, :], top[:, t, :], prob[:, t, :], -1.0).then_inc(s["dve"], 1)
                own.t.n += 2
            v.wait_ge(s["dve"], own.t.n)
            own(v.tensor_scalar(mask[:], prob2[:], 0.0, None, ALU.is_lt))
            own(v.tensor_copy(seen[:, 1, :], mask[:, 0, :]))
            for t in range(2, NT):
                own(v.tensor_tensor(seen[:, t, :], seen[:, t - 1, :], mask[:, t - 1, :], ALU.add))
            v.sem_inc(s["mask_ready"], 1)
            own(v.tensor_reduce(rsum[:], top[:], AX.X, ALU.add))
            own(v.reciprocal(rsum[:], rsum[:]))
            own(v.tensor_tensor(top[:], top[:], rsum[:].rearrange("p (t a) -> p t a", a=1).broadcast_to([P, NT, TOPK]), ALU.mult))
            own(v.tensor_copy(idxf[:], idx[:]))
            v.wait_ge(s["pos_done"], 1)
            own(v.tensor_copy(pos[:], LP[:]))
            for t in range(NT):
                own(v.tensor_tensor(hit[:], eid[:].rearrange("p (a e) -> p a e", a=1).broadcast_to([P, TOPK, E]),
                                    idxf[:, t, :].rearrange("p (k a) -> p k a", a=1).broadcast_to([P, TOPK, E]), ALU.is_equal))
                own(v.tensor_tensor(hit2[:], hit[:], pos[:, t, :].rearrange("p (a e) -> p a e", a=1).broadcast_to([P, TOPK, E]), ALU.mult))
                own(v.tensor_reduce(posk[:, t, :], hit2[:], AX.X, ALU.add))
                v.wait_ge(s["v_done"], t + 1)
                v.tensor_tensor(mem.v1[:, t, :, 0:HD], VALUES[t % 2].rearrange("p (h d) -> p h d", d=HD),
                                bv[:].rearrange("p (h d) -> p h d", d=HD), ALU.add).then_inc(s["v_free"], 1)
            own(v.tensor_scalar(valid[:], posk[:], float(CAP), None, ALU.is_lt))
            own(v.tensor_tensor(l1.weight[:], top[:], valid[:], ALU.mult))
            own(v.tensor_scalar(posk[:], posk[:], float(CAP - 1), None, ALU.min))
            own(v.scalar_tensor_tensor(posk[:], idxf[:], float(CAP), posk[:], ALU.mult, ALU.add))
            own(v.tensor_copy(l1.take[:], posk[:]))
            own(v.tensor_scalar(tk[:], valid[:], -float(E * CAP), float(E * CAP), ALU.mult, ALU.add))
            own(v.tensor_tensor(tk[:], posk[:], tk[:], ALU.add))
            own(v.tensor_copy(l1.send[:], tk[:]))


def attention1_phase(nc, io, mem, l1, part, pool_work, combine=None):
    with ExitStack() as ctx:
        sb = lambda n, s, d=F32: ctx.enter_context(nc.sbuf_tensor(f"{n}_{part}", s, d))
        ps = lambda n, s, d=F32: ctx.enter_context(nc.psum_tensor(f"{n}_{part}", s, d))
        sem = lambda n: ctx.enter_context(nc.semaphore(f"a1{part}_" + n))
        PT = sb("PT1", [P, 2, 4, CH])
        oT = sb("oT1", [P, CH])
        pmax = sb("pmax", [P, 4, NT, NC])
        negm = sb("negm", [P, 4, NT])
        rest = sb("restm", [P, 4, NT])
        mp = sb("mp", [P, 4, 3, NT], BF16)
        msb = sb("msb", [96, 2, P], BF16)
        rinv = sb("rinv1", [P, 4, 4])
        ST = [ps(f"ST{i}", [P, 2, CH]) for i in range(2)]
        MX = [ps(f"MX{i}", [P, CH]) for i in range(2)]
        O = ps("O1", [P, CH])
        TR = ps("TR", [P, CH])
        TRb = TR[:].bitcast(BF16)[0:96, 0:2 * P].rearrange("p (a q) -> p a q", a=2)
        arrivals = [f"in{b}{pair}" for b in (range(2) if part == 0 else [1]) for pair in range(2)]
        names = ("m_out m_in st_done exp_done mx_done mx_free o_done oT_ready tr_done tr_free "
                 "mp_ready mt_done msb_ready main_done dve")
        s = {n: sem(n) for n in arrivals + names.split()}
        block = ctx.enter_context(nc.Block())
        IDLE = MX + [bank[:, i] for bank in ST for i in range(2)]
        UNITS = [(c, kb) for c in range(NC) for kb in range(4 * c + 4)]
        MAXES = [(hd, t, r) for hd in range(4) for t in range(NT) for r in range(t // 4 + 1)]
        PACE = {1: (2, 5), 2: (6, 6), 3: (8, 6)}
        stages = [(None, 0), (0, 1), (1, 2)] if part == 0 else [(2, 3), (3, None)]

        def maxes_at(gm, u):
            if gm is None or u < PACE[gm][0]:
                return []
            start, per = PACE[gm]
            return MAXES[(u - start) * per:(u - start + 1) * per]

        def last_max(gm):
            return None if gm is None else PACE[gm][0] + -(-len(MAXES) // PACE[gm][1]) - 1

        combine_at = [(2, u) for u in range(4, 40)] + [(3, u) for u in range(4, 32)] if combine else []

        @block.gpsimd
        def _(pool):
            pool_work(pool)

        @block.sync
        def _(sp):
            t_ = {n: Tally(s[n]) for n in "msb_ready main_done".split()}
            n_out = [0]

            def load(g):
                q, k = l1.qs[g % 2], l1.ks[g % 2]
                for pair in range(2):
                    heads, h0 = slice(2 * pair, 2 * pair + 2), 4 * g + 2 * pair
                    arrived = s[f"in{g % 2}{pair}"]
                    of_heads = slice(h0 * HD, (h0 + 2) * HD)
                    for n, (a, b) in enumerate(PARTS):
                        rows = slice(n * HD, (n + 1) * HD)
                        sp.dma_start(q[rows, heads, :], mem.qd[a, of_heads, :].rearrange("(h d) n -> d h n", d=HD)).then_inc(arrived, 16)
                        sp.dma_start(k[rows, heads, :], mem.kd[b, of_heads, :].rearrange("(h d) n -> d h n", d=HD)).then_inc(arrived, 16)
                    sp.dma_start(q[KS - 6:KS, heads, :],
                                 io["alibi_q"][h0:h0 + 2].bitcast(BF16).rearrange("h r n -> r h n")).then_inc(arrived, 16)
                    places = io["alibi_k"].bitcast(BF16).rearrange("r (a n) -> r a n", a=1).broadcast_to([KM - KS + 6, 2, N])
                    sp.dma_start(k[KS - 6:KM, heads, :], places).then_inc(arrived, 16)

            def send_max(g):
                t_["msb_ready"].need(sp)
                for a in range(2):
                    sp.dma_start(mem.md[g, 2 * a:2 * a + 2].rearrange("h k t q -> (h k t) q"), msb[:, a, :]).then_inc(s["m_out"], 16)
                n_out[0] += 2 * 16
                sp.wait_ge(s["m_out"], n_out[0])
                sp.dma_start(l1.qs[g % 2][KS:KM], mem.md[g].rearrange("h k t q -> k h (t q)")).then_inc(s["m_in"], 16)

            if part == 0:
                load(0)
                load(1)
                send_max(0)
                send_max(1)
                t_["main_done"].need(sp)
                load(2)
                send_max(2)
            else:
                load(3)
                send_max(3)
            sp.wait_ge(s["m_in"], 16 * (3 if part == 0 else 1))

        @block.tensor
        def _(pe):
            t_ = {n: Tally(s[n]) for n in arrivals + "m_in exp_done mx_free oT_ready tr_free mp_ready".split()}
            n_max = [0]

            def first_pass(g, hd, t, r, banks=MX):
                if (t, r) == (0, 0) and hd % 2 == 0:
                    t_[f"in{g % 2}{hd // 2}"].need(pe, 14 * 16)
                w = min(CH, P * (t + 1) - CH * r)
                bank = banks[n_max[0] % len(banks)]
                n_max[0] += 1
                t_["mx_free"].need(pe)
                last = r == t // 4
                ins = pe.matmul(bank[:, 0:w], l1.qs[g % 2][0:KS, hd, P * t:P * (t + 1)],
                                l1.ks[g % 2][0:KS, hd, CH * r:CH * r + w], start=True, stop=not last)
                if last:
                    ins = pe.matmul(bank[:, w - P:w], mem.ident_bf[:], mem.mask_bf[:], start=False, stop=True)
                ins.then_inc(s["mx_done"], 1)

            def turn_max():
                t_["mp_ready"].need(pe)
                t_["tr_free"].need(pe)
                for a in range(2):
                    ins = pe.transpose(TRb[:, a, :], mp[:, 2 * a:2 * a + 2].rearrange("p h k t -> p (h k t)"), mem.ident_bf[:])
                ins.then_inc(s["mt_done"], 1)

            def second_pass(g, u, then):
                c, kb = UNITS[u]
                q0 = P * max(0, kb - 4 * c)
                for pr in range(2):
                    if u > 0:
                        t_["exp_done"].need(pe)
                    for i in range(2):
                        hd = 2 * pr + i
                        ins = pe.matmul(ST[pr][:, i, q0:CH], l1.ks[g % 2][0:KM, hd, P * kb:P * (kb + 1)],
                                        l1.qs[g % 2][0:KM, hd, CH * c + q0:CH * (c + 1)], start=True, stop=(kb < 4 * c))
                        if kb >= 4 * c:
                            ins = pe.matmul(ST[pr][:, i, q0:q0 + P], mem.ident_bf[:], mem.maskT_bf[:], start=False, stop=True)
                    ins.then_inc(s["st_done"], 1)
                    then()

            def weigh(g, u, then):
                c, kb = UNITS[u]
                q0 = P * max(0, kb - 4 * c)
                if kb == 0 and not (u == 0):
                    t_["oT_ready"].need(pe)
                    turn_out()
                for hd in range(4):
                    ins = pe.matmul(O[32 * hd:32 * hd + 32, q0:CH], mem.v1[:, kb, 4 * g + hd, :], PT[:, u % 2, hd, q0:CH],
                                    start=(kb == 0), stop=(kb == 4 * c + 3), tile_position=(0, 32 * hd))
                    if hd == 3 and kb == 4 * c + 3:
                        ins.then_inc(s["o_done"], 1)
                    then()

            def turn_out():
                t_["tr_free"].need(pe)
                for q in range(4):
                    ins = pe.transpose(TR[:, P * q:P * (q + 1)], oT[:, P * q:P * (q + 1)], mem.ident[:])
                ins.then_inc(s["tr_done"], 1)

            for g, gm in stages:
                if g is None:
                    for m in MAXES:
                        first_pass(gm, *m, IDLE)
                    t_["mx_free"].need(pe, len(IDLE) - len(MX))
                    n_max[0] = 0
                    turn_max()
                    continue
                if (part, g) != (1, 2):
                    t_["m_in"].need(pe, 16)
                for u in range(len(UNITS)):
                    maxes = list(maxes_at(gm, u))

                    def one_max():
                        if maxes:
                            first_pass(gm, *maxes.pop(0))

                    second_pass(g, u, one_max)
                    if u - 1 == last_max(gm):
                        turn_max()
                    if u > 0:
                        weigh(g, u - 1, one_max)
                    while maxes:
                        one_max()
                t_["exp_done"].need(pe, 2)
                weigh(g, len(UNITS) - 1, lambda: None)
                t_["oT_ready"].need(pe)
                turn_out()

        @block.vector
        def _(v):
            own = Chain(v, s["dve"])
            t_ = {n: Tally(s[n]) for n in "mx_done tr_done mt_done".split()}
            v.sem_inc(s["mx_free"], len(IDLE if part == 0 else MX))
            v.sem_inc(s["tr_free"], 1)
            n_max = [0]

            def row_max(hd, t, r, banks=MX):
                w = min(CH, P * (t + 1) - CH * r)
                bank = banks[n_max[0] % len(banks)]
                n_max[0] += 1
                t_["mx_done"].need(v)
                ins = v.tensor_reduce(pmax[:, hd, t, r:r + 1], bank[:, 0:w], AX.X, ALU.max)
                if (hd, t, r) == MAXES[-1]:
                    own(ins)
                    v.sem_inc(s["mx_free"], 1)
                else:
                    ins.then_inc(s["mx_free"], 1)

            def split_max():
                for c in range(NC):
                    ins = v.tensor_reduce(negm[:, :, 4 * c:4 * c + 4], pmax[:, :, 4 * c:4 * c + 4, 0:c + 1], AX.X, ALU.max, negate=True)
                    ins.then_inc(s["dve"], 1)
                    own.t.n += 1
                v.wait_ge(s["dve"], own.t.n)
                own(v.tensor_copy(mp[:, :, 0, :], negm[:]))
                own(v.tensor_tensor(rest[:], negm[:], mp[:, :, 0, :], ALU.subtract))
                own(v.tensor_copy(mp[:, :, 1, :], rest[:]))
                v.tensor_tensor(mp[:, :, 2, :], rest[:], mp[:, :, 1, :], ALU.subtract).then_inc(s["mp_ready"], 1)

            def pass_max():
                t_["mt_done"].need(v)
                own(v.tensor_copy(msb[:], TRb))
                v.sem_inc(s["tr_free"], 1)
                v.sem_inc(s["msb_ready"], 1)

            def finish(g, c):
                t_["tr_done"].need(v)
                rows = TR[:].rearrange("p (q h d) -> p q h d", q=4, h=4)
                own(v.reciprocal(rinv[:], rows[:, :, :, HD]))
                v.tensor_tensor(mem.ctx[:, 4 * c:4 * c + 4, 4 * HD * g:4 * HD * (g + 1)].rearrange("p q (h d) -> p q h d", h=4),
                                rows[:, :, :, 0:HD], rinv[:].rearrange("p q (h a) -> p q h a", a=1).broadcast_to([P, 4, 4, HD]),
                                ALU.mult).then_inc(s["tr_free"], 1)

            n_step = [0]

            def combine_step(g, u):
                if (g, u) in combine_at:
                    combine(v, n_step[0] // TOPK, n_step[0] % TOPK)
                    n_step[0] += 1

            for g, gm in stages:
                if g is None:
                    for m in MAXES:
                        row_max(*m, IDLE)
                    n_max[0] = 0
                    split_max()
                    pass_max()
                    continue
                for u in range(len(UNITS)):
                    for n, m in enumerate(maxes_at(gm, u)):
                        row_max(*m)
                        if n in (0, 2):
                            combine_step(g, u)
                    if not maxes_at(gm, u):
                        combine_step(g, u)
                        combine_step(g, u)
                    if u == last_max(gm):
                        split_max()
                    if u - 1 == last_max(gm):
                        pass_max()
                    c, kb = UNITS[u]
                    if kb == 1 and c > 0:
                        finish(g, c - 1)
                finish(g, NC - 1)
                v.sem_inc(s["main_done"], 1)

        @block.scalar
        def _(act):
            t_ = {n: Tally(s[n]) for n in "st_done o_done".split()}

            def copy_out():
                t_["o_done"].need(act)
                act.copy(oT[:], O[:]).then_inc(s["oT_ready"], 1)

            for g, gm in stages:
                if g is None:
                    continue
                for u in range(len(UNITS)):
                    c, kb = UNITS[u]
                    q0 = P * max(0, kb - 4 * c)
                    for pr in range(2):
                        t_["st_done"].need(act)
                        act.activation(PT[:, u % 2, 2 * pr:2 * pr + 2, q0:CH], ST[pr][:, :, q0:CH], ACT.Exp).then_inc(s["exp_done"], 1)
                    if kb == 0 and c > 0:
                        copy_out()
                copy_out()


def experts_phase(nc, io, mem, l1):
    with ExitStack() as ctx:
        sb = lambda n, s, d=F32: ctx.enter_context(nc.sbuf_tensor(n, s, d))
        ps = lambda n, s, d=F32: ctx.enter_context(nc.psum_tensor(n, s, d))
        sem = lambda n: ctx.enter_context(nc.semaphore("e_" + n))
        room = [x[:].rearrange("p h n -> p (h n)").bitcast(F32) for x in (l1.qs[1], l1.ks[1])]
        rows = room[0][:, 0:2 * EG * D].rearrange("p (u e c) -> p u e c", u=2, e=EG)
        res = room[1][:, 0:2 * EG * D].rearrange("p (u e c) -> p u e c", u=2, e=EG)
        wd = room[1][0:I, 2 * EG * D:4 * EG * D].rearrange("p (u e c) -> p u e c", u=2, e=EG)
        wg, wu = sb("wg", [P, 2, EG, KT, I]), sb("wu", [P, 2, EG, KT, I])
        rT = sb("rT", [P, 2, EG, KT, P])
        th, hid = sb("the", [I, EG, P]), sb("hide", [I, EG, P])
        RT = ps("RT", [P, EG, KT, P])
        G, U = ps("GE", [I, EG, P]), ps("UE", [I, EG, P])
        R = ps("RE", [P, EG, D])
        names = ("rows0 rows1 weights0 weights1 in_free turned_act turned_dve rT_act rT_dve gate_done up_done tanhed hid_ready "
                 "res_done r_free copied stored0 stored1 dve")
        s = {n: sem(n) for n in names.split()}
        block = ctx.enter_context(nc.Block())
        ITER = E // EG // 2

        def first_expert(it, u):
            return it * 2 * EG + u * EG

        @block.sync
        def _(sp):
            in_free = Tally(s["in_free"])
            with sp.Fori(0, ITER) as it:
                for u in range(2):
                    in_free.need(sp)
                    e0 = first_expert(it, u)
                    sp.dma_start(rows[:, u], mem.xe[bass.ds(e0 * CAP, EG * CAP), :].rearrange("(e p) c -> p e c", p=P)).then_inc(s[f"rows{u}"], 16)
                    for wt, src in ((wg, "gate"), (wu, "up")):
                        sp.dma_start(wt[:, u].rearrange("p e k i -> p (e k) i"),
                                     io[src][bass.ds(e0, EG)].rearrange("e (k p) i -> p (e k) i", p=P)).then_inc(s[f"weights{u}"], 16)
                    sp.dma_start(wd[:, u], io["down"][bass.ds(e0, EG)].rearrange("e i d -> i e d")).then_inc(s[f"weights{u}"], 16)
                in_free.give_back(sp)

        @block.tensor
        def _(pe):
            t_ = {n: Tally(s[n]) for n in "rows0 rows1 weights0 weights1 rT_act rT_dve hid_ready r_free".split()}

            def turn(u):
                t_[f"rows{u}"].need(pe, 16)
                for e in range(EG):
                    for k in range(KT):
                        ins = pe.transpose(RT[:, e, k, :], rows[:, u, e, P * k:P * (k + 1)], mem.ident[:])
                    if e == 1:
                        ins.then_inc(s["turned_act"], 1)
                ins.then_inc(s["turned_dve"], 1)

            def gate_up(u):
                t_[f"weights{u}"].need(pe, 3 * 16)
                t_["rT_act"].need(pe)
                t_["rT_dve"].need(pe)
                for wt, bank, done in ((wg, G, "gate_done"), (wu, U, "up_done")):
                    for e in range(EG):
                        for k in range(KT):
                            ins = pe.matmul(bank[:, e, :], wt[:, u, e, k, :], rT[:, u, e, k, :],
                                            start=(k == 0), stop=(k == KT - 1))
                    ins.then_inc(s[done], 1)

            def down(u):
                t_["hid_ready"].need(pe)
                t_["r_free"].need(pe)
                for e in range(EG):
                    ins = pe.matmul(R[:, e, :], hid[:, e, :], wd[:, u, e, :], start=True, stop=True)
                ins.then_inc(s["res_done"], 1)

            def groups(more):
                gate_up(0)
                turn(1)
                down(0)
                gate_up(1)
                if more:
                    turn(0)
                down(1)
                for x in t_.values():
                    x.give_back(pe)

            turn(0)
            t_["rows0"].give_back(pe)
            with pe.Fori(0, ITER - 1) as it:
                groups(True)
            groups(False)

        @block.scalar
        def _(act):
            own = Chain(act, s["copied"])
            t_ = {n: Tally(s[n]) for n in "turned_act gate_done res_done stored0 stored1".split()}
            act.sem_inc(s["r_free"], 1)
            act.sem_inc(s["in_free"], 2)
            act.sem_inc(s["stored0"], 16)
            act.sem_inc(s["stored1"], 16)

            def turned(u):
                t_["turned_act"].need(act)
                act.copy(rT[:, u, 0:2], RT[:, 0:2]).then_inc(s["rT_act"], 1)

            def tanh_half():
                t_["gate_done"].need(act)
                act.activation(th[:], G[:], ACT.Tanh, scale=0.5).then_inc(s["tanhed"], 1)

            def store(it, u):
                t_["res_done"].need(act)
                t_[f"stored{u}"].need(act, 16)
                act.sem_inc(s["in_free"], 1)
                own(act.copy(res[:, u], R[:]))
                act.sem_inc(s["r_free"], 1)
                act.dma_start(mem.ye[bass.ds(first_expert(it, u) * CAP, EG * CAP), :].rearrange("(e p) c -> p e c", p=P),
                              res[:, u]).then_inc(s[f"stored{u}"], 16)

            def groups(it, more):
                tanh_half()
                turned(1)
                store(it, 0)
                tanh_half()
                if more:
                    turned(0)
                store(it, 1)
                for x in t_.values():
                    x.give_back(act)
                own.give_back()

            turned(0)
            t_["turned_act"].give_back(act)
            with act.Fori(0, ITER - 1) as it:
                groups(it, True)
            groups(ITER - 1, False)
            act.wait_ge(s["stored0"], 16)
            act.wait_ge(s["stored1"], 16)

        @block.vector
        def _(v):
            own = Chain(v, s["dve"])
            t_ = {n: Tally(s[n]) for n in "turned_dve up_done tanhed".split()}

            def turned(u):
                t_["turned_dve"].need(v)
                v.tensor_copy(rT[:, u, 2:4], RT[:, 2:4]).then_inc(s["rT_dve"], 1)

            def hidden():
                t_["tanhed"].need(v)
                own(v.scalar_tensor_tensor(th[:], th[:], 1.0, G[:], ALU.add, ALU.mult))
                t_["up_done"].need(v)
                v.scalar_tensor_tensor(hid[:], th[:], 0.5, U[:], ALU.mult, ALU.mult).then_inc(s["hid_ready"], 1)

            def groups(more):
                turned(1)
                hidden()
                if more:
                    turned(0)
                hidden()
                for x in t_.values():
                    x.give_back(v)
                own.give_back()

            turned(0)
            t_["turned_dve"].give_back(v)
            with v.Fori(0, ITER - 1) as it:
                groups(True)
            groups(False)


def output_phase(nc, io, mem, l1):
    with ExitStack() as ctx:
        sb = lambda n, s, d=F32: ctx.enter_context(nc.sbuf_tensor(n, s, d))
        ps = lambda n, s, d=F32: ctx.enter_context(nc.psum_tensor(n, s, d))
        sem = lambda n: ctx.enter_context(nc.semaphore("o_" + n))
        wo = sb("wo1", [P, KT, D])
        bo = sb("bo", [P, D])
        th = sb("tho", [P, NT, D])
        att = sb("att", [P, 2, 2, D])
        TP = [ps(f"TO{i}", [P, 4, P]) for i in range(2)]
        Y = [ps(f"YO{i}", [P, 2, D]) for i in range(2)]
        s = {n: sem(n) for n in "w_in turned t_out y_done y_free tanhed out_ready stored dve".split()}
        block = ctx.enter_context(nc.Block())
        PAIRS = NT // 2

        @block.sync
        def _(sp):
            sp.dma_start(wo[:], io["Wo1"].rearrange("(k p) n -> p k n", p=P)).then_inc(s["w_in"], 16)
            sp.dma_start(bo[:], io["bo1"].rearrange("(a n) -> a n", a=1).broadcast_to([P, D])).then_inc(s["w_in"], 16)
            ov = io["out"][0].rearrange("(t p) c -> p t c", p=P)
            for n in range(PAIRS):
                sp.wait_ge(s["out_ready"], n + 1)
                sp.dma_start(ov[:, 2 * n:2 * n + 2, :], mem.x[:, 2 * n:2 * n + 2, :]).then_inc(s["stored"], 16)
            sp.wait_ge(s["stored"], 16 * PAIRS)

        @block.tensor
        def _(pe):
            def turn(n):
                if n >= 2:
                    pe.wait_ge(s["t_out"], n - 1)
                for a in range(2):
                    for j in range(KT):
                        ins = pe.transpose(TP[n % 2][:, 2 * a + j, :], mem.ctx[:, 2 * n + a, P * j:P * (j + 1)], mem.ident[:])
                ins.then_inc(s["turned"], 1)

            turn(0)
            pe.wait_ge(s["w_in"], 2 * 16)
            for n in range(PAIRS):
                if n + 1 < PAIRS:
                    turn(n + 1)
                pe.wait_ge(s["t_out"], n + 1)
                if n >= 2:
                    pe.wait_ge(s["y_free"], n - 1)
                for a in range(2):
                    t = 2 * n + a
                    for j in range(KT):
                        ins = pe.matmul(Y[n % 2][:, a, :], mem.xT[:, j, P * t:P * (t + 1)], wo[:, j, :],
                                        start=(j == 0), stop=(j == KT - 1))
                ins.then_inc(s["y_done"], 1)

        @block.scalar
        def _(act):
            for n in range(PAIRS):
                act.activation(th[:, 2 * n:2 * n + 2, :], mem.f[:, 2 * n:2 * n + 2, :], ACT.Tanh, scale=0.5).then_inc(s["tanhed"], 1)
                act.wait_ge(s["turned"], n + 1)
                tp = TP[n % 2][:].rearrange("p (a k) c -> p k a c", a=2)
                dst = mem.xT[:, :, 2 * P * n:2 * P * (n + 1)].rearrange("p k (a c) -> p k a c", a=2)
                act.copy(dst[:, 0], tp[:, 0])
                act.copy(dst[:, 1], tp[:, 1]).then_inc(s["t_out"], 1)

        @block.vector
        def _(v):
            own = Chain(v, s["dve"])
            v.wait_ge(s["w_in"], 2 * 16)
            bias = bo[:].rearrange("p (a c) -> p a c", a=1).broadcast_to([P, 2, D])
            for n in range(PAIRS):
                now = slice(2 * n, 2 * n + 2)
                v.wait_ge(s["tanhed"], n + 1)
                own(v.scalar_tensor_tensor(th[:, now, :], th[:, now, :], 1.0, mem.f[:, now, :], ALU.add, ALU.mult))
                v.wait_ge(s["y_done"], n + 1)
                v.tensor_tensor(att[:, n % 2], Y[n % 2][:], bias, ALU.add).then_inc(s["y_free"], 1)
                v.wait_ge(s["y_free"], n + 1)
                own(v.scalar_tensor_tensor(th[:, now, :], th[:, now, :], 0.5, att[:, n % 2], ALU.mult, ALU.mult))
                v.tensor_tensor(mem.x[:, now, :], mem.x[:, now, :], th[:, now, :], ALU.add).then_inc(s["out_ready"], 1)


def layer1(nc, io, mem):
    l1 = Memory()
    with ExitStack() as ctx:
        sb = lambda n, s, d=F32: ctx.enter_context(nc.sbuf_tensor(n, s, d))
        mem.xT = sb("xT", [P, KT, N])
        sem = lambda n: ctx.enter_context(nc.semaphore("l1_" + n))
        l1.xn = sb("xn1", [P, NT, D])
        l1.weight = sb("weight", [P, NT, TOPK])
        l1.take, l1.send = sb("take", [P, NT, TOPK], U32), sb("send", [P, NT, TOPK], U32)
        mem.v1 = sb("v1", [P, NT, HEADS, 32])
        mem.f = l1.xn
        mem.ctx = mem.acc
        got = mem.xT[:].rearrange("p k (b c) -> p k b c", c=D)
        sent, taken, combined = sem("sent"), [sem("taken0"), sem("taken1")], sem("combined")
        project1_phase(nc, io, mem, l1)
        l1.qs = [sb(f"qs{i}", [P, 4, N], BF16) for i in range(2)]
        l1.ks = [sb(f"ks{i}", [P, 4, N], BF16) for i in range(2)]

        def send_rows(eng):
            eng.wait_ge(mem.xe_zeroed, 8 * 16)
            for t in range(NT):
                for k in range(TOPK):
                    eng.indirect_dma_start(mem.xe, bass.IndirectOffsetOnAxis(l1.send[:, t, k:k + 1], 0), l1.xn[:, t, :], None,
                                           bounds_check=E * CAP - 1, oob_is_err=False).then_inc(sent, 16)
            eng.wait_ge(sent, 16 * NT * TOPK)

        def take_rows(eng):
            for t in range(NT):
                if t >= 2:
                    eng.wait_ge(combined, TOPK * (t - 1))
                for k in range(TOPK):
                    eng.indirect_dma_start(got[:, t % 2, k, :], None, mem.ye, bass.IndirectOffsetOnAxis(l1.take[:, t, k:k + 1], 0),
                                           bounds_check=E * CAP - 1, oob_is_err=False).then_inc(taken[t % 2], 16)

        def combine(eng, t, k):
            f, w = mem.f[:, t, :], l1.weight[:, t, k:k + 1]
            if k == 0:
                eng.wait_ge(taken[t % 2], 16 * TOPK * (t // 2 + 1))
                eng.tensor_scalar(f, got[:, t % 2, 0], w, None, ALU.mult).then_inc(combined, 1)
            else:
                eng.wait_ge(combined, TOPK * t + k)
                eng.scalar_tensor_tensor(f, got[:, t % 2, k], w, f, ALU.mult, ALU.add).then_inc(combined, 1)

        attention1_phase(nc, io, mem, l1, 0, send_rows)
        experts_phase(nc, io, mem, l1)
        attention1_phase(nc, io, mem, l1, 1, take_rows, combine)
        output_phase(nc, io, mem, l1)


class Memory:
    pass


def build(nc, io):
    mem = Memory()
    with ExitStack() as ctx:
        sb = lambda n, s, d=F32: ctx.enter_context(nc.sbuf_tensor(n, s, d))
        sem = lambda n: ctx.enter_context(nc.semaphore(n))
        dram = lambda n, s, d=F32: nc.dram_tensor(n, s, d, kind="Internal").ap()
        mem.xe = dram("xe", [E * CAP, D])
        mem.ye = dram("ye", [E * CAP, D])
        mem.qd = dram("qd", [3, D, N], BF16)
        mem.kd = dram("kd", [3, D, N], BF16)
        mem.md = dram("md", [4, 4, 3, NT, P], BF16)
        mem.xe_zeroed = sem("xe_zeroed")
        mem.x = sb("x", [P, NT, D])
        mem.acc = sb("acc", [P, NT, D])
        mem.ident = sb("ident", [P, P])
        mem.ident_bf = sb("ident_bf", [P, P], BF16)
        mem.mask_bf = sb("mask_bf", [P, P], BF16)
        mem.maskT_bf = sb("maskT_bf", [P, P], BF16)
        with ExitStack() as layer0:
            sb0 = lambda n, s, d=F32: layer0.enter_context(nc.sbuf_tensor(n, s, d))
            mem.W = [[sb0(f"W{i}{part}", [P, 3, N], F16) for part in range(2)] for i in range(2)]
            mem.xT = [sb0(f"xT0{part}", [P, KT, N + CH], F16) for part in range(2)]
            with ExitStack() as attn0:
                sba = lambda n, s, d=F32: attn0.enter_context(nc.sbuf_tensor(n, s, d))
                mem.gxT = [sba(f"gxT{i}", [P, KT, N], F16) for i in range(2)]
                mem.cos = sba("cosT", [P, N])
                mem.sin = sba("sinT", [P, N])
                mem.kT = [sba(f"k_part{i}", [P, N], F16) for i in range(2)]
                mem.v = [sba(f"v_part{i}", [P, NT, DH], F16) for i in range(2)]
                setup_phase(nc, io, mem)
                attention0_phase(nc, io, mem)
            mlp0_phase(nc, io, mem)
        layer1(nc, io, mem)


def constants():
    inv = (1.0 / 10000.0 ** (np.arange(0, DH, 2, dtype=np.float32) / np.float32(DH))).astype(np.float32)
    freqs = (np.arange(N, dtype=np.float32)[:, None] * inv[None, :]).astype(np.float32).T
    cos, sin = np.cos(freqs).astype(np.float32), np.sin(freqs).astype(np.float32)
    slopes = (np.float32(2.0 ** (-8.0 / HEADS)) ** np.arange(1, HEADS + 1, dtype=np.float32)).astype(np.float32)
    r = np.arange(P)

    def parts(w):
        out = []
        for _ in range(3):
            out.append((w.view(np.uint32) >> 16).astype(np.uint16))
            w = w - (out[-1].astype(np.uint32) << 16).view(np.float32)
        return out

    slope, place = parts(slopes), parts(np.arange(1 - N, 1, dtype=np.float32))
    alibi_q = np.stack([slope[a] for a, _ in PARTS], 1)[:, :, None] + np.zeros((1, 1, N), np.uint16)
    ones = parts(np.ones(N, np.float32))[0]
    alibi_k = np.stack([place[b] for _, b in PARTS] + [ones] * 3)
    return {
        "cos": np.concatenate([cos, cos]),
        "sin": np.concatenate([sin, -sin]),
        "identity": np.eye(P, dtype=np.float32),
        "causal": np.where(r[None, :] > r[:, None], np.float32(NEG), np.float32(0)).astype(np.float32),
        "before": (r[:, None] < r[None, :]).astype(np.float32),
        "alibi_q": alibi_q, "alibi_k": alibi_k,
        "causalT": np.where(r[:, None] > r[None, :], np.float32(NEG), np.float32(0)).astype(np.float32),
        "expert_ids": np.ascontiguousarray(np.broadcast_to(np.arange(E, dtype=np.float32), (P, E))),
    }


def layouts(a):
    def gate_like(w):
        return w.reshape(8, P, 2, -1).transpose(0, 2, 3, 1).reshape(NBLK, -1, P)

    def down_like(w, k):
        return w.reshape(2, P, 8, k).transpose(2, 0, 3, 1).reshape(NBLK, k, P)

    def col(w):
        return w.reshape(KT, P).T

    packed = [gate_like(a["L0_ffn_gate_W_packed"]), gate_like(a["L0_ffn_up_W_packed"]),
              down_like(a["L0_ffn_down_W_packed"], P)]
    scales = [gate_like(a["L0_ffn_gate_scales"]), gate_like(a["L0_ffn_up_scales"]),
              down_like(a["L0_ffn_down_scales"], 8)]
    wq = a["L0_attn_Wq"].reshape(D, HEADS, DH).transpose(1, 0, 2)
    out = {
        "x": a["L0_attn_x"], "gamma": col(a["L0_attn_gamma"]), "Wkv": a["L0_attn_Wkv"], "Wo": a["L0_attn_Wo"],
        "Wq": np.concatenate([wq, wq[:1]]),
        "packed": np.stack(packed, axis=2), "scales": np.stack(scales, axis=2),
        "Wq1": a["L1_attn_Wq"], "Wk1": a["L1_attn_Wk"], "Wv1": a["L1_attn_Wv"], "Wo1": a["L1_attn_Wo"],
        "bq1": col(a["L1_attn_bq"]), "bk1": col(a["L1_attn_bk"]), "bv1": a["L1_attn_bv"], "bo1": a["L1_attn_bo"],
        "router": a["L1_ffn_router_weight"], "gate": a["L1_ffn_gate_proj"], "up": a["L1_ffn_up_proj"],
        "down": a["L1_ffn_down_proj"],
    }
    return {k: np.ascontiguousarray(v) for k, v in out.items()}


def kernel(**inputs):
    import concourse.bacc as bacc
    from concourse.bass_utils import run_bass_kernel_spmd

    nc = bacc.Bacc("TRN2", target_bir_lowering=False, num_devices=1)
    arrays, io = {}, {}
    for name, a in {**layouts({k: np.asarray(v) for k, v in inputs.items()}), **constants()}.items():
        arrays["in_" + name] = a
        io[name] = nc.dram_tensor("in_" + name, a.shape, mybir.dt.from_np(a.dtype), kind="ExternalInput").ap()
    io["out"] = nc.dram_tensor("out", [1, N, D], F32, kind="ExternalOutput").ap()
    build(nc, io)
    r = run_bass_kernel_spmd(nc, [arrays], core_ids=[0])
    return r.results[0]["out"]
```
